# Optimizing a Trainium2 kernel written in Bass

```python
import numpy as np
import jax
import jax.numpy as jnp

def _softmax(x, axis=-1):
    return jax.nn.softmax(x, axis=axis)

def _gelu(x):
    return jax.nn.gelu(x, approximate=True)

def _silu(x):
    return jax.nn.silu(x)

def _sigmoid(x):
    return jax.nn.sigmoid(x)

def _layernorm(x, axis=-1, eps=1e-05):
    m = jnp.mean(x, axis=axis, keepdims=True)
    v = jnp.var(x, axis=axis, keepdims=True)
    return (x - m) / jnp.sqrt(v + eps)

def _scatter_add(tgt, idx, src, axis=0):
    return tgt.at[idx].add(src)

def _segment_sum(src, seg, n):
    return jax.ops.segment_sum(src, seg, n)
kernel_name = 'mk_recurrent_d2_jaxref_r8_e7a4bd'

def setup_inputs(seed: int=0):
    np.random.seed(seed)
    _w = jnp.asarray

    def _L0_attn_setup():
        import jax, jax.numpy as jnp
        import numpy as np
        HIDDEN = 128
        STATE = 16
        BATCH = 4
        SEQ = 256
        key = jax.random.key(seed)
        k0, k1, k2, k3 = jax.random.split(key, 4)
        x = jax.random.normal(k0, (BATCH, SEQ, HIDDEN), jnp.float32)
        Wx = jax.random.normal(k1, (2 * STATE + HIDDEN, HIDDEN), jnp.float32) / np.sqrt(HIDDEN)
        A_log = jax.random.normal(k2, (STATE,), jnp.float32)
        D = jnp.ones((HIDDEN,), jnp.float32)
        Wout = jax.random.normal(k3, (HIDDEN, HIDDEN), jnp.float32) / np.sqrt(HIDDEN)
        return {'x': x, 'Wx': Wx, 'A_log': A_log, 'D': D, 'Wout': Wout}
    _L0_attn_in = _L0_attn_setup()

    def _L0_ffn_setup():
        import jax, jax.numpy as jnp
        import numpy as np
        EPS = 1e-05
        N_HEADS = 16
        TOP_K = 2

        def _ln(x, g, b):
            m = x.mean(-1, keepdims=True)
            v = ((x - m) ** 2).mean(-1, keepdims=True)
            return (x - m) / jnp.sqrt(v + EPS) * g + b

        def _block_fwd(x, ln1_g, ln1_b, ln2_g, ln2_b, Wq, bq, Wk, bk, Wv, bv, Wo, bo, Wr, br, e_w1, e_b1, e_w2, e_b2):
            B, S, D = x.shape
            H = N_HEADS
            hd = D // H
            h = _ln(x, ln1_g, ln1_b)
            q = (h @ Wq + bq).reshape(B, S, H, hd).transpose(0, 2, 1, 3)
            k = (h @ Wk + bk).reshape(B, S, H, hd).transpose(0, 2, 1, 3)
            v = (h @ Wv + bv).reshape(B, S, H, hd).transpose(0, 2, 1, 3)
            scores = jnp.einsum('bhqd,bhkd->bhqk', q, k) / hd ** 0.5
            causal = jnp.tril(jnp.ones((S, S), dtype=bool))
            scores = jnp.where(causal, scores, -jnp.inf)
            attn = jax.nn.softmax(scores, axis=-1)
            o = jnp.einsum('bhqk,bhkd->bhqd', attn, v).transpose(0, 2, 1, 3).reshape(B, S, D)
            a = o @ Wo + bo + x
            h2 = _ln(a, ln2_g, ln2_b)
            logits = h2 @ Wr + br
            topv = jax.lax.top_k(logits, TOP_K)[0]
            kmask = logits >= topv[..., -1:]
            w = jax.nn.softmax(jnp.where(kmask, logits, -jnp.inf), axis=-1)
            mid = jax.nn.gelu(jnp.einsum('bsd,edf->bsef', h2, e_w1) + e_b1, approximate=False)
            eo = jnp.einsum('bsef,efd->bsed', mid, e_w2) + e_b2
            moe = jnp.einsum('bse,bsed->bsd', w, eo)
            return moe + a
        key = jax.random.key(seed)
        B, S, D, E = (1, 256, 128, 8)
        F = 4 * D
        ks = jax.random.split(key, 8)

        def n(k, shape):
            return jax.random.normal(k, shape, jnp.float32) * 0.02
        return dict(x=jax.random.normal(ks[0], (B, S, D), jnp.float32), ln1_g=jnp.ones((D,), jnp.float32), ln1_b=jnp.zeros((D,), jnp.float32), ln2_g=jnp.ones((D,), jnp.float32), ln2_b=jnp.zeros((D,), jnp.float32), Wq=n(ks[1], (D, D)), bq=jnp.zeros((D,), jnp.float32), Wk=n(ks[2], (D, D)), bk=jnp.zeros((D,), jnp.float32), Wv=n(ks[3], (D, D)), bv=jnp.zeros((D,), jnp.float32), Wo=n(ks[4], (D, D)), bo=jnp.zeros((D,), jnp.float32), Wr=n(ks[5], (D, E)), br=jnp.zeros((E,), jnp.float32), e_w1=n(ks[6], (E, D, F)), e_b1=jnp.zeros((E, F), jnp.float32), e_w2=n(ks[7], (E, F, D)), e_b2=jnp.zeros((E, D), jnp.float32))
    _L0_ffn_in = _L0_ffn_setup()

    def _L1_attn_setup():
        import jax, jax.numpy as jnp
        import numpy as np
        import math
        _DENSE_LOCAL_W = 64
        _DYADIC = [96, 128, 192, 32, 48, 64, 96, 128, 192]
        OFFSETS = sorted(set(range(0, _DENSE_LOCAL_W + 1)) | set(_DYADIC))
        B, N, D, H = (1, 256, 128, 16)
        HD = D // H
        key = jax.random.key(seed)
        ks = jax.random.split(key, 8)
        s = 1.0 / math.sqrt(D)
        x = jax.random.normal(ks[0], (B, N, D), dtype=jnp.float32)
        Wqkv = jax.random.uniform(ks[1], (3 * D, D), jnp.float32, -s, s)
        bqkv = jax.random.uniform(ks[2], (3 * D,), jnp.float32, -s, s)
        Wgate = jax.random.uniform(ks[3], (D, D), jnp.float32, -s, s)
        bgate = jax.random.uniform(ks[4], (D,), jnp.float32, -s, s)
        Wout = jax.random.uniform(ks[5], (D, D), jnp.float32, -s, s)
        bout = jax.random.uniform(ks[6], (D,), jnp.float32, -s, s)
        alphas = jnp.linspace(0.2, 2.0, H)
        deltas = jnp.array([math.log(1.0 + d) for d in OFFSETS], dtype=jnp.float32)
        pos_bias = -deltas[:, None] * alphas[None, :]
        offsets = jnp.array(OFFSETS, dtype=jnp.int32)
        return {'x': x, 'Wqkv': Wqkv, 'bqkv': bqkv, 'Wgate': Wgate, 'bgate': bgate, 'Wout': Wout, 'bout': bout, 'pos_bias': pos_bias, 'offsets': offsets}
    _L1_attn_in = _L1_attn_setup()

    def _L1_ffn_setup():
        import jax, jax.numpy as jnp
        import numpy as np
        HIDDEN = 128
        NUM_EXPERTS = 8
        TOP_K = 2
        FFN = 512
        BATCH, SEQ = (4, 256)
        key = jax.random.key(seed)
        k_x, k_r, k_w1, k_w2 = jax.random.split(key, 4)
        x = jax.random.normal(k_x, (BATCH, SEQ, HIDDEN), dtype=jnp.float32)
        router_w = jax.random.normal(k_r, (NUM_EXPERTS, HIDDEN), dtype=jnp.float32) * (1.0 / np.sqrt(HIDDEN))
        lim = float(np.sqrt(6.0 / (FFN + HIDDEN)))
        expert_w1 = jax.random.uniform(k_w1, (NUM_EXPERTS, FFN, HIDDEN), dtype=jnp.float32, minval=-lim, maxval=lim)
        expert_w2 = jax.random.uniform(k_w2, (NUM_EXPERTS, HIDDEN, FFN), dtype=jnp.float32, minval=-lim, maxval=lim)
        return {'x': x, 'router_w': router_w, 'expert_w1': expert_w1, 'expert_w2': expert_w2}
    _L1_ffn_in = _L1_ffn_setup()
    _d = {'L0_attn_x': _L0_attn_in['x'], 'L0_attn_Wx': _L0_attn_in['Wx'], 'L0_attn_A_log': _L0_attn_in['A_log'], 'L0_attn_D': _L0_attn_in['D'], 'L0_attn_Wout': _L0_attn_in['Wout'], 'L0_ffn_ln1_g': _L0_ffn_in['ln1_g'], 'L0_ffn_ln1_b': _L0_ffn_in['ln1_b'], 'L0_ffn_ln2_g': _L0_ffn_in['ln2_g'], 'L0_ffn_ln2_b': _L0_ffn_in['ln2_b'], 'L0_ffn_Wq': _L0_ffn_in['Wq'], 'L0_ffn_bq': _L0_ffn_in['bq'], 'L0_ffn_Wk': _L0_ffn_in['Wk'], 'L0_ffn_bk': _L0_ffn_in['bk'], 'L0_ffn_Wv': _L0_ffn_in['Wv'], 'L0_ffn_bv': _L0_ffn_in['bv'], 'L0_ffn_Wo': _L0_ffn_in['Wo'], 'L0_ffn_bo': _L0_ffn_in['bo'], 'L0_ffn_Wr': _L0_ffn_in['Wr'], 'L0_ffn_br': _L0_ffn_in['br'], 'L0_ffn_e_w1': _L0_ffn_in['e_w1'], 'L0_ffn_e_b1': _L0_ffn_in['e_b1'], 'L0_ffn_e_w2': _L0_ffn_in['e_w2'], 'L0_ffn_e_b2': _L0_ffn_in['e_b2'], 'L1_attn_Wqkv': _L1_attn_in['Wqkv'], 'L1_attn_bqkv': _L1_attn_in['bqkv'], 'L1_attn_Wgate': _L1_attn_in['Wgate'], 'L1_attn_bgate': _L1_attn_in['bgate'], 'L1_attn_Wout': _L1_attn_in['Wout'], 'L1_attn_bout': _L1_attn_in['bout'], 'L1_attn_pos_bias': _L1_attn_in['pos_bias'], 'L1_attn_offsets': _L1_attn_in['offsets'], 'L1_ffn_router_w': _L1_ffn_in['router_w'], 'L1_ffn_expert_w1': _L1_ffn_in['expert_w1'], 'L1_ffn_expert_w2': _L1_ffn_in['expert_w2']}
    _x0 = _d['L0_attn_x']
    _d['L0_attn_x'] = jax.random.normal(jax.random.fold_in(jax.random.key(seed), 1), (4, 512, 128), dtype=_x0.dtype)
    del _x0
    return _d

def reference(L0_attn_x, L0_attn_Wx, L0_attn_A_log, L0_attn_D, L0_attn_Wout, L0_ffn_ln1_g, L0_ffn_ln1_b, L0_ffn_ln2_g, L0_ffn_ln2_b, L0_ffn_Wq, L0_ffn_bq, L0_ffn_Wk, L0_ffn_bk, L0_ffn_Wv, L0_ffn_bv, L0_ffn_Wo, L0_ffn_bo, L0_ffn_Wr, L0_ffn_br, L0_ffn_e_w1, L0_ffn_e_b1, L0_ffn_e_w2, L0_ffn_e_b2, L1_attn_Wqkv, L1_attn_bqkv, L1_attn_Wgate, L1_attn_bgate, L1_attn_Wout, L1_attn_bout, L1_attn_pos_bias, L1_attn_offsets, L1_ffn_router_w, L1_ffn_expert_w1, L1_ffn_expert_w2):

    def _L0_attn_ref(x, Wx, A_log, D, Wout):
        import jax, jax.numpy as jnp
        import numpy as np
        HIDDEN = 128
        STATE = 16
        BATCH = 4
        SEQ = 256
        B, L, H = x.shape
        N = A_log.shape[0]
        xp = x @ Wx.T
        Bm = xp[..., :N]
        Cm = xp[..., N:2 * N]
        delta = jax.nn.softplus(xp[..., 2 * N:])
        A = -jnp.exp(A_log)

        def step(h, inp):
            dt, bt, ct, xt = inp
            dA = jnp.exp(dt[:, None, :] * A[None, :, None])
            h = dA * h + dt[:, None, :] * bt[:, :, None] * xt[:, None, :]
            y = jnp.einsum('bnh,bn->bh', h, ct) + D * xt
            return (h, y)
        h0 = jnp.zeros((B, N, H), x.dtype)
        xs = (jnp.swapaxes(delta, 0, 1), jnp.swapaxes(Bm, 0, 1), jnp.swapaxes(Cm, 0, 1), jnp.swapaxes(x, 0, 1))
        _, ys = jax.lax.scan(step, h0, xs)
        y = jnp.swapaxes(ys, 0, 1)
        return y @ Wout.T

    def _L0_ffn_ref(x, ln1_g, ln1_b, ln2_g, ln2_b, Wq, bq, Wk, bk, Wv, bv, Wo, bo, Wr, br, e_w1, e_b1, e_w2, e_b2):
        import jax, jax.numpy as jnp
        import numpy as np
        EPS = 1e-05
        N_HEADS = 16
        TOP_K = 2

        def _ln(x, g, b):
            m = x.mean(-1, keepdims=True)
            v = ((x - m) ** 2).mean(-1, keepdims=True)
            return (x - m) / jnp.sqrt(v + EPS) * g + b

        def _block_fwd(x, ln1_g, ln1_b, ln2_g, ln2_b, Wq, bq, Wk, bk, Wv, bv, Wo, bo, Wr, br, e_w1, e_b1, e_w2, e_b2):
            B, S, D = x.shape
            H = N_HEADS
            hd = D // H
            h = _ln(x, ln1_g, ln1_b)
            q = (h @ Wq + bq).reshape(B, S, H, hd).transpose(0, 2, 1, 3)
            k = (h @ Wk + bk).reshape(B, S, H, hd).transpose(0, 2, 1, 3)
            v = (h @ Wv + bv).reshape(B, S, H, hd).transpose(0, 2, 1, 3)
            scores = jnp.einsum('bhqd,bhkd->bhqk', q, k) / hd ** 0.5
            causal = jnp.tril(jnp.ones((S, S), dtype=bool))
            scores = jnp.where(causal, scores, -jnp.inf)
            attn = jax.nn.softmax(scores, axis=-1)
            o = jnp.einsum('bhqk,bhkd->bhqd', attn, v).transpose(0, 2, 1, 3).reshape(B, S, D)
            a = o @ Wo + bo + x
            h2 = _ln(a, ln2_g, ln2_b)
            logits = h2 @ Wr + br
            topv = jax.lax.top_k(logits, TOP_K)[0]
            kmask = logits >= topv[..., -1:]
            w = jax.nn.softmax(jnp.where(kmask, logits, -jnp.inf), axis=-1)
            mid = jax.nn.gelu(jnp.einsum('bsd,edf->bsef', h2, e_w1) + e_b1, approximate=False)
            eo = jnp.einsum('bsef,efd->bsed', mid, e_w2) + e_b2
            moe = jnp.einsum('bse,bsed->bsd', w, eo)
            return moe + a
        return _block_fwd(x, ln1_g, ln1_b, ln2_g, ln2_b, Wq, bq, Wk, bk, Wv, bv, Wo, bo, Wr, br, e_w1, e_b1, e_w2, e_b2)

    def _L1_attn_ref(x, Wqkv, bqkv, Wgate, bgate, Wout, bout, pos_bias, offsets):
        import jax, jax.numpy as jnp
        import numpy as np
        import math
        _DENSE_LOCAL_W = 64
        _DYADIC = [96, 128, 192, 32, 48, 64, 96, 128, 192]
        OFFSETS = sorted(set(range(0, _DENSE_LOCAL_W + 1)) | set(_DYADIC))
        B, N, D, H = (1, 256, 128, 16)
        HD = D // H
        Bx, Nx, Dx = x.shape
        qkv = x @ Wqkv.T + bqkv
        q, k, v = jnp.split(qkv, 3, axis=-1)
        q = q.reshape(Bx, Nx, H, HD).transpose(0, 2, 1, 3)
        k = k.reshape(Bx, Nx, H, HD).transpose(0, 2, 1, 3)
        v = v.reshape(Bx, Nx, H, HD).transpose(0, 2, 1, 3)
        scale = HD ** (-0.5)
        n_idx = jnp.arange(Nx, dtype=jnp.int32)[:, None]
        idx = n_idx - offsets[None, :]
        valid = idx >= 0
        idx_c = jnp.clip(idx, 0, Nx - 1)
        K_all = k[:, :, idx_c, :]
        V_all = v[:, :, idx_c, :]
        scores = jnp.einsum('bhnd,bhnod->bhno', q, K_all) * scale
        scores = scores + pos_bias.T[None, :, None, :]
        scores = jnp.where(valid[None, None], scores, -jnp.inf)
        alpha = jax.nn.softmax(scores, axis=-1)
        out = jnp.einsum('bhno,bhnod->bhnd', alpha, V_all)
        flat = out.transpose(0, 2, 1, 3).reshape(Bx, Nx, Dx)
        gate = jax.nn.sigmoid(x @ Wgate.T + bgate)
        return flat * gate @ Wout.T + bout

    def _L1_ffn_ref(x, router_w, expert_w1, expert_w2):
        import jax, jax.numpy as jnp
        import numpy as np
        HIDDEN = 128
        NUM_EXPERTS = 8
        TOP_K = 2
        FFN = 512
        BATCH, SEQ = (4, 256)
        B, S, D = x.shape
        xf = x.reshape(-1, D)
        scores = xf @ router_w.T
        top_v, top_i = jax.lax.top_k(scores, TOP_K)
        routing_w = jax.nn.softmax(top_v, axis=-1)
        out = jnp.zeros_like(xf)
        for e in range(NUM_EXPERTS):
            w_e = jnp.sum(jnp.where(top_i == e, routing_w, 0.0), axis=-1)
            h = jax.nn.gelu(xf @ expert_w1[e].T, approximate=False)
            out = out + h @ expert_w2[e].T * w_e[:, None]
        return out.reshape(B, S, D)
    x = L0_attn_x
    xn = _layernorm(x, axis=-1)
    s = _L0_attn_ref(xn, L0_attn_Wx, L0_attn_A_log, L0_attn_D, L0_attn_Wout)
    g = _silu(_L0_ffn_ref(xn, L0_ffn_ln1_g, L0_ffn_ln1_b, L0_ffn_ln2_g, L0_ffn_ln2_b, L0_ffn_Wq, L0_ffn_bq, L0_ffn_Wk, L0_ffn_bk, L0_ffn_Wv, L0_ffn_bv, L0_ffn_Wo, L0_ffn_bo, L0_ffn_Wr, L0_ffn_br, L0_ffn_e_w1, L0_ffn_e_b1, L0_ffn_e_w2, L0_ffn_e_b2))
    x = x + s * g
    xn = _layernorm(x, axis=-1)
    s = _L1_attn_ref(xn, L1_attn_Wqkv, L1_attn_bqkv, L1_attn_Wgate, L1_attn_bgate, L1_attn_Wout, L1_attn_bout, L1_attn_pos_bias, L1_attn_offsets)
    g = _silu(_L1_ffn_ref(xn, L1_ffn_router_w, L1_ffn_expert_w1, L1_ffn_expert_w2))
    x = x + s * g
    return x

_drawn_inputs = setup_inputs


def setup_inputs(seed=0):
    import zlib

    import numpy as np

    out = dict(_drawn_inputs(seed))
    spreads = {'L0_attn_D': (1.0, 0.2),
     'L0_ffn_ln1_g': (1.0, 0.6),
     'L0_ffn_ln1_b': (0.0, 0.8),
     'L0_ffn_ln2_g': (1.0, 0.2),
     'L0_ffn_ln2_b': (0.0, 0.507),
     'L0_ffn_bq': (0.0, 0.8),
     'L0_ffn_bk': (0.0, 0.8),
     'L0_ffn_bv': (0.0, 0.329),
     'L0_ffn_bo': (0.0, 0.1),
     'L0_ffn_br': (0.0, 0.1),
     'L0_ffn_e_b1': (0.0, 0.469),
     'L0_ffn_e_b2': (0.0, 0.1)}
    factors = {'L0_ffn_Wq': 8.0,
     'L0_ffn_Wk': 8.0,
     'L0_ffn_Wv': 5.084,
     'L1_attn_Wqkv': 8.0,
     'L1_attn_bqkv': 8.0,
     'L1_attn_Wgate': 8.0,
     'L1_attn_bgate': 8.0,
     'L1_attn_Wout': 8.0,
     'L1_attn_bout': 8.0,
     'L1_attn_pos_bias': 8.0,
     'L1_ffn_router_w': 8.0,
     'L1_ffn_expert_w1': 8.0,
     'L1_ffn_expert_w2': 8.0}
    for name, (base, spread) in spreads.items():
        noise = np.random.default_rng([zlib.crc32(name.encode()), seed]).standard_normal(out[name].shape)
        drawn = base * np.exp(spread * noise) if base else spread * noise
        out[name] = jnp.asarray(drawn.astype(out[name].dtype))
    for name, factor in factors.items():
        out[name] = (out[name] * factor).astype(out[name].dtype)
    return out
```

```python
from contextlib import ExitStack

import concourse.bass as bass
from concourse import mybir

F32 = mybir.dt.float32
BF16 = mybir.dt.bfloat16
I32 = mybir.dt.int32
ACT = mybir.ActivationFunctionType
ALU = mybir.AluOpType
AX = mybir.AxisListType

P = 128
NEG = -1.0e30
LOWEST = -3.0e38
EPS = 1e-5
PARTS = 3
VW = 32
WSLOTS = 4

Q_BANK, K_BANK, V_BANK, GATE_BANK = 0, 1, 2, 3
MAX_BANKS = (4, 5)
UNIT_BANKS = ((0, 1), (2, 3))
O_BANK = 6
SMALL_BANK = 7
T_BANKS = (6, 7)
PROJ_BANK = 0
MID_BANKS = (0, 1)
OUT_BANKS = (2, 3)
B_BANK, C_BANK = 4, 5
MISC_BANK = 6
S_BANK = 7


def build(nc, d, out):
    B, T, D = d["x"].shape
    NT = T // P
    N = d["A_log"].shape[1]
    NO, H = d["pos_bias"].shape
    HD = D // H
    E = d["b2"].shape[0]
    F = d["w1_0"].shape[2]
    FT = F // P
    NF = E * FT
    SCALE = float(HD) ** -0.5
    PAIRS = PARTS * PARTS
    KR = PAIRS * HD
    G = H // 4
    LBW = T + P
    assert D == P and HD == 8 and NT == 4 and G * NT == 16

    with ExitStack() as ctx:
        def sb(name, shape, dt=F32):
            return ctx.enter_context(nc.sbuf_tensor(name, shape, dt))

        def sem(name):
            return ctx.enter_context(nc.semaphore(name))

        ident = sb("ident", [P, P])
        ident_bf = sb("ident_bf", [P, P], BF16)
        bcast_sel = sb("bcast_sel", [3 * 32, 32], BF16)
        ones_row = sb("ones_row", [1, P])
        ones_bf = sb("ones_bf", [H, T], BF16)
        minus_half = sb("minus_half", [P, NT])
        mask_q = sb("mask_q", [P, T])
        mask_kT = sb("mask_kT", [P, P], BF16)
        cols = sb("cols", [P, d["cols"].shape[1]])
        rows = sb("rows", [1, d["rows"].shape[1]])
        b1c = sb("b1c", [P, NF])
        b2r = sb("b2r", [E, D])
        negA = sb("negA", [P, N])
        wbc = sb("wbc", [P, 3 * 32])
        wdelta = sb("wdelta", [P, D])
        wmat = {k: sb("w_" + k, [P, d[k].shape[1]]) for k in
                ("wq0", "wk0", "wv0", "wo0", "wr0", "wout0", "wq1", "wk1", "wv1", "wgate1", "wo1", "wr1")}
        bias_q = sb("bias_q", [P, H, T], BF16)
        bias_kT = sb("bias_kT", [P, H, T])
        D_COL, G1, B1, G2, B2, BQ0, BK0, BQ1, BK1, BG1 = (cols[:, i:i + 1] for i in range(10))
        BV0, BO0, BV1, BO1 = (rows[0:1, i * D:(i + 1) * D] for i in range(4))
        BR0 = rows[0:1, 4 * D:4 * D + E]

        x_tok = sb("x_tok", [P, NT, D])
        xn_tok = sb("xn_tok", [P, NT, D])
        a_tok = sb("a_tok", [P, NT, D])
        xnT = sb("xnT", [P, T])
        hT = sb("hT", [P, T])
        stats = sb("stats", [P, NT, 6])
        mv = sb("mv", [P, NT, 2])
        ve = sb("ve", [P, NT])
        rstd = sb("rstd", [P, NT])
        q32 = sb("q32", [P, T])
        qres = sb("qres", [P, T])
        k32 = sb("k32", [P, T])
        kres = sb("kres", [P, T])
        qpart = [sb(f"qpart{i}", [P, T], BF16) for i in range(PARTS)]
        kpart = [sb(f"kpart{i}", [P, T], BF16) for i in range(PARTS)]
        stackQ = sb("stackQ", [P, H, T], BF16)
        stackK = sb("stackK", [P, H, T], BF16)
        vAug = sb("vAug", [P, NT, H, VW])
        maxq = sb("maxq", [P, G * 16])
        mparts = sb("mparts", [16, 2, 2, P], BF16)
        probs = sb("probs", [P, 4, 4, T])
        o_sb = sb("o_sb", [P, 2, T])
        recip = sb("recip", [P, NT, 4])
        flat = sb("flat", [P, NT, H, HD])
        oT = sb("oT", [P, T])
        gateT = sb("gateT", [P, T])
        w1s = sb("w1s", [P, WSLOTS, F])
        w2s = sb("w2s", [P, WSLOTS, FT, D])
        mid = sb("mid", [P, 4, T])
        acc = sb("acc", [P, NT, D])
        logits = sb("logits", [P, NT, E])
        top8 = sb("top8", [P, NT, 8])
        ex = sb("ex", [P, NT, E])
        gt = sb("gt", [P, NT, E])
        eq = sb("eq", [P, NT, E])
        rank = sb("rank", [P, NT, E])
        keep = sb("keep", [P, NT, E])
        wts = sb("wts", [P, NT, E])
        tsum = sb("tsum", [P, NT])
        cnt = sb("cnt", [P, NT])
        wT = sb("wT", [E, T])
        bcS = sb("bcS", [3 * 32, T], BF16)
        bcR = sb("bcR", [3 * 32, T])

        fQ = stackQ[:].rearrange("p h t -> p (h t)").bitcast(F32).rearrange("p (n t) -> p n t", t=T)
        fK = stackK[:].rearrange("p h t -> p (h t)").bitcast(F32).rearrange("p (n t) -> p n t", t=T)
        u_buf = [fQ[:, i, :] for i in (0, 1)]
        h_buf = [fQ[:, i, :] for i in (2, 3)]
        p_buf = [fQ[:, i, :] for i in (4, 5)]
        sp1, dt, dtx, dx, sp2 = (fK[:, i, :] for i in range(5))

        ps = ctx.enter_context(nc.psum_tensor("ps", [P, 8, T], F32))
        scrF = nc.dram_tensor("scrF", [P, H, LBW], F32).ap()
        scrR = nc.dram_tensor("scrR", [P, H, LBW], BF16).ap()

        ld, ld_first = sem("ld"), sem("ld_first")
        pool_step, dve_step, act_step, pe_step = (sem(n) for n in ("pool_step", "dve_step", "act_step", "pe_step"))
        rows_ready, bias_written, bias_loaded = sem("rows_ready"), sem("bias_written"), sem("bias_loaded")

        pf = probs[:].rearrange("p a b t -> p (a b t)")
        off_ci, off_ri = pf[0:NO, 0:1].bitcast(I32), pf[0:NO, 8:8 + NO].bitcast(I32)
        off_c, off_r = pf[0:NO, 96:97], pf[0:NO, 104:104 + NO]
        same, apart, before = (pf[0:NO, a:a + NO] for a in (200, 300, 400))
        dup, first = pf[0:NO, 500:501], pf[0:NO, 501:502]
        iota_i = pf[0:NO, 512:512 + 2 * T].bitcast(I32)
        iota_f = pf[0:NO, 1536:1536 + 2 * T]
        onehot = pf[0:NO, 2560:2560 + 2 * T]
        pb = pf[0:NO, 3584:3584 + H * NO].rearrange("p (h o) -> p h o", h=H)
        pbmax, pbsum, joint, ones_oh = (pf[0:NO, a:a + H] for a in (4700, 4720, 4740, 4760))
        biasrow = pf[0:H, 5120:5120 + 2 * LBW]
        pen = pf[0:H, 6400:6400 + 2 * T]
        rev_bf = pf[0:H, 7424:7424 + LBW // 2].bitcast(BF16)
        N_LD = 6 + len(wmat)

        with nc.Block() as block:
            @block.sync
            def _(sp):
                sp.dma_start(off_ci, d["offsets"].rearrange("(o a) -> o a", a=1)).then_inc(ld_first, 16)
                sp.dma_start(off_ri, d["offsets"].partition_broadcast(NO)).then_inc(ld_first, 16)
                sp.dma_start(pb, d["pos_biasT"].partition_broadcast(NO)).then_inc(ld_first, 16)
                sp.dma_start(negA[:], d["A_log"][0, :].partition_broadcast(P)).then_inc(ld_first, 16)
                sp.dma_start(cols[:], d["cols"]).then_inc(ld, 16)
                sp.dma_start(rows[:], d["rows"]).then_inc(ld, 16)
                sp.dma_start(b1c[:], d["b1"]).then_inc(ld, 16)
                sp.dma_start(b2r[:], d["b2"]).then_inc(ld, 16)
                sp.dma_start(wbc[:], d["wbc"]).then_inc(ld, 16)
                sp.dma_start(wdelta[:], d["wdelta"]).then_inc(ld, 16)
                for k, w in wmat.items():
                    sp.dma_start(w[:], d[k]).then_inc(ld, 16)
                sp.wait_ge(ld, 16 * N_LD)
                sp.wait_ge(rows_ready, 1)
                fwd = biasrow[:, 0:LBW].unsqueeze(1).to_broadcast([H, P, LBW])
                rev = rev_bf.unsqueeze(1).to_broadcast([H, P, LBW])
                sp.dma_start(scrF.rearrange("c h t -> h c t"), fwd).then_inc(bias_written, 16)
                sp.dma_start(scrR.rearrange("c h t -> h c t"), rev).then_inc(bias_written, 16)
                sp.wait_ge(bias_written, 32)
                for scr, dst in ((scrF, bias_kT), (scrR, bias_q)):
                    skew = bass.AP(tensor=scr.tensor, offset=P - 1, ap=[[H * LBW - 1, P], [LBW, H], [1, T]])
                    sp.dma_start(dst[:], skew).then_inc(bias_loaded, 16)

            @block.gpsimd
            def _(pool):
                nc.gpsimd.memset(ident[:], 0.0)
                nc.gpsimd.memset(mask_q[:], 0.0)
                nc.gpsimd.memset(ones_bf[:], 1.0)
                nc.gpsimd.memset(ones_row[:], 1.0)
                nc.gpsimd.memset(minus_half[:], -0.5)
                nc.gpsimd.memset(keep[:], 1.0)
                nc.gpsimd.memset(vAug[:], 0.0).then_inc(pool_step, 1)
                nc.gpsimd.iota(iota_i[:, 0:T], pattern=[[1, T]], base=0, channel_multiplier=0)
                nc.gpsimd.iota(iota_i[:, T:2 * T], pattern=[[-1, T]], base=T - 1,
                               channel_multiplier=0).then_inc(pool_step, 1)
                pool.wait_ge(pool_step, 1)
                nc.gpsimd.memset(keep[:, :, 0:1], 0.0)
                nc.gpsimd.memset(vAug[:, :, :, HD:HD + 1], 1.0)
                nc.gpsimd.affine_select(out=ident[:], in_=ident[:], compare_op=ALU.not_equal, fill=1.0,
                                        base=0, pattern=[[-1, P]], channel_multiplier=1)
                nc.gpsimd.affine_select(out=mask_kT[:], in_=mask_q[:, 0:P], compare_op=ALU.is_ge,
                                        fill=NEG, base=0, pattern=[[1, P]], channel_multiplier=-1)
                nc.gpsimd.affine_select(out=mask_q[:, T - P:T], in_=mask_q[:, T - P:T], compare_op=ALU.is_ge,
                                        fill=NEG, base=0, pattern=[[-1, P]],
                                        channel_multiplier=1).then_inc(pool_step, 1)
                pool.wait_ge(pool_step, 3)
                nc.gpsimd.tensor_copy(ident_bf[:], ident[:]).then_inc(pool_step, 1)
                for r in range(3):
                    pool.wait_ge(pool_step, 4 + r)
                    nc.gpsimd.tensor_copy(bcast_sel[32 * r:32 * r + 32, :],
                                          ident[32 * r:32 * r + 32, 32 * r:32 * r + 32]).then_inc(pool_step, 1)
                pool.wait_ge(pool_step, 7)
                pool.wait_ge(dve_step, 3)
                nc.gpsimd.affine_select(out=before, in_=same, compare_op=ALU.is_gt, fill=0.0,
                                        base=0, pattern=[[-1, NO]],
                                        channel_multiplier=1).then_inc(pool_step, 1)

            @block.scalar
            def _(act):
                act.wait_ge(ld_first, 64)
                nc.scalar.activation(negA[:], negA[:], ACT.Exp).then_inc(act_step, 1)
                act.wait_ge(dve_step, 7)
                nc.scalar.activation(pb, pb, ACT.Exp).then_inc(act_step, 1)
                act.wait_ge(dve_step, 8)
                nc.scalar.activation(pbsum, pbsum, ACT.Ln).then_inc(act_step, 1)

            @block.tensor
            def _(pe):
                pe.wait_ge(dve_step, 14)
                for r in range(2):
                    oh = onehot[:, r * T:(r + 1) * T]
                    nc.tensor.matmul(ps[0:H, r, :], joint, oh, start=True, stop=True)
                    nc.tensor.matmul(ps[0:H, 2 + r, :], ones_oh, oh, start=True, stop=True).then_inc(pe_step, 1)

            @block.vector
            def _(dve):
                done = [0]

                def step(ins):
                    done[0] += 1
                    ins.then_inc(dve_step, 1)
                    dve.wait_ge(dve_step, done[0])

                dve.wait_ge(ld_first, 64)
                step(nc.vector.tensor_copy(off_c, off_ci))
                step(nc.vector.tensor_copy(off_r, off_ri))
                step(nc.vector.tensor_scalar(same, off_r, off_c, None, ALU.is_equal))
                step(nc.vector.tensor_scalar(apart, same, -1.0, -NEG, ALU.add, ALU.mult))
                step(nc.vector.tensor_tensor(pb, pb, apart.unsqueeze(1).to_broadcast([NO, H, NO]), ALU.add))
                step(nc.vector.tensor_reduce(pbmax, pb, AX.X, ALU.max))
                step(nc.vector.tensor_tensor(pb, pb, pbmax.unsqueeze(2).to_broadcast([NO, H, NO]),
                                             ALU.subtract))
                dve.wait_ge(act_step, 2)
                step(nc.vector.tensor_reduce(pbsum, pb, AX.X, ALU.add))
                dve.wait_ge(act_step, 3)
                step(nc.vector.tensor_tensor(joint, pbsum, pbmax, ALU.add))
                dve.wait_ge(pool_step, 8)
                step(nc.vector.tensor_reduce(dup, before, AX.X, ALU.add))
                step(nc.vector.tensor_scalar(first, dup, 0.0, None, ALU.is_equal))
                step(nc.vector.tensor_copy(iota_f, iota_i))
                step(nc.vector.memset(ones_oh, 1.0))
                step(nc.vector.tensor_scalar(onehot, iota_f, off_c, first, ALU.is_equal, ALU.mult))
                nc.vector.tensor_scalar(negA[:], negA[:], -1.0, None, ALU.mult)
                step(nc.vector.memset(biasrow, NEG))
                dve.wait_ge(pe_step, 2)
                step(nc.vector.tensor_scalar(pen.rearrange("h (a t) -> h a t", a=2), ps[0:H, 2:4, :],
                                             -1.0, -NEG, ALU.add, ALU.mult))
                nc.vector.tensor_tensor(biasrow[:, P - 1:P - 1 + T], ps[0:H, 0, :], pen[:, 0:T], ALU.add)
                step(nc.vector.tensor_tensor(biasrow[:, LBW:LBW + T], ps[0:H, 1, :], pen[:, T:2 * T], ALU.add))
                nc.vector.tensor_copy(rev_bf, biasrow[:, LBW:2 * LBW]).then_inc(rows_ready, 1)

        loop_sems = []

        def lsem(name):
            loop_sems.append(sem(name))
            return loop_sems[-1]

        def both(name):
            return lsem(name + "_0"), lsem(name + "_1")

        x_loaded, stored = lsem("x_loaded"), lsem("stored")
        dve_seq, act_seq, pool_seq = lsem("dve_seq"), lsem("act_seq"), lsem("pool_seq")
        var_ready = [lsem(f"var_ready_{i}") for i in range(4)]
        rstd_ready = [lsem(f"rstd_ready_{i}") for i in range(4)]
        xn_ready, xnT_ps, xnT_ready = both("xn_ready"), both("xnT_ps"), both("xnT_ready")
        hh_ready, hT_ps, hT_ready = lsem("hh_ready"), lsem("hT_ps"), lsem("hT_ready")
        h2_ready, h2T_ps, h2T_ready = lsem("h2_ready"), lsem("h2T_ps"), lsem("h2T_ready")
        proj_ps = both("proj_ps")
        k32_ready, v_ready = both("k32_ready"), both("v_ready")
        gate_ready = lsem("gate_ready")
        q_parts, k_parts = both("q_parts"), both("k_parts")
        stacks_ready = both("stacks_ready")
        s1_ps, max_done = both("s1_ps"), both("max_done")
        small_ps, small_free = both("small_ps"), both("small_free")
        m_rows = both("m_rows_even"), both("m_rows_odd")
        s2_ps, p_ready, pv_done, osb_ready = both("s2_ps"), both("p_ready"), both("pv_done"), both("osb_ready")
        biased = lsem("biased")
        fT_ps, oT_ready, att_ps = both("fT_ps"), both("oT_ready"), both("att_ps")
        a_ready, s1_ready = lsem("a_ready"), lsem("s1_ready")
        bcd_ps, bc_ready, sp_ready, dt_ready, dtx_ready, dx_ready = (
            lsem(n) for n in ("bcd_ps", "bc_ready", "sp_ready", "dt_ready", "dtx_ready", "dx_ready"))
        dA_ready, b_ps, c_ps, b_used, scanned, c_used, s_acc = (
            lsem(n) for n in ("dA_ready", "b_ps", "c_ps", "b_used", "scanned", "c_used", "s_acc"))
        lg_ps, ex_in, ex_ready, w_ready = both("lg_ps"), both("ex_in"), both("ex_ready"), both("w_ready")
        wT_ps, wT_ready, b2_ps, acc_init = (lsem(n) for n in ("wT_ps", "wT_ready", "b2_ps", "acc_init"))
        mid_ps, mid_ready, mid_used = both("mid_ps"), both("mid_ready"), both("mid_used")
        w_loaded = [both(f"w_loaded_{k}") for k in range(WSLOTS)]
        acc_done, silu_ready, prod_ready, x_ready = (
            both("acc_done"), both("silu_ready"), both("prod_ready"), both("x_ready"))

        NMAX, NUNIT = H * NT, 2 * G * NT
        LEAD = 5
        order = []
        for m in range(NMAX):
            order.append(("max", m))
            if m % 16 == 15:
                order.append(("turn", m // 16))
            if m >= 16 + LEAD and (m - 16 - LEAD) % 2 == 0:
                order.append(("unit", (m - 16 - LEAD) // 2))
        order += [("unit", v) for v in range((NMAX - 1 - 16 - LEAD) // 2 + 1, NUNIT)]
        for g in range(G):
            at = order.index(("unit", 8 * g + 9)) + 1 if g < G - 1 else len(order)
            order.insert(at, ("out", g))
        small_use = {e: i + 1 for i, e in enumerate(e for e in order if e[0] in ("turn", "out"))}

        def window(i):
            return slice(T - P * (i + 1), T)

        def tile(i):
            return slice(i * P, (i + 1) * P)

        wq, wk, wv, wo, wr = ([wmat[n + s] for s in "01"] for n in ("wq", "wk", "wv", "wo", "wr"))
        BQ, BK, BV, BO = (BQ0, BQ1), (BK0, BK1), (BV0, BV1), (BO0, BO1)
        flat_tok = flat[:].rearrange("p a h i -> p a (h i)")
        att_in, att_in_ready = (hT, xnT), (hT_ready, xnT_ready[1])
        moe_in, moe_in_ready = (hT, xnT), (h2T_ready, xnT_ready[1])

        with nc.Fori(0, B) as b:
            with nc.Block() as block:
                @block.sync
                def _(sp):
                    sp.dma_start(x_tok[:], d["x"][bass.ds(b, 1)].rearrange("b (a p) d -> p (b a) d", p=P))\
                        .then_inc(x_loaded, 16)

                    def load_expert(l, e):
                        k = e % WSLOTS
                        sp.dma_start(w1s[:, k, :], d[f"w1_{l}"][:, e, :]).then_inc(w_loaded[k][l], 16)
                        sp.dma_start(w2s[:, k, :, :], d[f"w2_{l}"][:, e * FT:(e + 1) * FT, :])\
                            .then_inc(w_loaded[k][l], 16)

                    for e in range(WSLOTS):
                        load_expert(0, e)
                    for l in range(2):
                        for a in range(PARTS):
                            sp.wait_ge(k_parts[l], a + 1)
                            for j in range(a, PAIRS, PARTS):
                                sp.dma_start(stackK[HD * j:HD * (j + 1), :, :], kpart[a][:])\
                                    .then_inc(stacks_ready[l], 16)
                            sp.wait_ge(q_parts[l], a + 1)
                            for j in range(a * PARTS, (a + 1) * PARTS):
                                sp.dma_start(stackQ[HD * j:HD * (j + 1), :, :], qpart[a][:])\
                                    .then_inc(stacks_ready[l], 16)
                        for r in range(2):
                            sp.dma_start(stackK[KR + r:KR + r + 1, :, :], ones_bf[:])\
                                .then_inc(stacks_ready[l], 16)
                        for g in range(G):
                            sp.wait_ge(small_free[l], small_use[("turn", g)])
                            for r in range(2):
                                sp.dma_start(stackQ[KR + r:KR + r + 1, 4 * g:4 * g + 4, :],
                                             mparts[:, g % 2, r, :]).then_inc(m_rows[g % 2][l], 16)
                        if l == 0:
                            for e in range(WSLOTS, E):
                                sp.wait_ge(mid_used[0], FT * (e - WSLOTS + 1))
                                load_expert(0, e)
                            for e in range(WSLOTS):
                                sp.wait_ge(mid_used[0], FT * (e + E - WSLOTS + 1))
                                load_expert(1, e)
                    for e in range(WSLOTS, E):
                        sp.wait_ge(mid_used[1], FT * (e - WSLOTS + 1))
                        load_expert(1, e)
                    sp.wait_ge(x_ready[1], 1)
                    sp.dma_start(out[bass.ds(b, 1)].rearrange("b (a p) d -> p (b a) d", p=P), x_tok[:])\
                        .then_inc(stored, 16)
                    sp.wait_ge(stored, 16)

                @block.tensor
                def _(pe):
                    def turn4(bank, src, signal):
                        for i in range(NT):
                            ins = nc.tensor.transpose(ps[:, bank, tile(i)], src(i), ident[:])
                        ins.then_inc(signal, 1)

                    def tokens_times(bank, lhs, rhs, row, signal, width=D):
                        for i in range(NT):
                            o = ps[:, bank, i * width:(i + 1) * width]
                            ins = nc.tensor.matmul(o, lhs[:, tile(i)], rhs, start=(i == 0),
                                                   stop=(row is None and i == NT - 1), skip_group_check=True)
                            if row is not None:
                                ins = nc.tensor.matmul(o, ones_row[:], row, start=False, stop=(i == NT - 1),
                                                       skip_group_check=True)
                        ins.then_inc(signal, 1)

                    def layer_input(l):
                        pe.wait_ge(xn_ready[l], 1)
                        turn4(T_BANKS[0], lambda i: xn_tok[:, i, :], xnT_ps[l])
                        if l == 0:
                            pe.wait_ge(hh_ready, 1)
                            turn4(T_BANKS[1], lambda i: a_tok[:, i, :], hT_ps)

                    def projections(l):
                        pe.wait_ge(att_in_ready[l], 1)
                        aT = att_in[l]
                        nc.tensor.matmul(ps[:, Q_BANK, :], wq[l][:], aT[:], start=True, stop=True)\
                            .then_inc(proj_ps[l], 1)
                        nc.tensor.matmul(ps[:, K_BANK, :], wk[l][:], aT[:], start=True, stop=True)\
                            .then_inc(proj_ps[l], 1)
                        tokens_times(V_BANK, aT, wv[l][:], BV[l], proj_ps[l])
                        if l == 1:
                            nc.tensor.matmul(ps[:, GATE_BANK, :], wmat["wgate1"][:], aT[:], start=True, stop=True)\
                                .then_inc(proj_ps[l], 1)

                    def max_scores(l, m):
                        h, i = m // NT, m % NT
                        if m == 0:
                            pe.wait_ge(stacks_ready[l], 16 * (2 * PAIRS + 2))
                        if m >= 2:
                            pe.wait_ge(max_done[l], m - 1)
                        nc.tensor.matmul(ps[:, MAX_BANKS[m % 2], 0:P * (i + 1)], stackQ[0:KR, h, tile(i)],
                                         stackK[0:KR, h, 0:P * (i + 1)], start=True, stop=True)\
                            .then_inc(s1_ps[l], 1)

                    def small_wait(l, event):
                        if small_use[event] > 1:
                            pe.wait_ge(small_free[l], small_use[event] - 1)

                    def turn_maxima(l, g):
                        pe.wait_ge(max_done[l], 16 * (g + 1))
                        small_wait(l, ("turn", g))
                        nc.tensor.transpose(ps[0:16, SMALL_BANK, 0:P], maxq[:, 16 * g:16 * g + 16], ident[:])\
                            .then_inc(small_ps[l], 1)

                    def unit_scores(l, v):
                        g, kt, pr = v // 8, v % 8 // 2, v % 2
                        W = T - P * kt
                        if v == 0:
                            pe.wait_ge(v_ready[l], 1)
                            if l == 1:
                                pe.wait_ge(gate_ready, 1)
                        if v % 8 == 0:
                            pe.wait_ge(m_rows[g % 2][l], 32 * (g // 2 + 1))
                        if v >= 2:
                            pe.wait_ge(p_ready[0] if l == 0 else biased, v - 1)
                        for r in range(2):
                            h = 4 * g + 2 * pr + r
                            o = UNIT_BANKS[v % 2][r]
                            ins = nc.tensor.matmul(ps[:, o, 0:W], stackK[0:KR + 2, h, tile(kt)],
                                                   stackQ[0:KR + 2, h, P * kt:T], start=True, stop=(l == 1),
                                                   skip_group_check=True)
                            if l == 0:
                                ins = nc.tensor.matmul(ps[:, o, 0:P], ident_bf[:], mask_kT[:], start=False,
                                                       stop=True, skip_group_check=True)
                        ins.then_inc(s2_ps[l], 1)

                    def weigh_values(l, w):
                        g, kt = w // NT, w % NT
                        pe.wait_ge(p_ready[l], 2 * w + 2)
                        if kt == 0 and g >= 1:
                            pe.wait_ge(osb_ready[l], g)
                        for j in range(4):
                            ins = nc.tensor.matmul(ps[32 * j:32 * j + VW, O_BANK, P * kt:T],
                                                   vAug[:, kt, 4 * g + j, :], probs[:, w % 4, j, 0:T - P * kt],
                                                   start=(kt == 0), stop=(kt == NT - 1), skip_group_check=True)
                        ins.then_inc(pv_done[l], 1)

                    def turn_output(l, g):
                        pe.wait_ge(osb_ready[l], g + 1)
                        small_wait(l, ("out", g))
                        turn4(SMALL_BANK, lambda i: o_sb[:, g % 2, tile(i)], small_ps[l])

                    def attention(l):
                        for kind, n in order:
                            if kind == "max":
                                max_scores(l, n)
                            elif kind == "turn":
                                turn_maxima(l, n)
                            elif kind == "unit":
                                unit_scores(l, n)
                                if n % 2 == 0 and n >= 2:
                                    weigh_values(l, n // 2 - 1)
                                if n == NUNIT - 1:
                                    weigh_values(l, n // 2)
                            else:
                                turn_output(l, n)

                    def recurrence_inputs():
                        pe.wait_ge(max_done[0], NMAX)
                        nc.tensor.matmul(ps[0:96, B_BANK, :], wbc[:], xnT[:], start=True, stop=True)\
                            .then_inc(bcd_ps, 1)
                        nc.tensor.matmul(ps[:, C_BANK, :], wdelta[:], xnT[:], start=True, stop=True)\
                            .then_inc(bcd_ps, 1)

                    def finish_attention(l):
                        pe.wait_ge(small_free[l], 2 * G)
                        turn4(O_BANK, lambda i: flat_tok[:, i, :], fT_ps[l])
                        pe.wait_ge(oT_ready[l], 1)
                        tokens_times(PROJ_BANK, oT, wo[l][:], BO[l], att_ps[l])

                    def state_step(m):
                        if m < N:
                            if m == 0:
                                pe.wait_ge(bc_ready, 1)
                                pe.wait_ge(dt_ready, 1)
                            else:
                                pe.wait_ge(b_used, m)
                            nc.tensor.matmul(ps[:, B_BANK, :], bcast_sel[:, m:m + 1].to_broadcast([96, P]),
                                             bcS[:], start=True, stop=True).then_inc(b_ps, 1)
                            if m >= 1:
                                pe.wait_ge(c_used, m)
                            nc.tensor.matmul(ps[:, C_BANK, :], bcast_sel[:, N + m:N + m + 1].to_broadcast([96, P]),
                                             bcS[:], start=True, stop=True).then_inc(c_ps, 1)
                        if m == 0:
                            pe.wait_ge(dx_ready, 1)
                        else:
                            pe.wait_ge(c_used, m)
                        src = dx if m == 0 else p_buf[(m - 1) % 2]
                        for i in range(NT):
                            ins = nc.tensor.matmul(ps[:, S_BANK, tile(i)], src[:, tile(i)], wmat["wout0"][:],
                                                   start=(m == 0 and i == 0), stop=(m == N and i == NT - 1),
                                                   skip_group_check=True)
                        ins.then_inc(s_acc, 1)

                    def experts(l):
                        pe.wait_ge(moe_in_ready[l], 1)
                        x_in = moe_in[l]
                        if l == 1:
                            pe.wait_ge(s1_ready, 1)
                        tokens_times(MISC_BANK, x_in, wr[l][:], BR0 if l == 0 else None, lg_ps[l], width=E)
                        for n in range(NF + 1):
                            if n < NF:
                                if n % FT == 0:
                                    pe.wait_ge(w_loaded[n // FT % WSLOTS][l], 32 * (n // FT // WSLOTS + 1))
                                if n >= 2:
                                    pe.wait_ge(mid_ready[l], n - 1)
                                nc.tensor.matmul(ps[:, MID_BANKS[n % 2], :],
                                                 w1s[:, n // FT % WSLOTS, tile(n % FT)], x_in[:],
                                                 start=True, stop=True).then_inc(mid_ps[l], 1)
                            if n >= 1:
                                k = n - 1
                                e, ft = k // FT, k % FT
                                pe.wait_ge(mid_ready[l], k + 1)
                                if ft == 0 and e >= 2:
                                    pe.wait_ge(acc_done[l], e - 1)
                                for i in range(NT):
                                    ins = nc.tensor.matmul(ps[:, OUT_BANKS[e % 2], tile(i)], mid[:, k % 4, tile(i)],
                                                           w2s[:, e % WSLOTS, ft, :], start=(ft == 0 and i == 0),
                                                           stop=(ft == FT - 1 and i == NT - 1),
                                                           skip_group_check=True)
                                ins.then_inc(mid_used[l], 1)
                            if l == 0 and n % 2 == 0:
                                state_step(n // 2)
                            if l == 0 and n == 4:
                                pe.wait_ge(w_ready[0], 1)
                                for i in range(NT):
                                    ins = nc.tensor.transpose(ps[0:E, MISC_BANK, tile(i)], wts[:, i, :], ident[:])
                                ins.then_inc(wT_ps, 1)
                            if l == 0 and n == 6:
                                pe.wait_ge(wT_ready, 1)
                                tokens_times(MISC_BANK, wT, b2r[:], None, b2_ps)

                    layer_input(0)
                    projections(0)
                    attention(0)
                    recurrence_inputs()
                    finish_attention(0)
                    pe.wait_ge(h2_ready, 1)
                    turn4(O_BANK, lambda i: flat_tok[:, i, :], h2T_ps)
                    experts(0)
                    layer_input(1)
                    projections(1)
                    attention(1)
                    finish_attention(1)
                    experts(1)

                @block.scalar
                def _(act):
                    def exp_unit(l, v):
                        w, pr = v // 2, v % 2
                        W = T - P * (w % NT)
                        o = probs[:, w % 4, 2 * pr:2 * pr + 2, 0:W]
                        if l == 0:
                            act.wait_ge(s2_ps[0], v + 1)
                            if w >= 4:
                                act.wait_ge(pv_done[0], w - 3)
                            b0 = UNIT_BANKS[v % 2][0]
                            nc.scalar.activation(o, ps[:, b0:b0 + 2, 0:W], ACT.Exp).then_inc(p_ready[0], 1)
                        else:
                            act.wait_ge(biased, v + 1)
                            nc.scalar.activation(o, o, ACT.Exp).then_inc(p_ready[1], 1)

                    def read_output(l, g):
                        act.wait_ge(pv_done[l], NT * (g + 1))
                        if g >= 2:
                            act.wait_ge(small_ps[l], small_use[("out", g - 2)])
                        nc.scalar.copy(o_sb[:, g % 2, :], ps[:, O_BANK, :]).then_inc(osb_ready[l], 1)

                    def front(l):
                        act.wait_ge(xnT_ps[l], 1)
                        nc.scalar.copy(xnT[:], ps[:, T_BANKS[0], :]).then_inc(xnT_ready[l], 1)
                        if l == 0:
                            act.wait_ge(hT_ps, 1)
                            nc.scalar.activation(hT[:], ps[:, T_BANKS[1], :], ACT.Identity, bias=B1, scale=G1)\
                                .then_inc(hT_ready, 1)
                        act.wait_ge(proj_ps[l], 2)
                        nc.scalar.activation(k32[:], ps[:, K_BANK, :], ACT.Identity, bias=BK[l], scale=1.0)\
                            .then_inc(k32_ready[l], 1)
                        act.wait_ge(proj_ps[l], 3)
                        nc.scalar.copy(vAug[:, :, :, 0:HD],
                                       ps[:, V_BANK, :].rearrange("p (a h i) -> p a h i", a=NT, h=H))\
                            .then_inc(v_ready[l], 1)
                        if l == 1:
                            act.wait_ge(proj_ps[1], 4)
                            nc.scalar.activation(gateT[:], ps[:, GATE_BANK, :], ACT.Sigmoid, bias=BG1, scale=1.0)\
                                .then_inc(gate_ready, 1)

                    def attention(l):
                        for v in range(NUNIT):
                            exp_unit(l, v)
                            if v % 8 == 0 and v >= 8:
                                read_output(l, v // 8 - 1)
                        read_output(l, G - 1)

                    def recurrence_inputs():
                        act.wait_ge(bcd_ps, 2)
                        nc.scalar.activation(sp1, ps[:, C_BANK, :], ACT.Abs).then_inc(act_seq, 1)
                        act.wait_ge(act_seq, 1)
                        nc.scalar.activation(sp2, sp1, ACT.Exp, scale=-1.0).then_inc(act_seq, 1)
                        act.wait_ge(act_seq, 2)
                        nc.scalar.activation(sp1, sp2, ACT.Ln, bias=1.0).then_inc(sp_ready, 1)

                    def decays():
                        act.wait_ge(dt_ready, 1)
                        act.wait_ge(pv_done[0], G * NT)
                        for m in range(N):
                            nc.scalar.activation(probs[:, m // 4, m % 4, :], dt, ACT.Exp, scale=negA[:, m:m + 1])\
                                .then_inc(dA_ready, 1)

                    def routing_exp(l):
                        act.wait_ge(ex_in[l], 1)
                        nc.scalar.activation(ex[:], ex[:], ACT.Exp).then_inc(ex_ready[l], 1)

                    def experts(l):
                        for n in range(NF):
                            act.wait_ge(mid_ps[l], n + 1)
                            if n >= 4:
                                act.wait_ge(mid_used[l], n - 3)
                            nc.scalar.activation(mid[:, n % 4, :], ps[:, MID_BANKS[n % 2], :], ACT.Gelu,
                                                 bias=b1c[:, n:n + 1] if l == 0 else 0.0, scale=1.0)\
                                .then_inc(mid_ready[l], 1)
                            if l == 0 and n == 4:
                                act.wait_ge(wT_ps, 1)
                                nc.scalar.copy(wT[:], ps[0:E, MISC_BANK, :]).then_inc(wT_ready, 1)
                        act.wait_ge(acc_done[l], E)
                        nc.scalar.activation(flat_tok, acc[:], ACT.Silu).then_inc(silu_ready[l], 1)

                    front(0)
                    attention(0)
                    act.wait_ge(fT_ps[0], 1)
                    nc.scalar.copy(oT[:], ps[:, O_BANK, :]).then_inc(oT_ready[0], 1)
                    recurrence_inputs()
                    act.wait_ge(h2T_ps, 1)
                    nc.scalar.activation(hT[:], ps[:, O_BANK, :], ACT.Identity, bias=B2, scale=G2)\
                        .then_inc(h2T_ready, 1)
                    decays()
                    routing_exp(0)
                    experts(0)
                    front(1)
                    attention(1)
                    act.wait_ge(att_ps[1], 1)
                    nc.scalar.copy(a_tok[:].rearrange("p a d -> p (a d)"), ps[:, PROJ_BANK, :])\
                        .then_inc(s1_ready, 1)
                    routing_exp(1)
                    experts(1)

                @block.gpsimd
                def _(pool):
                    def rsqrt(n, dst):
                        pool.wait_ge(var_ready[n], 1)
                        nc.gpsimd.tensor_tensor(dst[:], ve[:], minus_half[:], ALU.pow).then_inc(rstd_ready[n], 1)

                    seq = [0]

                    def step(ins):
                        seq[0] += 1
                        ins.then_inc(pool_seq, 1)
                        pool.wait_ge(pool_seq, seq[0])

                    def k_split(l):
                        pool.wait_ge(k32_ready[l], 1)
                        nc.gpsimd.tensor_copy(kpart[0][:], k32[:]).then_inc(k_parts[l], 1)
                        pool.wait_ge(k_parts[l], 1)
                        step(nc.gpsimd.tensor_tensor(kres[:], k32[:], kpart[0][:], ALU.subtract))
                        nc.gpsimd.tensor_copy(kpart[1][:], kres[:]).then_inc(k_parts[l], 1)
                        pool.wait_ge(k_parts[l], 2)
                        nc.gpsimd.tensor_tensor(kpart[2][:], kres[:], kpart[1][:], ALU.subtract)\
                            .then_inc(k_parts[l], 1)

                    rsqrt(0, rstd)
                    rsqrt(1, rstd)
                    k_split(0)
                    pool.wait_ge(bcd_ps, 2)
                    nc.gpsimd.tensor_scalar(dx, xnT[:], D_COL, None, ALU.mult).then_inc(dx_ready, 1)
                    rsqrt(2, rstd)
                    rsqrt(3, rstd)
                    k_split(1)

                @block.vector
                def _(dve):
                    seq = [0]

                    def step(ins):
                        seq[0] += 1
                        ins.then_inc(dve_seq, 1)
                        dve.wait_ge(dve_seq, seq[0])

                    def moments(src, n):
                        for i in range(NT):
                            ins = nc.vector.bn_stats(stats[:, i, :], src[:, i, :])
                        step(ins)
                        for i in range(NT):
                            ins = nc.vector.bn_aggr(mv[:, i, :], stats[:, i, :])
                        step(ins)
                        nc.vector.tensor_scalar(ve[:], mv[:, :, 1], EPS, None, ALU.add).then_inc(var_ready[n], 1)

                    def normalize(dst, src, n, signal):
                        dve.wait_ge(rstd_ready[n], 1)
                        for i in range(NT):
                            ins = nc.vector.tensor_scalar(dst[:, i, :], src[:, i, :], mv[:, i, 0:1],
                                                          rstd[:, i:i + 1], ALU.subtract, ALU.mult)
                        ins.then_inc(signal, 1)
                        dve.wait_ge(signal, 1)

                    def q_split(l):
                        dve.wait_ge(proj_ps[l], 1)
                        step(nc.vector.tensor_scalar(q32[:], ps[:, Q_BANK, :], BQ[l], SCALE, ALU.add, ALU.mult))
                        nc.vector.tensor_copy(qpart[0][:], q32[:]).then_inc(q_parts[l], 1)
                        dve.wait_ge(q_parts[l], 1)
                        step(nc.vector.tensor_tensor(qres[:], q32[:], qpart[0][:], ALU.subtract))
                        nc.vector.tensor_copy(qpart[1][:], qres[:]).then_inc(q_parts[l], 1)
                        dve.wait_ge(q_parts[l], 2)
                        nc.vector.tensor_tensor(qpart[2][:], qres[:], qpart[1][:], ALU.subtract)\
                            .then_inc(q_parts[l], 1)

                    def row_max(l, m):
                        i = m % NT
                        s = ps[:, MAX_BANKS[m % 2], 0:P * (i + 1)]
                        extra = mask_q[:, window(i)] if l == 0 else bias_q[:, m // NT, window(i)]
                        dve.wait_ge(s1_ps[l], m + 1)
                        nc.vector.tensor_tensor_reduce(out=s, in0=s, in1=extra, scale=1.0, scalar=LOWEST,
                                                       op0=ALU.add, op1=ALU.max, accum_out=maxq[:, m:m + 1])\
                            .then_inc(max_done[l], 1)

                    def max_parts(l, g):
                        t = ps[0:16, SMALL_BANK, 0:P]
                        dve.wait_ge(small_ps[l], small_use[("turn", g)])
                        if g >= 2:
                            dve.wait_ge(m_rows[g % 2][l], 32 * (g // 2))
                        step(nc.vector.tensor_scalar(mparts[:, g % 2, 0, :], t, -1.0, None, ALU.mult))
                        nc.vector.scalar_tensor_tensor(out=mparts[:, g % 2, 1, :], in0=t, scalar=-1.0,
                                                       in1=mparts[:, g % 2, 0, :], op0=ALU.mult,
                                                       op1=ALU.subtract).then_inc(small_free[l], 1)

                    def add_bias(v):
                        w, pr = v // 2, v % 2
                        W = T - P * (w % NT)
                        h = 4 * (v // 8) + 2 * pr
                        b0 = UNIT_BANKS[v % 2][0]
                        dve.wait_ge(s2_ps[1], v + 1)
                        if w >= 4:
                            dve.wait_ge(pv_done[1], w - 3)
                        nc.vector.tensor_tensor(probs[:, w % 4, 2 * pr:2 * pr + 2, 0:W], ps[:, b0:b0 + 2, 0:W],
                                                bias_kT[:, h:h + 2, 0:W], ALU.add).then_inc(biased, 1)

                    def divide_output(l, g):
                        o = ps[:, SMALL_BANK, :].rearrange("p (a j c) -> p a j c", a=NT, j=4)
                        dve.wait_ge(small_ps[l], small_use[("out", g)])
                        step(nc.vector.reciprocal(recip[:], o[:, :, :, HD]))
                        nc.vector.tensor_tensor(flat[:, :, 4 * g:4 * g + 4, :], o[:, :, :, 0:HD],
                                                recip[:].unsqueeze(3).to_broadcast([P, NT, 4, HD]), ALU.mult)\
                            .then_inc(small_free[l], 1)

                    def attention(l):
                        if l == 1:
                            dve.wait_ge(bias_loaded, 32)
                        for kind, n in order:
                            if kind == "max":
                                row_max(l, n)
                            elif kind == "turn":
                                max_parts(l, n)
                            elif kind == "unit":
                                if l == 1:
                                    add_bias(n)
                            else:
                                divide_output(l, n)

                    def recurrence_inputs():
                        z = ps[0:96, B_BANK, :]
                        dve.wait_ge(bcd_ps, 1)
                        step(nc.vector.tensor_copy(bcS[:], z))
                        step(nc.vector.tensor_tensor(bcR[:], z, bcS[:], ALU.subtract))
                        nc.vector.tensor_copy(bcS[32:64, :], bcR[32:64, :])
                        step(nc.vector.tensor_copy(bcS[64:96, :], bcR[64:96, :]))
                        step(nc.vector.tensor_tensor(bcR[64:96, :], bcR[64:96, :], bcS[64:96, :], ALU.subtract))
                        nc.vector.tensor_copy(bcS[64:96, :], bcR[64:96, :]).then_inc(bc_ready, 1)
                        dve.wait_ge(sp_ready, 1)
                        nc.vector.scalar_tensor_tensor(out=dt, in0=ps[:, C_BANK, :], scalar=0.0, in1=sp1,
                                                       op0=ALU.max, op1=ALU.add).then_inc(dt_ready, 1)
                        dve.wait_ge(dt_ready, 1)
                        nc.vector.tensor_tensor(dtx, dt, xnT[:], ALU.mult).then_inc(dtx_ready, 1)

                    def state_step(m):
                        if m < N:
                            dve.wait_ge(b_ps, m + 1)
                            if m == 0:
                                dve.wait_ge(dtx_ready, 1)
                            if m >= 2:
                                dve.wait_ge(scanned, m - 1)
                            nc.vector.tensor_tensor(u_buf[m % 2], dtx, ps[:, B_BANK, :], ALU.mult)\
                                .then_inc(b_used, 1)
                        if m >= 1:
                            dve.wait_ge(scanned, m)
                            dve.wait_ge(c_ps, m)
                            if m >= 3:
                                dve.wait_ge(s_acc, m - 1)
                            nc.vector.tensor_tensor(p_buf[(m - 1) % 2], h_buf[(m - 1) % 2], ps[:, C_BANK, :],
                                                    ALU.mult).then_inc(c_used, 1)
                        if m < N:
                            dve.wait_ge(b_used, m + 1)
                            dve.wait_ge(dA_ready, m + 1)
                            if m >= 2:
                                dve.wait_ge(c_used, m - 1)
                            nc.vector.tensor_tensor_scan(h_buf[m % 2], probs[:, m // 4, m % 4, :], u_buf[m % 2],
                                                         0.0, ALU.mult, ALU.add).then_inc(scanned, 1)

                    def routing(l):
                        def wide(ap):
                            return ap.to_broadcast([P, NT, E])

                        dve.wait_ge(lg_ps[l], 1)
                        step(nc.vector.tensor_copy(logits[:].rearrange("p a e -> p (a e)"),
                                                   ps[:, MISC_BANK, 0:NT * E]))
                        for i in range(NT):
                            ins = nc.vector.max(top8[:, i, :], logits[:, i, :])
                        step(ins)
                        nc.vector.tensor_tensor(ex[:], logits[:], wide(top8[:, :, 0:1]), ALU.subtract)\
                            .then_inc(ex_in[l], 1)
                        if l == 0:
                            step(nc.vector.tensor_tensor(gt[:], logits[:], wide(top8[:, :, 1:2]), ALU.is_ge))
                        else:
                            nc.vector.tensor_tensor(gt[:], logits[:], wide(top8[:, :, 1:2]), ALU.is_gt)
                            step(nc.vector.tensor_tensor(eq[:], logits[:], wide(top8[:, :, 1:2]), ALU.is_equal))
                            nc.vector.tensor_reduce(cnt[:], gt[:], AX.X, ALU.add)
                            step(nc.vector.tensor_tensor_scan(rank[:].rearrange("p a e -> p (a e)"),
                                                              keep[:].rearrange("p a e -> p (a e)"),
                                                              eq[:].rearrange("p a e -> p (a e)"),
                                                              0.0, ALU.mult, ALU.add))
                            step(nc.vector.tensor_tensor(rank[:], rank[:], wide(cnt[:].unsqueeze(2)), ALU.add))
                            step(nc.vector.tensor_scalar(rank[:], rank[:], 2.5, None, ALU.is_le))
                            step(nc.vector.tensor_tensor(eq[:], eq[:], rank[:], ALU.mult))
                            step(nc.vector.tensor_tensor(gt[:], gt[:], eq[:], ALU.add))
                        dve.wait_ge(ex_ready[l], 1)
                        step(nc.vector.tensor_tensor(gt[:], ex[:], gt[:], ALU.mult))
                        step(nc.vector.tensor_reduce(tsum[:], gt[:], AX.X, ALU.add))
                        step(nc.vector.reciprocal(cnt[:], tsum[:]))
                        nc.vector.tensor_tensor(wts[:], gt[:], wide(cnt[:].unsqueeze(2)), ALU.mult)\
                            .then_inc(w_ready[l], 1)
                        dve.wait_ge(w_ready[l], 1)

                    def add_expert(l, e):
                        dve.wait_ge(mid_used[l], FT * (e + 1))
                        if e >= 1:
                            dve.wait_ge(acc_done[l], e)
                        for i in range(NT):
                            o, w = ps[:, OUT_BANKS[e % 2], tile(i)], wts[:, i, e:e + 1]
                            if l == 1 and e == 0:
                                ins = nc.vector.tensor_scalar(acc[:, i, :], o, w, None, ALU.mult)
                            else:
                                ins = nc.vector.scalar_tensor_tensor(out=acc[:, i, :], in0=o, scalar=w,
                                                                     in1=acc[:, i, :], op0=ALU.mult, op1=ALU.add)
                        ins.then_inc(acc_done[l], 1)

                    def update(l, s):
                        dve.wait_ge(silu_ready[l], 1)
                        nc.vector.tensor_tensor(a_tok[:], s, flat_tok, ALU.mult).then_inc(prod_ready[l], 1)
                        dve.wait_ge(prod_ready[l], 1)
                        nc.vector.tensor_tensor(x_tok[:], x_tok[:], a_tok[:], ALU.add).then_inc(x_ready[l], 1)

                    dve.wait_ge(x_loaded, 16)
                    moments(x_tok, 0)
                    normalize(xn_tok, x_tok, 0, xn_ready[0])
                    step(nc.vector.tensor_tensor(ve[:], mv[:, :, 1], rstd[:], ALU.mult))
                    step(nc.vector.tensor_tensor(ve[:], ve[:], rstd[:], ALU.mult))
                    nc.vector.tensor_scalar(ve[:], ve[:], EPS, None, ALU.add).then_inc(var_ready[1], 1)
                    dve.wait_ge(rstd_ready[1], 1)
                    for i in range(NT):
                        ins = nc.vector.tensor_scalar(a_tok[:, i, :], xn_tok[:, i, :], rstd[:, i:i + 1], None,
                                                      ALU.mult)
                    ins.then_inc(hh_ready, 1)
                    q_split(0)
                    attention(0)
                    recurrence_inputs()
                    dve.wait_ge(att_ps[0], 1)
                    nc.vector.tensor_tensor(a_tok[:].rearrange("p a d -> p (a d)"), ps[:, PROJ_BANK, :],
                                            xn_tok[:].rearrange("p a d -> p (a d)"), ALU.add).then_inc(a_ready, 1)
                    dve.wait_ge(a_ready, 1)
                    moments(a_tok, 2)
                    normalize(flat_tok, a_tok, 2, h2_ready)
                    routing(0)
                    for e in range(E):
                        state_step(2 * e)
                        state_step(2 * e + 1)
                        if e == 1:
                            dve.wait_ge(b2_ps, 1)
                            nc.vector.tensor_tensor(acc[:].rearrange("p a d -> p (a d)"), ps[:, MISC_BANK, :],
                                                    a_tok[:].rearrange("p a d -> p (a d)"), ALU.add)\
                                .then_inc(acc_init, 1)
                            dve.wait_ge(acc_init, 1)
                        if e >= 1:
                            add_expert(0, e - 1)
                    state_step(N)
                    add_expert(0, E - 1)
                    dve.wait_ge(s_acc, N + 1)
                    update(0, ps[:, S_BANK, :].rearrange("p (a d) -> p a d", a=NT))

                    dve.wait_ge(x_ready[0], 1)
                    moments(x_tok, 3)
                    normalize(xn_tok, x_tok, 3, xn_ready[1])
                    q_split(1)
                    attention(1)
                    dve.wait_ge(fT_ps[1], 1)
                    nc.vector.tensor_tensor(oT[:], ps[:, O_BANK, :], gateT[:], ALU.mult).then_inc(oT_ready[1], 1)
                    routing(1)
                    for e in range(E):
                        add_expert(1, e)
                    update(1, a_tok[:])

            nums = [s.num for s in loop_sems]
            assert nums == list(range(nums[0], nums[0] + len(nums)))
            nc.multi_engine_barrier(list(nc.engines), sems_to_clear=range(nums[0], nums[-1] + 1))


def kernel(**inputs):
    import numpy as np
    import concourse.bacc as bacc
    from concourse.bass_utils import run_bass_kernel_spmd

    v = {k: np.asarray(a) for k, a in inputs.items()}
    x = v["L0_attn_x"]
    D = x.shape[2]
    N = v["L0_attn_A_log"].shape[0]
    H, HD, FT = 16, D // 16, v["L0_ffn_e_w1"].shape[2] // 128
    by_dim = np.arange(D).reshape(H, HD).T.ravel()
    Wx = v["L0_attn_Wx"]
    Wqkv, bqkv = v["L1_attn_Wqkv"], v["L1_attn_bqkv"]
    E, F = v["L0_ffn_e_b1"].shape
    data = {
        "x": x,
        "A_log": v["L0_attn_A_log"].reshape(1, N),
        "pos_bias": v["L1_attn_pos_bias"],
        "pos_biasT": v["L1_attn_pos_bias"].T,
        "offsets": v["L1_attn_offsets"],
        "cols": np.stack([v["L0_attn_D"], v["L0_ffn_ln1_g"], v["L0_ffn_ln1_b"], v["L0_ffn_ln2_g"],
                          v["L0_ffn_ln2_b"], v["L0_ffn_bq"][by_dim], v["L0_ffn_bk"][by_dim],
                          bqkv[:D][by_dim], bqkv[D:2 * D][by_dim], v["L1_attn_bgate"]], axis=1),
        "rows": np.concatenate([v["L0_ffn_bv"], v["L0_ffn_bo"], bqkv[2 * D:], v["L1_attn_bout"],
                                v["L0_ffn_br"]])[None, :],
        "b1": v["L0_ffn_e_b1"].reshape(E * FT, 128).T,
        "b2": v["L0_ffn_e_b2"],
        "wbc": np.concatenate([Wx[:2 * N].T] * 3, axis=1),
        "wdelta": Wx[2 * N:].T,
        "wout0": v["L0_attn_Wout"].T,
        "wq0": v["L0_ffn_Wq"][:, by_dim], "wk0": v["L0_ffn_Wk"][:, by_dim],
        "wv0": v["L0_ffn_Wv"], "wo0": v["L0_ffn_Wo"], "wr0": v["L0_ffn_Wr"],
        "wq1": Wqkv[:D][by_dim].T, "wk1": Wqkv[D:2 * D][by_dim].T, "wv1": Wqkv[2 * D:].T,
        "wgate1": v["L1_attn_Wgate"].T, "wo1": v["L1_attn_Wout"].T, "wr1": v["L1_ffn_router_w"].T,
        "w1_0": v["L0_ffn_e_w1"].transpose(1, 0, 2),
        "w2_0": v["L0_ffn_e_w2"].reshape(E * FT, 128, D).transpose(1, 0, 2),
        "w1_1": v["L1_ffn_expert_w1"].transpose(2, 0, 1),
        "w2_1": v["L1_ffn_expert_w2"].transpose(2, 0, 1).reshape(FT, 128, E, D).transpose(1, 2, 0, 3)
                .reshape(128, E * FT, D),
    }
    nc = bacc.Bacc("TRN2", target_bir_lowering=False, num_devices=1)
    arrays, aps = {}, {}
    for name, a in data.items():
        a = np.ascontiguousarray(a)
        arrays["in_" + name] = a
        aps[name] = nc.dram_tensor("in_" + name, a.shape, mybir.dt.from_np(a.dtype), kind="ExternalInput").ap()
    out = nc.dram_tensor("out_0", x.shape, mybir.dt.float32, kind="ExternalOutput").ap()
    build(nc, aps, out)
    r = run_bass_kernel_spmd(nc, [arrays], core_ids=[0])
    return r.results[0]["out_0"]
```

```python
from contextlib import ExitStack

import concourse.bass as bass
from concourse import mybir

F32 = mybir.dt.float32
BF16 = mybir.dt.bfloat16
I32 = mybir.dt.int32
ACT = mybir.ActivationFunctionType
ALU = mybir.AluOpType
AX = mybir.AxisListType

P = 128
NEG = -1.0e30
LOWEST = -3.0e38
EPS = 1e-5
PARTS = 3
VW = 32
WSLOTS = 4
MIDS = 8

RING_BANKS = (0, 1, 2, 3)
O_BANK = 4
SMALL_BANK = 5
OUT_BANK = 6
BC_BANK = 7


def build(nc, d, out):
    B, T, D = d["x"].shape
    NT = T // P
    N = d["A_log"].shape[1]
    NO, H = d["pos_bias"].shape
    HD = D // H
    E = d["b2"].shape[0]
    F = d["w1_0"].shape[2]
    FT = F // P
    NF = E * FT
    SCALE = float(HD) ** -0.5
    PAIRS = PARTS * PARTS
    KR = PAIRS * HD
    G = H // 4
    LBW = T + P
    assert D == P and HD == 8 and NT == 4 and G * NT == 16

    with ExitStack() as ctx:
        def sb(name, shape, dt=F32):
            return ctx.enter_context(nc.sbuf_tensor(name, shape, dt))

        def sem(name):
            return ctx.enter_context(nc.semaphore(name))

        ident = sb("ident", [P, P])
        ident_bf = sb("ident_bf", [P, P], BF16)
        bcast_sel = sb("bcast_sel", [3 * 32, 32], BF16)
        ones_row = sb("ones_row", [1, P])
        ones_bf = sb("ones_bf", [H, T], BF16)
        minus_half = sb("minus_half", [P, NT])
        mask_q = sb("mask_q", [P, T], BF16)
        mask_kT = sb("mask_kT", [P, P], BF16)
        cols = sb("cols", [P, d["cols"].shape[1]])
        rows = sb("rows", [1, d["rows"].shape[1]])
        b1c = sb("b1c", [P, NF])
        b2r = sb("b2r", [E, D])
        negA = sb("negA", [P, N])
        wbc = sb("wbc", [P, 3 * 32])
        wdelta = sb("wdelta", [P, D])
        wmat = {k: sb("w_" + k, [P, d[k].shape[1]]) for k in
                ("wq0", "wk0", "wv0", "wo0", "wr0", "wout0", "wq1", "wk1", "wv1", "wgate1", "wo1", "wr1")}
        bias_q = sb("bias_q", [P, H, T], BF16)
        bias_kT = sb("bias_kT", [P, H, T])
        bias_loaded = sem("bias_loaded")
        D_COL, G1, B1, G2, B2, BQ0, BK0, BQ1, BK1, BG1 = (cols[:, i:i + 1] for i in range(10))
        BV0, BO0, BV1, BO1 = (rows[0:1, i * D:(i + 1) * D] for i in range(4))
        BR0 = rows[0:1, 4 * D:4 * D + E]

        xn0 = sb("xn0", [P, NT, D])
        xcur = sb("xcur", [P, NT, D])
        g_tok = sb("g_tok", [P, NT, D])
        a_tok = sb("a_tok", [P, NT, D])
        s_tok = sb("s_tok", [P, NT, D])
        acc = sb("acc", [P, NT, D])
        acc_next = sb("acc_next", [P, NT, D])
        xnT = (sb("xnT0", [P, T]), sb("xnT1", [P, T]))
        h2T = sb("h2T", [P, T])
        oT = sb("oT", [P, T])
        gateT = sb("gateT", [P, T])
        flat = sb("flat", [P, NT, H, HD])
        stats = sb("stats", [P, NT, 6])
        mv = sb("mv", [P, NT, 2])
        ve = sb("ve", [P, NT])
        rstd = sb("rstd", [P, NT])
        stackQ = sb("stackQ", [P, H, T], BF16)
        stackK = sb("stackK", [P, H, T], BF16)
        vAug = sb("vAug", [P, NT, H, VW])
        maxq = sb("maxq", [P, G * 16])
        mparts = sb("mparts", [16, 2, 2, P], BF16)
        probs_all = sb("probs_all", [P, 4 * (4 + 3 + 2 + 1) * P])
        o_sb = sb("o_sb", [P, 2, T])
        recip = sb("recip", [P, NT, 4])
        w1s = sb("w1s", [P, WSLOTS, F])
        w2s = sb("w2s", [P, WSLOTS, FT, D])
        mid = sb("mid", [P, MIDS, T])
        logits = sb("logits", [P, NT, E])
        top8 = sb("top8", [P, NT, 8])
        ex = sb("ex", [P, NT, E])
        gt = sb("gt", [P, NT, E])
        eq = sb("eq", [P, NT, E])
        rank = sb("rank", [P, NT, E])
        keep = sb("keep", [P, NT, E])
        wts = (sb("wts0", [P, NT, E]), sb("wts1", [P, NT, E]))
        tsum = sb("tsum", [P, NT])
        cnt = sb("cnt", [P, NT])
        bcS = sb("bcS", [3 * 32, T], BF16)
        dA = sb("dA", [P, 3, T])
        u_buf = sb("u_buf", [P, 2, T])
        h_buf = sb("h_buf", [P, 3, T])
        dt = sb("dt", [P, T])
        y = sb("y", [P, T])

        flat_tok = flat[:].rearrange("p a h i -> p a (h i)")
        x_next = flat_tok
        xn1 = g_tok
        hT = oT
        wT = oT[0:E, :]
        dtx = xnT[0]
        sp, bcR = u_buf[:, 0, :], u_buf[0:96, 1, :]
        at, probs = 0, []
        for kt in range(NT):
            W = T - P * kt
            probs.append(probs_all[:, at:at + 4 * W].rearrange("p (j t) -> p j t", j=4))
            at += 4 * W
        q32, qres, k32, kres = (probs_all[:, i * T:(i + 1) * T] for i in range(4))
        half = probs_all[:, 4 * T:7 * T].bitcast(BF16)
        qpart = [half[:, i * T:(i + 1) * T] for i in range(PARTS)]
        kpart = [half[:, (PARTS + i) * T:(PARTS + i + 1) * T] for i in range(PARTS)]

        ps = ctx.enter_context(nc.psum_tensor("ps", [P, 8, T], F32))
        scrF = nc.dram_tensor("scrF", [P, H, LBW], F32).ap()
        scrR = nc.dram_tensor("scrR", [P, H, LBW], BF16).ap()

        ld, ld_first = sem("ld"), sem("ld_first")
        pool_step, dve_step, act_step, pe_step = (sem(n) for n in ("pool_step", "dve_step", "act_step", "pe_step"))
        rows_ready, bias_written = sem("rows_ready"), sem("bias_written")

        fQ, fK = (bias_kT[:, i * H // 2:(i + 1) * H // 2, :].rearrange("p h t -> p (h t)") for i in range(2))
        off_ci, off_ri = fQ[0:NO, 0:1].bitcast(I32), fQ[0:NO, 8:8 + NO].bitcast(I32)
        off_c, off_r = fQ[0:NO, 96:97], fQ[0:NO, 104:104 + NO]
        same, apart, before = (fQ[0:NO, a:a + NO] for a in (200, 300, 400))
        dup, first = fQ[0:NO, 500:501], fQ[0:NO, 501:502]
        iota_i = fQ[0:NO, 512:512 + 2 * T].bitcast(I32)
        iota_f = fQ[0:NO, 1536:1536 + 2 * T]
        onehot = fQ[0:NO, 2560:2560 + 2 * T]
        pbmax, pbsum, joint, ones_oh = (fQ[0:NO, a:a + H] for a in (3600, 3620, 3640, 3660))
        pb = fK[0:NO, 0:H * NO].rearrange("p (h o) -> p h o", h=H)
        biasrow = fK[0:H, 1100:1100 + 2 * LBW]
        pen = fK[0:H, 2400:2400 + 2 * T]
        rev_bf = fK[0:H, 3440:3440 + LBW // 2].bitcast(BF16)
        N_LD = 6 + len(wmat)

        with nc.Block() as block:
            @block.sync
            def _(sp):
                sp.dma_start(off_ci, d["offsets"].rearrange("(o a) -> o a", a=1)).then_inc(ld_first, 16)
                sp.dma_start(off_ri, d["offsets"].partition_broadcast(NO)).then_inc(ld_first, 16)
                sp.dma_start(pb, d["pos_biasT"].partition_broadcast(NO)).then_inc(ld_first, 16)
                sp.dma_start(negA[:], d["A_log"][0, :].partition_broadcast(P)).then_inc(ld_first, 16)
                sp.dma_start(cols[:], d["cols"]).then_inc(ld, 16)
                sp.dma_start(rows[:], d["rows"]).then_inc(ld, 16)
                sp.dma_start(b1c[:], d["b1"]).then_inc(ld, 16)
                sp.dma_start(b2r[:], d["b2"]).then_inc(ld, 16)
                sp.dma_start(wbc[:], d["wbc"]).then_inc(ld, 16)
                sp.dma_start(wdelta[:], d["wdelta"]).then_inc(ld, 16)
                for k, w in wmat.items():
                    sp.dma_start(w[:], d[k]).then_inc(ld, 16)
                sp.wait_ge(pool_step, 1)
                for row in (KR, KR + 1):
                    sp.dma_start(stackK[row:row + 1, :, :], ones_bf[:]).then_inc(ld, 16)
                sp.wait_ge(ld, 16 * (N_LD + 2))

            @block.gpsimd
            def _(pool):
                nc.gpsimd.memset(ident[:], 0.0)
                nc.gpsimd.memset(mask_q[:], 0.0)
                nc.gpsimd.memset(ones_bf[:], 1.0)
                nc.gpsimd.memset(ones_row[:], 1.0)
                nc.gpsimd.memset(minus_half[:], -0.5)
                nc.gpsimd.memset(keep[:], 1.0)
                nc.gpsimd.memset(vAug[:], 0.0).then_inc(pool_step, 1)
                nc.gpsimd.iota(iota_i[:, 0:T], pattern=[[1, T]], base=0, channel_multiplier=0)
                nc.gpsimd.iota(iota_i[:, T:2 * T], pattern=[[-1, T]], base=T - 1,
                               channel_multiplier=0).then_inc(pool_step, 1)
                pool.wait_ge(pool_step, 1)
                nc.gpsimd.memset(keep[:, :, 0:1], 0.0)
                nc.gpsimd.memset(vAug[:, :, :, HD:HD + 1], 1.0)
                nc.gpsimd.affine_select(out=ident[:], in_=ident[:], compare_op=ALU.not_equal, fill=1.0,
                                        base=0, pattern=[[-1, P]], channel_multiplier=1)
                nc.gpsimd.affine_select(out=mask_kT[:], in_=mask_q[:, 0:P], compare_op=ALU.is_ge,
                                        fill=NEG, base=0, pattern=[[1, P]], channel_multiplier=-1)
                nc.gpsimd.affine_select(out=mask_q[:, T - P:T], in_=mask_q[:, T - P:T], compare_op=ALU.is_ge,
                                        fill=NEG, base=0, pattern=[[-1, P]],
                                        channel_multiplier=1).then_inc(pool_step, 1)
                pool.wait_ge(pool_step, 3)
                nc.gpsimd.tensor_copy(ident_bf[:], ident[:]).then_inc(pool_step, 1)
                for r in range(3):
                    pool.wait_ge(pool_step, 4 + r)
                    nc.gpsimd.tensor_copy(bcast_sel[32 * r:32 * r + 32, :],
                                          ident[32 * r:32 * r + 32, 32 * r:32 * r + 32]).then_inc(pool_step, 1)
                pool.wait_ge(pool_step, 7)
                pool.wait_ge(dve_step, 3)
                nc.gpsimd.affine_select(out=before, in_=same, compare_op=ALU.is_gt, fill=0.0,
                                        base=0, pattern=[[-1, NO]],
                                        channel_multiplier=1).then_inc(pool_step, 1)

            @block.scalar
            def _(act):
                act.wait_ge(ld_first, 64)
                nc.scalar.activation(negA[:], negA[:], ACT.Exp).then_inc(act_step, 1)
                act.wait_ge(dve_step, 7)
                nc.scalar.activation(pb, pb, ACT.Exp).then_inc(act_step, 1)
                act.wait_ge(dve_step, 8)
                nc.scalar.activation(pbsum, pbsum, ACT.Ln).then_inc(act_step, 1)

            @block.tensor
            def _(pe):
                pe.wait_ge(dve_step, 14)
                for r in range(2):
                    oh = onehot[:, r * T:(r + 1) * T]
                    nc.tensor.matmul(ps[0:H, r, :], joint, oh, start=True, stop=True)
                    nc.tensor.matmul(ps[0:H, 2 + r, :], ones_oh, oh, start=True, stop=True).then_inc(pe_step, 1)

            @block.vector
            def _(dve):
                done = [0]

                def step(ins):
                    done[0] += 1
                    ins.then_inc(dve_step, 1)
                    dve.wait_ge(dve_step, done[0])

                dve.wait_ge(ld_first, 64)
                step(nc.vector.tensor_copy(off_c, off_ci))
                step(nc.vector.tensor_copy(off_r, off_ri))
                step(nc.vector.tensor_scalar(same, off_r, off_c, None, ALU.is_equal))
                step(nc.vector.tensor_scalar(apart, same, -1.0, -NEG, ALU.add, ALU.mult))
                step(nc.vector.tensor_tensor(pb, pb, apart.unsqueeze(1).to_broadcast([NO, H, NO]), ALU.add))
                step(nc.vector.tensor_reduce(pbmax, pb, AX.X, ALU.max))
                step(nc.vector.tensor_tensor(pb, pb, pbmax.unsqueeze(2).to_broadcast([NO, H, NO]),
                                             ALU.subtract))
                dve.wait_ge(act_step, 2)
                step(nc.vector.tensor_reduce(pbsum, pb, AX.X, ALU.add))
                dve.wait_ge(act_step, 3)
                step(nc.vector.tensor_tensor(joint, pbsum, pbmax, ALU.add))
                dve.wait_ge(pool_step, 8)
                step(nc.vector.tensor_reduce(dup, before, AX.X, ALU.add))
                step(nc.vector.tensor_scalar(first, dup, 0.0, None, ALU.is_equal))
                step(nc.vector.tensor_copy(iota_f, iota_i))
                step(nc.vector.memset(ones_oh, 1.0))
                step(nc.vector.tensor_scalar(onehot, iota_f, off_c, first, ALU.is_equal, ALU.mult))
                nc.vector.tensor_scalar(negA[:], negA[:], -1.0, None, ALU.mult)
                step(nc.vector.memset(biasrow, NEG))
                dve.wait_ge(pe_step, 2)
                step(nc.vector.tensor_scalar(pen.rearrange("h (a t) -> h a t", a=2), ps[0:H, 2:4, :],
                                             -1.0, -NEG, ALU.add, ALU.mult))
                nc.vector.tensor_tensor(biasrow[:, P - 1:P - 1 + T], ps[0:H, 0, :], pen[:, 0:T], ALU.add)
                step(nc.vector.tensor_tensor(biasrow[:, LBW:LBW + T], ps[0:H, 1, :], pen[:, T:2 * T], ALU.add))
                nc.vector.tensor_copy(rev_bf, biasrow[:, LBW:2 * LBW]).then_inc(rows_ready, 1)

        stackK_ready = sem("stackK_ready_0"), sem("stackK_ready_1")
        loop_sems = []

        def lsem(name):
            loop_sems.append(sem(name))
            return loop_sems[-1]

        def both(name):
            return lsem(name + "_0"), lsem(name + "_1")

        x_loaded, xcur_loaded, stored = (lsem(n) for n in ("x_loaded", "xcur_loaded", "stored"))
        dve_seq, act_seq = lsem("dve_seq"), lsem("act_seq")
        var_ready = [lsem(f"var_ready_{i}") for i in range(4)]
        rstd_ready = [lsem(f"rstd_ready_{i}") for i in range(4)]
        xn_ready = both("xn_ready")
        hh_ready, hT_ps, hT_ready, h2_ready = (lsem(n) for n in ("hh_ready", "hT_ps", "hT_ready", "h2_ready"))
        q_ps, k_ps, q32_ready, k32_ready = both("q_ps"), both("k_ps"), both("q32_ready"), both("k32_ready")
        gate_ps, gate_ready = lsem("gate_ps"), lsem("gate_ready")
        q_parts, k_parts, q_rest, k_rest = both("q_parts"), both("k_parts"), both("q_rest"), both("k_rest")
        stack_ready = both("stack_ready")
        s1_ps, max_done = both("s1_ps"), both("max_done")
        small_ps, small_free = lsem("small_ps"), lsem("small_free")
        m_rows = both("m_rows_even"), both("m_rows_odd")
        s2_ps, p_ready, pv_done, osb_ready = both("s2_ps"), both("p_ready"), both("pv_done"), both("osb_ready")
        biased = lsem("biased")
        bcd_ps, bc_ready, sp_ready, dt_ready, dtx_ready, y_ready = (
            lsem(n) for n in ("bcd_ps", "bc_ready", "sp_ready", "dt_ready", "dtx_ready", "y_ready"))
        dA_ready, b_ps, c_ps, b_used, scanned, c_used, y_added = (
            lsem(n) for n in ("dA_ready", "b_ps", "c_ps", "b_used", "scanned", "c_used", "y_added"))
        ex_in, ex_ready, w_ready = both("ex_in"), both("ex_ready"), both("w_ready")
        mid_ps, mid_ready, mid_used = both("mid_ps"), both("mid_ready"), both("mid_used")
        w_first_loaded = lsem("w_first_loaded")
        w_loaded = [both(f"w_loaded_{k}") for k in range(WSLOTS)]
        acc_done, silu_ready, prod_ready, x_ready = (
            both("acc_done"), both("silu_ready"), both("prod_ready"), both("x_ready"))

        units, pv_after = [], {}
        for g in range(G):
            for kt in range(NT):
                nh = (1, 1, 2, 4)[kt]
                for j in range(0, 4, nh):
                    units.append((g, kt, j, nh))
                pv_after[(g, kt)] = len(units)
        UPG = len(units) // G

        fills = []
        for h in range(0, H, 2):
            fills += [[(h, 0, 0), (h, 2, P)], [(h, 3, 0)], [(h, 1, 0), (h + 1, 1, 2 * P)],
                      [(h + 1, 0, 0), (h + 1, 2, P)], [(h + 1, 3, 0)]]
        FPG = len(fills) // G

        def steps(cur, nxt):
            place = []

            def put(t, *step):
                place.append((t, len(place), step))

            def spread(t0, t1, lst):
                for i, s in enumerate(lst):
                    put(t0 + (t1 - t0) * (i + 0.5) / len(lst), *s)

            def maxima(l, g, t0, t1):
                spread(t0, t1, [("max", l, f) for f in range(FPG * g, FPG * (g + 1))] + [("turn", l, g)])

            def group(l, g, t0, t1):
                lst, kt = [], 0
                for u in range(UPG * g, UPG * (g + 1)):
                    lst.append(("unit", l, u))
                    while kt < NT and u >= pv_after[(g, kt)] + 1:
                        lst.append(("pv", l, g, kt))
                        kt += 1
                lst += [("pv", l, g, k) for k in range(kt, NT)] + [("osb", l, g)]
                spread(t0, t1, lst)

            def first(l, r, t0, t1):
                spread(t0, t1, [("mm1", l, n) for n in range(8 * r, 8 * r + 8)])

            def second(l, r, t0, t1):
                lst = []
                for n in range(8 * r, 8 * r + 8):
                    lst.append(("mm2", l, n))
                    if n % FT == FT - 1:
                        lst.append(("add", l, n // FT))
                        e = l * E + n // FT + WSLOTS
                        if e < 2 * E or nxt:
                            lst.append(("weights", e // E, e % E))
                spread(t0, t1, lst)

            if nxt:
                put(7.7, "norm", 0)
                put(2.1, "turnx", 0)
                put(6.8, "turnhh")
                put(8.1, "proj", 0)
                put(10.8, "bc")
                put(37.3, "delta")
                maxima(0, 0, 20.6, 30.7)
                maxima(0, 1, 45.6, 65.4)
                maxima(0, 2, 68.9, 73.6)
                maxima(0, 3, 79.2, 90.4)
                for g, (t0, t1, t_out) in enumerate(((40.4, 57.3, 59.6), (70.5, 81.9, 91.2), (81.8, 91.3, 102.0), (100.9, 104.9, 107.2))):
                    group(0, g, t0, t1)
                    put(t_out, "out", 0, g)
                put(112.3, "flatT", 0)
                put(112.7, "attout", 0)
                put(125.9, "turnh")
                put(133.8, "route", 0)
                put(151.9, "rexp", 0)
                put(161.2, "wts", 0)
                put(166.1, "wT")
                put(183.6, "b2")
                at = [47.6, 53.7, 64.4, 71.9, 88.4, 91.9, 100.4, 106.3, 156.4, 168.8, 179.7, 185.6, 210.4, 221.1, 238.0, 243.1]
                for m, t in enumerate(at):
                    put(t, "dA", m)
                    put(t + 0.0, "stB", m)
                    put(t + 1.8, "stC", m)
                put(259.5, "sout")
            if not cur:
                put(102.3, "biases")
            if cur:
                first(0, 0, 0.0, 1.5)
                second(0, 0, 3.6, 19.9)
                first(0, 1, 5.2, 21.7)
                second(0, 1, 19.2, 32.2)
                first(0, 2, 24.1, 35.2)
                second(0, 2, 38.8, 57.7)
                first(0, 3, 56.0, 68.0)
                second(0, 3, 68.9, 74.9)
                put(74.2, "upd", 0)
                put(76.0, "norm", 1)
                put(97.4, "turnx", 1)
                put(101.0, "route", 1)
                put(101.6, "rexp", 1)
                put(106.9, "wts", 1)
                put(122.4, "proj", 1)
                first(1, 0, 108.3, 121.4)
                second(1, 0, 121.9, 147.4)
                first(1, 1, 124.6, 151.4)
                second(1, 1, 147.4, 158.6)
                first(1, 2, 151.1, 161.2)
                second(1, 2, 163.2, 171.9)
                first(1, 3, 170.3, 179.2)
                second(1, 3, 181.0, 189.3)
                maxima(1, 0, 148.2, 155.9)
                maxima(1, 1, 162.5, 178.1)
                maxima(1, 2, 177.3, 186.6)
                maxima(1, 3, 197.1, 226.9)
                for g, (t0, t1, t_out) in enumerate(((162.7, 172.1, 172.5), (183.2, 189.0, 202.5), (222.6, 234.6, 235.5), (231.8, 241.3, 241.5))):
                    group(1, g, t0, t1)
                    put(t_out, "out", 1, g)
                put(189.2, "silu", 1)
                put(243.4, "flatT", 1)
                put(245.2, "attout", 1)
                put(259.7, "upd", 1)
            return [s for _, _, s in sorted(place)]

        SMALL_STEPS = ("turnx", "projv", "turn", "out", "flatT", "attout", "turnh", "route", "wT", "b2", "sout")

        def window(i):
            return slice(T - P * (i + 1), T)

        def tile(i):
            return slice(i * P, (i + 1) * P)

        wq, wk, wv, wo, wr = ([wmat[n + s] for s in "01"] for n in ("wq", "wk", "wv", "wo", "wr"))
        BQ, BK, BV, BO = (BQ0, BQ1), (BK0, BK1), (BV0, BV1), (BO0, BO1)
        moe_in = (h2T, xnT[1])

        def segment(cur, nxt):
            has_cur, has_nxt = cur is not None, nxt is not None
            order = steps(has_cur, has_nxt)
            small_of, ring_of = {}, []
            for s in order:
                k = ("projv", s[1]) if s[0] == "proj" else s
                if k[0] in SMALL_STEPS:
                    small_of[k] = len(small_of) + 1
                if s[0] in ("mm1", "unit", "max"):
                    ring_of.append(s)
                if s[0] == "proj":
                    ring_of += [("q", s[1], 0)] + [("gate", 1, 0)] * s[1]
            ring_at = {s: i for i, s in enumerate(ring_of)}

            def small(*step):
                return small_of[step]

            def ring_bank(step):
                return RING_BANKS[ring_at[step] % len(RING_BANKS)]

            def ring_wait(pe, step):
                i = ring_at[step] - len(RING_BANKS)
                if i >= 0:
                    kind, l, n = ring_of[i]
                    done = {"mm1": mid_ready[l], "unit": (p_ready[0], biased)[l], "max": max_done[l],
                            "q": q32_ready[l], "gate": gate_ready}[kind]
                    pe.wait_ge(done, n + 1)

            def order_of(table):
                for s in order:
                    if s[0] in table:
                        table[s[0]](*s[1:])

            with nc.Block() as block:
                @block.sync
                def _(sp):
                    if has_nxt:
                        sp.dma_start(x_next, d["x"][bass.ds(nxt, 1)].rearrange("b (a p) d -> p (b a) d", p=P))\
                            .then_inc(x_loaded, 16)

                    def weights(l, e):
                        if has_cur:
                            o = l * E + e - WSLOTS
                            sp.wait_ge(mid_used[o // E], FT * (o % E + 1))
                        k = e % WSLOTS
                        loaded = w_loaded[k][l] if l < 2 else w_first_loaded
                        sp.dma_start(w1s[:, k, :], d[f"w1_{l % 2}"][:, e, :]).then_inc(loaded, 16)
                        sp.dma_start(w2s[:, k, :, :], d[f"w2_{l % 2}"][:, e * FT:(e + 1) * FT, :])\
                            .then_inc(loaded, 16)

                    if not has_cur:
                        for e in range(WSLOTS):
                            weights(2, e)
                    else:
                        sp.dma_start(xcur[:], d["x"][bass.ds(cur, 1)].rearrange("b (a p) d -> p (b a) d", p=P))\
                            .then_inc(xcur_loaded, 16)

                    def stack_parts(l):
                        for a in range(PARTS):
                            sp.wait_ge(q_parts[l], a + 1)
                            for j in range(a * PARTS, (a + 1) * PARTS):
                                sp.dma_start(stackQ[HD * j:HD * (j + 1), :, :], qpart[a])\
                                    .then_inc(stack_ready[l], 16)
                        sp.wait_ge(k_parts[l], PARTS)
                        for j in range(PARTS - 1, PAIRS, PARTS):
                            sp.dma_start(stackK[HD * j:HD * (j + 1), :, :], kpart[PARTS - 1])\
                                .then_inc(stack_ready[l], 16)

                    def biases():
                        sp.wait_ge(rows_ready, 1)
                        fwd = biasrow[:, 0:LBW].unsqueeze(1).to_broadcast([H, P, LBW])
                        rev = rev_bf.unsqueeze(1).to_broadcast([H, P, LBW])
                        sp.dma_start(scrF.rearrange("c h t -> h c t"), fwd).then_inc(bias_written, 16)
                        sp.dma_start(scrR.rearrange("c h t -> h c t"), rev).then_inc(bias_written, 16)
                        sp.wait_ge(bias_written, 32)
                        for scr, dst in ((scrF, bias_kT), (scrR, bias_q)):
                            skew = bass.AP(tensor=scr.tensor, offset=P - 1, ap=[[H * LBW - 1, P], [LBW, H], [1, T]])
                            sp.dma_start(dst[:], skew).then_inc(bias_loaded, 16)

                    def maxima_rows(l, g):
                        sp.wait_ge(small_free, small("turn", l, g))
                        for r in range(2):
                            sp.dma_start(stackQ[KR + r:KR + r + 1, 4 * g:4 * g + 4, :],
                                         mparts[:, g % 2, r, :]).then_inc(m_rows[g % 2][l], 16)

                    order_of({"weights": weights, "proj": stack_parts, "biases": biases, "turn": maxima_rows})
                    if has_nxt:
                        sp.wait_ge(w_first_loaded, 32 * WSLOTS)
                    if has_cur:
                        sp.wait_ge(x_ready[1], 1)
                        sp.dma_start(out[bass.ds(cur, 1)].rearrange("b (a p) d -> p (b a) d", p=P), xcur[:])\
                            .then_inc(stored, 16)
                        sp.wait_ge(stored, 16)

                @block.tensor
                def _(pe):
                    def small_bank(*step):
                        if small(*step) > 1:
                            pe.wait_ge(small_free, small(*step) - 1)

                    def turn4(bank, src, signal):
                        for i in range(NT):
                            ins = nc.tensor.transpose(ps[:, bank, tile(i)], src(i), ident[:])
                        ins.then_inc(signal, 1)

                    def tokens_times(lhs, rhs, row, width=D):
                        for i in range(NT):
                            o = ps[:, SMALL_BANK, i * width:(i + 1) * width]
                            ins = nc.tensor.matmul(o, lhs[:, tile(i)], rhs, start=(i == 0),
                                                   stop=(row is None and i == NT - 1), skip_group_check=True)
                            if row is not None:
                                ins = nc.tensor.matmul(o, ones_row[:], row, start=False, stop=(i == NT - 1),
                                                       skip_group_check=True)
                        ins.then_inc(small_ps, 1)

                    def turn_x(l):
                        pe.wait_ge(xn_ready[l], 1)
                        small_bank("turnx", l)
                        xn = (xn0, xn1)[l]
                        turn4(SMALL_BANK, lambda i: xn[:, i, :], small_ps)

                    def turn_hh():
                        pe.wait_ge(hh_ready, 1)
                        turn4(O_BANK, lambda i: a_tok[:, i, :], hT_ps)

                    def projections(l):
                        if l == 0:
                            pe.wait_ge(hT_ready, 1)
                        else:
                            pe.wait_ge(small_free, small("turnx", 1))
                            if has_nxt:
                                pe.wait_ge(osb_ready[0], G)
                        aT = (hT, xnT[1])[l]
                        ring_wait(pe, ("q", l, 0))
                        nc.tensor.matmul(ps[:, ring_bank(("q", l, 0)), :], wq[l][:], aT[:], start=True, stop=True)\
                            .then_inc(q_ps[l], 1)
                        nc.tensor.matmul(ps[:, O_BANK, :], wk[l][:], aT[:], start=True, stop=True)\
                            .then_inc(k_ps[l], 1)
                        small_bank("projv", l)
                        tokens_times(aT, wv[l][:], BV[l])
                        if l == 1:
                            ring_wait(pe, ("gate", 1, 0))
                            nc.tensor.matmul(ps[:, ring_bank(("gate", 1, 0)), :], wmat["wgate1"][:], aT[:], start=True, stop=True)\
                                .then_inc(gate_ps, 1)

                    def max_scores(l, f):
                        if f == 0:
                            pe.wait_ge(stack_ready[l], 16 * (PAIRS + PARTS))
                            pe.wait_ge(stackK_ready[l], ((nxt, cur)[l] + 1) * (16 * (PAIRS - PARTS)))
                        ring_wait(pe, ("max", l, f))
                        for h, i, c in fills[f]:
                            ins = nc.tensor.matmul(ps[:, ring_bank(("max", l, f)), c:c + P * (i + 1)],
                                                   stackQ[0:KR, h, tile(i)], stackK[0:KR, h, 0:P * (i + 1)],
                                                   start=True, stop=True, skip_group_check=True)
                        ins.then_inc(s1_ps[l], 1)

                    def turn_maxima(l, g):
                        pe.wait_ge(max_done[l], FPG * (g + 1))
                        small_bank("turn", l, g)
                        nc.tensor.transpose(ps[0:16, SMALL_BANK, 0:P], maxq[:, 16 * g:16 * g + 16], ident[:])\
                            .then_inc(small_ps, 1)

                    def unit_scores(l, u):
                        g, kt, j0, nh = units[u]
                        W = T - P * kt
                        if u % UPG == 0:
                            pe.wait_ge(m_rows[g % 2][l], 32 * (g // 2 + 1))
                        ring_wait(pe, ("unit", l, u))
                        bank = ring_bank(("unit", l, u))
                        for j in range(nh):
                            h, o = 4 * g + j0 + j, j * W
                            ins = nc.tensor.matmul(ps[:, bank, o:o + W], stackK[0:KR + 2, h, tile(kt)],
                                                   stackQ[0:KR + 2, h, P * kt:T], start=True, stop=(l == 1),
                                                   skip_group_check=True)
                            if l == 0:
                                ins = nc.tensor.matmul(ps[:, bank, o:o + P], ident_bf[:], mask_kT[:],
                                                       start=False, stop=True, skip_group_check=True)
                        ins.then_inc(s2_ps[l], 1)

                    def weigh_values(l, g, kt):
                        pe.wait_ge(p_ready[l], pv_after[(g, kt)])
                        if kt == 0:
                            if g >= 1:
                                pe.wait_ge(osb_ready[l], g)
                            else:
                                pe.wait_ge(small_free, small("projv", l))
                        for j in range(4):
                            ins = nc.tensor.matmul(ps[32 * j:32 * j + VW, O_BANK, P * kt:T],
                                                   vAug[:, kt, 4 * g + j, :], probs[kt][:, j, :],
                                                   start=(kt == 0), stop=(kt == NT - 1), skip_group_check=True)
                        ins.then_inc(pv_done[l], 1)

                    def turn_output(l, g):
                        pe.wait_ge(osb_ready[l], g + 1)
                        small_bank("out", l, g)
                        turn4(SMALL_BANK, lambda i: o_sb[:, g % 2, tile(i)], small_ps)

                    def turn_flat(l):
                        pe.wait_ge(small_free, small("out", l, G - 1))
                        small_bank("flatT", l)
                        turn4(SMALL_BANK, lambda i: flat_tok[:, i, :], small_ps)

                    def attention_out(l):
                        small_bank("attout", l)
                        pe.wait_ge(small_free, small("flatT", l))
                        tokens_times(oT, wo[l][:], BO[l])

                    def turn_h():
                        pe.wait_ge(h2_ready, 1)
                        small_bank("turnh")
                        turn4(SMALL_BANK, lambda i: flat_tok[:, i, :], small_ps)

                    def route(l):
                        pe.wait_ge(small_free, small(*(("turnh",) if l == 0 else ("turnx", 1))))
                        small_bank("route", l)
                        tokens_times(moe_in[l], wr[l][:], BR0 if l == 0 else None, width=E)

                    def turn_weights():
                        pe.wait_ge(w_ready[0], 1)
                        small_bank("wT")
                        for i in range(NT):
                            ins = nc.tensor.transpose(ps[0:E, SMALL_BANK, tile(i)], wts[0][:, i, :], ident[:])
                        ins.then_inc(small_ps, 1)

                    def second_biases():
                        pe.wait_ge(small_free, small("wT"))
                        small_bank("b2")
                        tokens_times(wT, b2r[:], None)

                    def first_product(l, n):
                        if n == 0 and l == 1:
                            pe.wait_ge(small_free, small("turnx", 1))
                        if n % FT == 0 and (l == 1 or n // FT >= WSLOTS):
                            pe.wait_ge(w_loaded[n // FT % WSLOTS][l], 32 * (n // FT // WSLOTS + l))
                        ring_wait(pe, ("mm1", l, n))
                        nc.tensor.matmul(ps[:, ring_bank(("mm1", l, n)), :],
                                         w1s[:, n // FT % WSLOTS, tile(n % FT)], moe_in[l][:],
                                         start=True, stop=True).then_inc(mid_ps[l], 1)

                    def second_product(l, n):
                        e, ft = n // FT, n % FT
                        pe.wait_ge(mid_ready[l], n + 1)
                        if ft == 0 and e >= 1:
                            pe.wait_ge(acc_done[l], e)
                        elif ft == 0 and l == 1:
                            pe.wait_ge(acc_done[0], E)
                        for i in range(NT):
                            ins = nc.tensor.matmul(ps[:, OUT_BANK, tile(i)], mid[:, n % MIDS, tile(i)],
                                                   w2s[:, e % WSLOTS, ft, :], start=(ft == 0 and i == 0),
                                                   stop=(ft == FT - 1 and i == NT - 1), skip_group_check=True)
                        ins.then_inc(mid_used[l], 1)

                    def b_and_c():
                        pe.wait_ge(small_free, small("turnx", 0))
                        nc.tensor.matmul(ps[0:96, BC_BANK, :], wbc[:], xnT[0][:], start=True, stop=True)\
                            .then_inc(bcd_ps, 1)

                    def delta():
                        pe.wait_ge(bc_ready, 1)
                        nc.tensor.matmul(ps[:, BC_BANK, :], wdelta[:], xnT[0][:], start=True, stop=True)\
                            .then_inc(bcd_ps, 1)

                    def state_b(m):
                        if m == 0:
                            pe.wait_ge(dt_ready, 1)
                        else:
                            pe.wait_ge(c_used, m)
                        nc.tensor.matmul(ps[:, BC_BANK, :], bcast_sel[:, m:m + 1].to_broadcast([96, P]),
                                         bcS[:], start=True, stop=True).then_inc(b_ps, 1)

                    def state_c(m):
                        pe.wait_ge(b_used, m + 1)
                        nc.tensor.matmul(ps[:, BC_BANK, :], bcast_sel[:, N + m:N + m + 1].to_broadcast([96, P]),
                                         bcS[:], start=True, stop=True).then_inc(c_ps, 1)

                    def state_out():
                        pe.wait_ge(y_added, N)
                        small_bank("sout")
                        tokens_times(y, wmat["wout0"][:], None)

                    order_of({
                        "turnx": turn_x, "turnhh": turn_hh, "proj": projections, "max": max_scores,
                        "turn": turn_maxima, "unit": unit_scores, "pv": weigh_values, "out": turn_output,
                        "flatT": turn_flat, "attout": attention_out, "turnh": turn_h, "route": route,
                        "wT": turn_weights, "b2": second_biases, "mm1": first_product, "mm2": second_product,
                        "bc": b_and_c, "delta": delta, "stB": state_b, "stC": state_c, "sout": state_out})

                @block.scalar
                def _(act):
                    def small_in(*step):
                        act.wait_ge(small_ps, small(*step))

                    def turn_x(l):
                        small_in("turnx", l)
                        nc.scalar.copy(xnT[l][:], ps[:, SMALL_BANK, :]).then_inc(small_free, 1)

                    def turn_hh():
                        act.wait_ge(hT_ps, 1)
                        nc.scalar.activation(hT[:], ps[:, O_BANK, :], ACT.Identity, bias=B1, scale=G1)\
                            .then_inc(hT_ready, 1)

                    def projections(l):
                        small_in("projv", l)
                        nc.scalar.copy(vAug[:, :, :, 0:HD],
                                       ps[:, SMALL_BANK, :].rearrange("p (a h i) -> p a h i", a=NT, h=H))\
                            .then_inc(small_free, 1)
                        if l == 1:
                            act.wait_ge(gate_ps, 1)
                            nc.scalar.activation(gateT[:], ps[:, ring_bank(("gate", 1, 0)), :], ACT.Sigmoid,
                                                 bias=BG1, scale=1.0)\
                                .then_inc(gate_ready, 1)

                    def exp_unit(l, u):
                        g, kt, j, nh = units[u]
                        W = T - P * kt
                        o = probs[kt][:, j:j + nh, :]
                        if l == 0:
                            act.wait_ge(s2_ps[0], u + 1)
                            if g >= 1:
                                act.wait_ge(pv_done[0], NT * (g - 1) + kt + 1)
                            i = ps[:, ring_bank(("unit", l, u)), 0:nh * W].rearrange("p (j t) -> p j t", j=nh)
                            nc.scalar.activation(o, i, ACT.Exp).then_inc(p_ready[0], 1)
                        else:
                            act.wait_ge(biased, u + 1)
                            nc.scalar.activation(o, o, ACT.Exp).then_inc(p_ready[1], 1)

                    def read_output(l, g):
                        act.wait_ge(pv_done[l], NT * (g + 1))
                        if g >= 2:
                            act.wait_ge(small_ps, small("out", l, g - 2))
                        elif l == 1 and has_nxt:
                            act.wait_ge(small_ps, small("out", 0, g + 2))
                        nc.scalar.copy(o_sb[:, g % 2, :], ps[:, O_BANK, :]).then_inc(osb_ready[l], 1)

                    def turn_flat(l):
                        if l == 0:
                            small_in("flatT", 0)
                            nc.scalar.copy(oT[:], ps[:, SMALL_BANK, :]).then_inc(small_free, 1)

                    def attention_out(l):
                        if l == 1:
                            small_in("attout", 1)
                            nc.scalar.copy(a_tok[:].rearrange("p a d -> p (a d)"), ps[:, SMALL_BANK, :])\
                                .then_inc(small_free, 1)

                    def turn_h():
                        small_in("turnh")
                        nc.scalar.activation(h2T[:], ps[:, SMALL_BANK, :], ACT.Identity, bias=B2, scale=G2)\
                            .then_inc(small_free, 1)

                    def routing_exp(l):
                        act.wait_ge(ex_in[l], 1)
                        nc.scalar.activation(ex[:], ex[:], ACT.Exp).then_inc(ex_ready[l], 1)

                    def turn_weights():
                        small_in("wT")
                        nc.scalar.copy(wT, ps[0:E, SMALL_BANK, :]).then_inc(small_free, 1)

                    def gelu(l, n):
                        act.wait_ge(mid_ps[l], n + 1)
                        if n >= MIDS:
                            act.wait_ge(mid_used[l], n - MIDS + 1)
                        elif l == 1:
                            act.wait_ge(mid_used[0], NF - MIDS + n + 1)
                        nc.scalar.activation(mid[:, n % MIDS, :], ps[:, ring_bank(("mm1", l, n)), :], ACT.Gelu,
                                             bias=b1c[:, n:n + 1] if l == 0 else 0.0, scale=1.0)\
                            .then_inc(mid_ready[l], 1)

                    def silu(l):
                        act.wait_ge(acc_done[l], E)
                        nc.scalar.activation(g_tok[:], acc[:], ACT.Silu).then_inc(silu_ready[l], 1)

                    def update(l):
                        if l == 0:
                            silu(0)

                    def delta():
                        act.wait_ge(bcd_ps, 2)
                        nc.scalar.activation(sp, ps[:, BC_BANK, :], ACT.Abs).then_inc(act_seq, 1)
                        act.wait_ge(act_seq, 1)
                        nc.scalar.activation(sp, sp, ACT.Exp, scale=-1.0).then_inc(act_seq, 1)
                        act.wait_ge(act_seq, 2)
                        nc.scalar.activation(sp, sp, ACT.Ln, bias=1.0).then_inc(sp_ready, 1)

                    def decay(m):
                        if m == 0:
                            act.wait_ge(dt_ready, 1)
                        if m >= 3:
                            act.wait_ge(scanned, m - 2)
                        nc.scalar.activation(dA[:, m % 3, :], dt[:], ACT.Exp, scale=negA[:, m:m + 1])\
                            .then_inc(dA_ready, 1)

                    def state_out():
                        small_in("sout")
                        nc.scalar.copy(s_tok[:].rearrange("p a d -> p (a d)"), ps[:, SMALL_BANK, :])\
                            .then_inc(small_free, 1)

                    order_of({
                        "turnx": turn_x, "turnhh": turn_hh, "proj": projections, "unit": exp_unit,
                        "osb": read_output, "flatT": turn_flat, "attout": attention_out, "turnh": turn_h,
                        "rexp": routing_exp, "wT": turn_weights, "mm1": gelu, "silu": silu, "upd": update,
                        "delta": delta, "dA": decay, "sout": state_out})

                @block.gpsimd
                def _(pool):
                    def rsqrt(n):
                        pool.wait_ge(var_ready[n], 1)
                        nc.gpsimd.tensor_tensor(rstd[:], ve[:], minus_half[:], ALU.pow).then_inc(rstd_ready[n], 1)

                    def norm(l):
                        if l == 0:
                            rsqrt(0)
                            rsqrt(1)
                        else:
                            rsqrt(3)

                    def stack_parts(l):
                        for b in range(PARTS - 1):
                            pool.wait_ge(k_parts[l], b + 1)
                            for j in range(b, PAIRS, PARTS):
                                nc.gpsimd.dma_start(stackK[HD * j:HD * (j + 1), :, :], kpart[b])\
                                    .then_inc(stackK_ready[l], 16)

                    def attention_out(l):
                        if l == 0:
                            rsqrt(2)

                    def y_start():
                        pool.wait_ge(small_free, small("turnx", 0))
                        nc.gpsimd.tensor_scalar(y[:], xnT[0][:], D_COL, None, ALU.mult).then_inc(y_ready, 1)

                    def state_add(m):
                        pool.wait_ge(c_used, m + 1)
                        if m == 0:
                            pool.wait_ge(y_ready, 1)
                        else:
                            pool.wait_ge(y_added, m)
                        nc.gpsimd.tensor_tensor(y[:], y[:], h_buf[:, m % 3, :], ALU.add).then_inc(y_added, 1)

                    order_of({"norm": norm, "proj": stack_parts, "attout": attention_out, "bc": y_start,
                                      "stC": state_add})

                @block.vector
                def _(dve):
                    seq = [0]

                    def step(ins):
                        seq[0] += 1
                        ins.then_inc(dve_seq, 1)
                        dve.wait_ge(dve_seq, seq[0])

                    def moments(src, n):
                        for i in range(NT):
                            ins = nc.vector.bn_stats(stats[:, i, :], src[:, i, :])
                        step(ins)
                        for i in range(NT):
                            ins = nc.vector.bn_aggr(mv[:, i, :], stats[:, i, :])
                        step(ins)
                        nc.vector.tensor_scalar(ve[:], mv[:, :, 1], EPS, None, ALU.add).then_inc(var_ready[n], 1)

                    def normalize(dst, src, n, signal):
                        dve.wait_ge(rstd_ready[n], 1)
                        for i in range(NT):
                            ins = nc.vector.tensor_scalar(dst[:, i, :], src[:, i, :], mv[:, i, 0:1],
                                                          rstd[:, i:i + 1], ALU.subtract, ALU.mult)
                        ins.then_inc(signal, 1)
                        dve.wait_ge(signal, 1)

                    def norm(l):
                        if l == 1:
                            dve.wait_ge(x_ready[0], 1)
                            moments(xcur, 3)
                            normalize(xn1, xcur, 3, xn_ready[1])
                            return
                        dve.wait_ge(x_loaded, 16)
                        moments(x_next, 0)
                        normalize(xn0, x_next, 0, xn_ready[0])
                        step(nc.vector.tensor_tensor(ve[:], mv[:, :, 1], rstd[:], ALU.mult))
                        step(nc.vector.tensor_tensor(ve[:], ve[:], rstd[:], ALU.mult))
                        nc.vector.tensor_scalar(ve[:], ve[:], EPS, None, ALU.add).then_inc(var_ready[1], 1)
                        dve.wait_ge(rstd_ready[1], 1)
                        for i in range(NT):
                            ins = nc.vector.tensor_scalar(a_tok[:, i, :], xn0[:, i, :], rstd[:, i:i + 1], None,
                                                          ALU.mult)
                        ins.then_inc(hh_ready, 1)
                        dve.wait_ge(hh_ready, 1)

                    def split(l):
                        dve.wait_ge(q_ps[l], 1)
                        nc.vector.tensor_scalar(q32, ps[:, ring_bank(("q", l, 0)), :], BQ[l], SCALE,
                                                ALU.add, ALU.mult).then_inc(q32_ready[l], 1)
                        dve.wait_ge(k_ps[l], 1)
                        nc.vector.tensor_scalar(k32, ps[:, O_BANK, :], BK[l], None, ALU.add)\
                            .then_inc(k32_ready[l], 1)
                        dve.wait_ge(q32_ready[l], 1)
                        nc.vector.tensor_copy(qpart[0], q32).then_inc(q_parts[l], 1)
                        dve.wait_ge(k32_ready[l], 1)
                        nc.vector.tensor_copy(kpart[0], k32).then_inc(k_parts[l], 1)
                        dve.wait_ge(q_parts[l], 1)
                        nc.vector.tensor_tensor(qres, q32, qpart[0], ALU.subtract).then_inc(q_rest[l], 1)
                        dve.wait_ge(k_parts[l], 1)
                        nc.vector.tensor_tensor(kres, k32, kpart[0], ALU.subtract).then_inc(k_rest[l], 1)
                        dve.wait_ge(q_rest[l], 1)
                        nc.vector.tensor_copy(qpart[1], qres).then_inc(q_parts[l], 1)
                        dve.wait_ge(k_rest[l], 1)
                        nc.vector.tensor_copy(kpart[1], kres).then_inc(k_parts[l], 1)
                        dve.wait_ge(q_parts[l], 2)
                        nc.vector.tensor_tensor(qpart[2], qres, qpart[1], ALU.subtract).then_inc(q_parts[l], 1)
                        dve.wait_ge(k_parts[l], 2)
                        nc.vector.tensor_tensor(kpart[2], kres, kpart[1], ALU.subtract).then_inc(k_parts[l], 1)

                    def row_max(l, f):
                        if l == 1 and f == 0:
                            dve.wait_ge(bias_loaded, 32)
                        dve.wait_ge(s1_ps[l], f + 1)
                        for h, i, c in fills[f]:
                            o = ps[:, ring_bank(("max", l, f)), c:c + P * (i + 1)]
                            extra = mask_q[:, window(i)] if l == 0 else bias_q[:, h, window(i)]
                            m = NT * h + i
                            ins = nc.vector.tensor_tensor_reduce(out=o, in0=o, in1=extra, scale=1.0,
                                                                 scalar=LOWEST, op0=ALU.add, op1=ALU.max,
                                                                 accum_out=maxq[:, m:m + 1])
                        ins.then_inc(max_done[l], 1)

                    def max_parts(l, g):
                        t = ps[0:16, SMALL_BANK, 0:P]
                        dve.wait_ge(small_ps, small("turn", l, g))
                        if g >= 2:
                            dve.wait_ge(m_rows[g % 2][l], 32 * (g // 2))
                        elif l == 1 and has_nxt:
                            dve.wait_ge(m_rows[g % 2][0], 64)
                        step(nc.vector.tensor_scalar(mparts[:, g % 2, 0, :], t, -1.0, None, ALU.mult))
                        nc.vector.scalar_tensor_tensor(out=mparts[:, g % 2, 1, :], in0=t, scalar=-1.0,
                                                       in1=mparts[:, g % 2, 0, :], op0=ALU.mult,
                                                       op1=ALU.subtract).then_inc(small_free, 1)

                    def add_bias(l, u):
                        if l == 0:
                            return
                        g, kt, j, nh = units[u]
                        W = T - P * kt
                        h = 4 * g + j
                        dve.wait_ge(s2_ps[1], u + 1)
                        if g >= 1:
                            dve.wait_ge(pv_done[1], NT * (g - 1) + kt + 1)
                        i = ps[:, ring_bank(("unit", l, u)), 0:nh * W].rearrange("p (j t) -> p j t", j=nh)
                        nc.vector.tensor_tensor(probs[kt][:, j:j + nh, :], i, bias_kT[:, h:h + nh, 0:W],
                                                ALU.add).then_inc(biased, 1)

                    def divide_output(l, g):
                        o = ps[:, SMALL_BANK, :].rearrange("p (a j c) -> p a j c", a=NT, j=4)
                        dve.wait_ge(small_ps, small("out", l, g))
                        step(nc.vector.reciprocal(recip[:], o[:, :, :, HD]))
                        nc.vector.tensor_tensor(flat[:, :, 4 * g:4 * g + 4, :], o[:, :, :, 0:HD],
                                                recip[:].unsqueeze(3).to_broadcast([P, NT, 4, HD]), ALU.mult)\
                            .then_inc(small_free, 1)
                        dve.wait_ge(small_free, small("out", l, g))

                    def turn_flat(l):
                        if l == 1:
                            dve.wait_ge(small_ps, small("flatT", 1))
                            dve.wait_ge(gate_ready, 1)
                            nc.vector.tensor_tensor(oT[:], ps[:, SMALL_BANK, :], gateT[:], ALU.mult)\
                                .then_inc(small_free, 1)

                    def attention_out(l):
                        if l == 0:
                            dve.wait_ge(small_ps, small("attout", 0))
                            nc.vector.tensor_tensor(a_tok[:].rearrange("p a d -> p (a d)"), ps[:, SMALL_BANK, :],
                                                    xn0[:].rearrange("p a d -> p (a d)"), ALU.add)\
                                .then_inc(small_free, 1)
                            dve.wait_ge(small_free, small("attout", 0))
                            moments(a_tok, 2)
                            normalize(flat_tok, a_tok, 2, h2_ready)

                    def second_biases():
                        dve.wait_ge(small_ps, small("b2"))
                        nc.vector.tensor_tensor(acc_next[:].rearrange("p a d -> p (a d)"), ps[:, SMALL_BANK, :],
                                                a_tok[:].rearrange("p a d -> p (a d)"), ALU.add)\
                            .then_inc(small_free, 1)

                    def b_and_c():
                        z = ps[0:96, BC_BANK, :]
                        dve.wait_ge(bcd_ps, 1)
                        step(nc.vector.tensor_copy(bcS[:], z))
                        step(nc.vector.tensor_tensor(bcR, z, bcS[:], ALU.subtract))
                        nc.vector.tensor_copy(bcS[32:64, :], bcR[32:64, :])
                        step(nc.vector.tensor_copy(bcS[64:96, :], bcR[64:96, :]))
                        step(nc.vector.tensor_tensor(bcR[64:96, :], bcR[64:96, :], bcS[64:96, :], ALU.subtract))
                        nc.vector.tensor_copy(bcS[64:96, :], bcR[64:96, :]).then_inc(bc_ready, 1)

                    def delta():
                        dve.wait_ge(sp_ready, 1)
                        nc.vector.scalar_tensor_tensor(out=dt[:], in0=ps[:, BC_BANK, :], scalar=0.0, in1=sp,
                                                       op0=ALU.max, op1=ALU.add).then_inc(dt_ready, 1)
                        dve.wait_ge(dt_ready, 1)
                        dve.wait_ge(y_ready, 1)
                        nc.vector.tensor_tensor(dtx[:], dt[:], xnT[0][:], ALU.mult).then_inc(dtx_ready, 1)

                    def state_b(m):
                        dve.wait_ge(b_ps, m + 1)
                        if m == 0:
                            dve.wait_ge(dtx_ready, 1)
                            dve.wait_ge(bc_ready, 1)
                        if m >= 2:
                            dve.wait_ge(scanned, m - 1)
                        nc.vector.tensor_tensor(u_buf[:, m % 2, :], dtx[:], ps[:, BC_BANK, :], ALU.mult)\
                            .then_inc(b_used, 1)

                    def state_c(m):
                        dve.wait_ge(b_used, m + 1)
                        dve.wait_ge(dA_ready, m + 1)
                        if m >= 3:
                            dve.wait_ge(y_added, m - 2)
                        nc.vector.tensor_tensor_scan(h_buf[:, m % 3, :], dA[:, m % 3, :], u_buf[:, m % 2, :],
                                                     0.0, ALU.mult, ALU.add).then_inc(scanned, 1)
                        dve.wait_ge(scanned, m + 1)
                        dve.wait_ge(c_ps, m + 1)
                        nc.vector.tensor_tensor(h_buf[:, m % 3, :], h_buf[:, m % 3, :], ps[:, BC_BANK, :],
                                                ALU.mult).then_inc(c_used, 1)

                    def wide(ap):
                        return ap.to_broadcast([P, NT, E])

                    def route(l):
                        dve.wait_ge(small_ps, small("route", l))
                        nc.vector.tensor_copy(logits[:].rearrange("p a e -> p (a e)"),
                                              ps[:, SMALL_BANK, 0:NT * E]).then_inc(small_free, 1)
                        dve.wait_ge(small_free, small("route", l))
                        for i in range(NT):
                            ins = nc.vector.max(top8[:, i, :], logits[:, i, :])
                        step(ins)
                        nc.vector.tensor_tensor(ex[:], logits[:], wide(top8[:, :, 0:1]), ALU.subtract)\
                            .then_inc(ex_in[l], 1)
                        if l == 0:
                            step(nc.vector.tensor_tensor(gt[:], logits[:], wide(top8[:, :, 1:2]), ALU.is_ge))
                        else:
                            step(nc.vector.tensor_tensor(gt[:], logits[:], wide(top8[:, :, 1:2]), ALU.is_gt))
                            step(nc.vector.tensor_tensor(eq[:], logits[:], wide(top8[:, :, 1:2]), ALU.is_equal))
                            nc.vector.tensor_reduce(cnt[:], gt[:], AX.X, ALU.add)
                            step(nc.vector.tensor_tensor_scan(rank[:].rearrange("p a e -> p (a e)"),
                                                              keep[:].rearrange("p a e -> p (a e)"),
                                                              eq[:].rearrange("p a e -> p (a e)"),
                                                              0.0, ALU.mult, ALU.add))
                            step(nc.vector.tensor_tensor(rank[:], rank[:], wide(cnt[:].unsqueeze(2)), ALU.add))
                            step(nc.vector.tensor_scalar(rank[:], rank[:], 2.5, None, ALU.is_le))
                            step(nc.vector.tensor_tensor(eq[:], eq[:], rank[:], ALU.mult))
                            step(nc.vector.tensor_tensor(gt[:], gt[:], eq[:], ALU.add))

                    def weights(l):
                        dve.wait_ge(ex_ready[l], 1)
                        if l == 0 and has_cur:
                            dve.wait_ge(acc_done[0], E)
                        step(nc.vector.tensor_tensor(gt[:], ex[:], gt[:], ALU.mult))
                        step(nc.vector.tensor_reduce(tsum[:], gt[:], AX.X, ALU.add))
                        step(nc.vector.reciprocal(cnt[:], tsum[:]))
                        nc.vector.tensor_tensor(wts[l][:], gt[:], wide(cnt[:].unsqueeze(2)), ALU.mult)\
                            .then_inc(w_ready[l], 1)
                        dve.wait_ge(w_ready[l], 1)

                    def add_expert(l, e):
                        dve.wait_ge(mid_used[l], FT * (e + 1))
                        if e >= 1:
                            dve.wait_ge(acc_done[l], e)
                        for i in range(NT):
                            o, w = ps[:, OUT_BANK, tile(i)], wts[l][:, i, e:e + 1]
                            if l == 1 and e == 0:
                                ins = nc.vector.tensor_scalar(acc[:, i, :], o, w, None, ALU.mult)
                            else:
                                before = (acc_next if e == 0 else acc)[:, i, :]
                                ins = nc.vector.scalar_tensor_tensor(out=acc[:, i, :], in0=o, scalar=w,
                                                                     in1=before, op0=ALU.mult, op1=ALU.add)
                        ins.then_inc(acc_done[l], 1)

                    def update(l):
                        dve.wait_ge(silu_ready[l], 1)
                        if l == 0:
                            dve.wait_ge(xcur_loaded, 16)
                        else:
                            dve.wait_ge(small_free, small("attout", 1))
                        s = (s_tok, a_tok)[l]
                        nc.vector.tensor_tensor(g_tok[:], s[:], g_tok[:], ALU.mult).then_inc(prod_ready[l], 1)
                        dve.wait_ge(prod_ready[l], 1)
                        nc.vector.tensor_tensor(xcur[:], xcur[:], g_tok[:], ALU.add).then_inc(x_ready[l], 1)

                    order_of({
                        "norm": norm, "proj": split, "max": row_max, "turn": max_parts, "unit": add_bias,
                        "out": divide_output, "flatT": turn_flat, "attout": attention_out,
                        "b2": second_biases, "bc": b_and_c, "delta": delta, "stB": state_b, "stC": state_c,
                        "route": route, "wts": weights, "add": add_expert, "upd": update})

            nums = [s.num for s in loop_sems]
            assert nums == list(range(nums[0], nums[0] + len(nums)))
            nc.multi_engine_barrier(list(nc.engines), sems_to_clear=range(nums[0], nums[-1] + 1))

        segment(None, 0)
        with nc.Fori(0, B - 1) as b:
            segment(b, b + 1)
        segment(B - 1, None)


def kernel(**inputs):
    import numpy as np
    import concourse.bacc as bacc
    from concourse.bass_utils import run_bass_kernel_spmd

    v = {k: np.asarray(a) for k, a in inputs.items()}
    x = v["L0_attn_x"]
    D = x.shape[2]
    N = v["L0_attn_A_log"].shape[0]
    H, HD, FT = 16, D // 16, v["L0_ffn_e_w1"].shape[2] // 128
    by_dim = np.arange(D).reshape(H, HD).T.ravel()
    Wx = v["L0_attn_Wx"]
    Wqkv, bqkv = v["L1_attn_Wqkv"], v["L1_attn_bqkv"]
    E, F = v["L0_ffn_e_b1"].shape
    data = {
        "x": x,
        "A_log": v["L0_attn_A_log"].reshape(1, N),
        "pos_bias": v["L1_attn_pos_bias"],
        "pos_biasT": v["L1_attn_pos_bias"].T,
        "offsets": v["L1_attn_offsets"],
        "cols": np.stack([v["L0_attn_D"], v["L0_ffn_ln1_g"], v["L0_ffn_ln1_b"], v["L0_ffn_ln2_g"],
                          v["L0_ffn_ln2_b"], v["L0_ffn_bq"][by_dim], v["L0_ffn_bk"][by_dim],
                          bqkv[:D][by_dim], bqkv[D:2 * D][by_dim], v["L1_attn_bgate"]], axis=1),
        "rows": np.concatenate([v["L0_ffn_bv"], v["L0_ffn_bo"], bqkv[2 * D:], v["L1_attn_bout"],
                                v["L0_ffn_br"]])[None, :],
        "b1": v["L0_ffn_e_b1"].reshape(E * FT, 128).T,
        "b2": v["L0_ffn_e_b2"],
        "wbc": np.concatenate([Wx[:2 * N].T] * 3, axis=1),
        "wdelta": Wx[2 * N:].T,
        "wout0": v["L0_attn_Wout"].T,
        "wq0": v["L0_ffn_Wq"][:, by_dim], "wk0": v["L0_ffn_Wk"][:, by_dim],
        "wv0": v["L0_ffn_Wv"], "wo0": v["L0_ffn_Wo"], "wr0": v["L0_ffn_Wr"],
        "wq1": Wqkv[:D][by_dim].T, "wk1": Wqkv[D:2 * D][by_dim].T, "wv1": Wqkv[2 * D:].T,
        "wgate1": v["L1_attn_Wgate"].T, "wo1": v["L1_attn_Wout"].T, "wr1": v["L1_ffn_router_w"].T,
        "w1_0": v["L0_ffn_e_w1"].transpose(1, 0, 2),
        "w2_0": v["L0_ffn_e_w2"].reshape(E * FT, 128, D).transpose(1, 0, 2),
        "w1_1": v["L1_ffn_expert_w1"].transpose(2, 0, 1),
        "w2_1": v["L1_ffn_expert_w2"].transpose(2, 0, 1).reshape(FT, 128, E, D).transpose(1, 2, 0, 3)
                .reshape(128, E * FT, D),
    }
    nc = bacc.Bacc("TRN2", target_bir_lowering=False, num_devices=1)
    arrays, aps = {}, {}
    for name, a in data.items():
        a = np.ascontiguousarray(a)
        arrays["in_" + name] = a
        aps[name] = nc.dram_tensor("in_" + name, a.shape, mybir.dt.from_np(a.dtype), kind="ExternalInput").ap()
    out = nc.dram_tensor("out_0", x.shape, mybir.dt.float32, kind="ExternalOutput").ap()
    build(nc, aps, out)
    r = run_bass_kernel_spmd(nc, [arrays], core_ids=[0])
    return r.results[0]["out_0"]
```

```python
from contextlib import ExitStack

import concourse.bass as bass
from concourse import mybir

F32 = mybir.dt.float32
BF16 = mybir.dt.bfloat16
I32 = mybir.dt.int32
ACT = mybir.ActivationFunctionType
ALU = mybir.AluOpType
AX = mybir.AxisListType

P = 128
NEG = -1.0e30
LOWEST = -3.0e38
EPS = 1e-5
PARTS = 3
VW = 32
WSLOTS = 4
MIDS = 8

RING_BANKS = (0, 1, 2, 3)
O_BANK = 4
SMALL_BANK = 5
OUT_BANK = 6
BC_BANK = 7


NEXT_STEPS = (("norm", 0), ("turnx", 0), ("turnhh",), ("proj", 0), ("bc",), ("delta",), ("flatT", 0),
              ("attout", 0), ("turnh",), ("route", 0), ("rexp", 0), ("wts", 0), ("wT",), ("b2",), ("sout",))
CURRENT_STEPS = (("upd", 0), ("norm", 1), ("turnx", 1), ("route", 1), ("rexp", 1), ("wts", 1), ("proj", 1),
              ("silu", 1), ("flatT", 1), ("attout", 1), ("upd", 1))
PLACES = {
    "first": {
        "steps": [0.2, 0.2, 0.2, 0.2, 0.2, 0.2, 135.9, 149.8, 151.8, 156.0, 162.6, 178.3, 170.8, 223.6,
            313.8],
        "maxima": [(0.2, 0.2), (0.4, 27.3), (48.0, 55.9), (58.9, 74.7)],
        "units": [(2.1, 29.8), (50.9, 61.6), (59.9, 77.2), (120.8, 132.0)],
        "out": [57.5, 94.8, 125.0, 134.2],
        "dA": [0.2, 19.6, 48.2, 50.1, 70.9, 97.0, 114.4, 135.0, 151.2, 191.6, 210.4, 215.3, 235.7, 255.8,
            287.0, 290.9],
        "stB": [0.2, 0.2, 48.4, 53.1, 66.4, 84.1, 124.4, 130.1, 150.6, 185.8, 210.2, 227.5, 243.0, 275.7,
            283.4, 301.1],
        "stC": [0.2, 25.7, 52.2, 59.3, 75.3, 90.7, 126.9, 135.3, 152.6, 199.8, 211.6, 232.2, 253.7, 282.4,
            293.1, 303.7],
    },
    "next": {
        "steps": [8.5, 8.2, 12.5, 12.7, 17.0, 43.7, 150.1, 155.0, 170.1, 171.4, 180.8, 190.7, 192.2, 211.5,
            298.1],
        "maxima": [(26.3, 35.2), (59.6, 82.2), (84.8, 90.2), (96.7, 102.9)],
        "units": [(55.4, 75.8), (86.9, 97.4), (97.4, 104.3), (111.0, 122.9)],
        "out": [78.1, 99.3, 111.3, 142.9],
        "dA": [61.9, 62.7, 77.6, 81.1, 97.3, 103.9, 108.8, 116.1, 164.2, 187.8, 201.6, 216.8, 221.4, 222.6,
            224.8, 288.6],
        "stB": [60.1, 70.1, 77.8, 88.8, 95.4, 103.7, 115.3, 120.9, 181.7, 200.1, 204.2, 217.0, 219.2, 231.2,
            238.1, 249.4],
        "stC": [62.6, 75.9, 80.6, 90.8, 103.3, 107.7, 119.5, 121.2, 183.4, 202.3, 210.7, 217.8, 228.8,
            234.8, 239.3, 250.7],
    },
    "current": {
        "steps": [91.4, 93.2, 101.2, 113.3, 122.1, 139.7, 156.2, 221.8, 249.6, 274.9, 286.0],
        "maxima": [(173.7, 190.0), (190.6, 208.5), (207.7, 216.5), (216.7, 227.5)],
        "units": [(195.3, 204.7), (213.8, 220.4), (223.3, 235.1), (232.4, 240.9)],
        "out": [205.7, 226.2, 239.7, 244.1],
        "first": [(1.4, 2.0), (13.4, 25.1), (29.0, 36.9), (73.2, 80.9), (137.8, 164.5), (162.8, 174.9),
            (183.9, 192.3), (205.0, 213.2)],
        "second": [(2.1, 23.9), (24.9, 35.6), (44.6, 76.6), (84.7, 91.6), (165.5, 173.2), (177.1, 193.0),
            (195.6, 205.1), (213.6, 220.7)],
    },
    "last": {
        "steps": [98.8, 99.4, 100.5, 112.3, 116.5, 112.6, 122.4, 193.4, 260.0, 280.4, 283.1],
        "maxima": [(146.2, 157.7), (156.2, 163.8), (169.3, 191.5), (187.2, 234.9)],
        "units": [(159.4, 164.3), (183.7, 194.8), (229.6, 239.4), (237.1, 249.6)],
        "out": [168.9, 228.6, 248.0, 257.6],
        "first": [(0.0, 0.0), (0.0, 25.3), (29.3, 43.3), (43.4, 75.4), (114.0, 136.1), (136.1, 145.8),
            (148.9, 160.1), (164.0, 177.9)],
        "second": [(1.5, 7.7), (26.9, 37.4), (37.8, 55.2), (57.5, 88.5), (130.9, 145.1), (148.4, 151.4),
            (158.3, 164.7), (181.9, 194.3)],
    },
}


def build(nc, d, out):
    B, T, D = d["x"].shape
    NT = T // P
    N = d["A_log"].shape[1]
    NO, H = d["pos_bias"].shape
    HD = D // H
    E = d["b2"].shape[0]
    F = d["w1_0"].shape[2]
    FT = F // P
    NF = E * FT
    SCALE = float(HD) ** -0.5
    PAIRS = PARTS * PARTS
    KR = PAIRS * HD
    G = H // 4
    LBW = T + P
    assert D == P and HD == 8 and NT == 4 and G * NT == 16

    with ExitStack() as ctx:
        def sb(name, shape, dt=F32):
            return ctx.enter_context(nc.sbuf_tensor(name, shape, dt))

        def sem(name):
            return ctx.enter_context(nc.semaphore(name))

        ident = sb("ident", [P, P])
        bcast_sel = sb("bcast_sel", [3 * 32, 32], BF16)
        ones_row = sb("ones_row", [1, P])
        ones_bf = sb("ones_bf", [H, T], BF16)
        minus_half = sb("minus_half", [P, NT])
        mask_q = sb("mask_q", [P, T], BF16)
        cols = sb("cols", [P, d["cols"].shape[1]])
        rowb = sb("rowb", [P, 4, D])
        br0 = sb("br0", [1, E])
        b1c = sb("b1c", [P, NF])
        b2r = sb("b2r", [E, D])
        negA = sb("negA", [P, N])
        wbc = sb("wbc", [P, 3 * 32])
        wdelta = sb("wdelta", [P, D])
        wmat = {k: sb("w_" + k, [P, d[k].shape[1]]) for k in
                ("wq0", "wk0", "wv0", "wo0", "wr0", "wout0", "wq1", "wk1", "wv1", "wgate1", "wo1", "wr1")}
        bias_q = sb("bias_q", [P, H, T], BF16)
        bias_kT = sb("bias_kT", [P, H, T])
        bias_loaded = sem("bias_loaded")
        D_COL, G1, B1, G2, B2, BQ0, BK0, BQ1, BK1, BG1 = (cols[:, i:i + 1] for i in range(10))

        xn0 = sb("xn0", [P, NT, D])
        xcur = sb("xcur", [P, NT, D])
        g_tok = sb("g_tok", [P, NT, D])
        a_tok = sb("a_tok", [P, NT, D])
        s_tok = sb("s_tok", [P, NT, D])
        acc = sb("acc", [P, NT, D])
        acc_next = sb("acc_next", [P, NT, D])
        xnT = (sb("xnT0", [P, T]), sb("xnT1", [P, T]))
        h2T = sb("h2T", [P, T])
        oT = sb("oT", [P, T])
        gateT = sb("gateT", [P, T])
        flat = sb("flat", [P, NT, H, HD])
        stats = sb("stats", [P, NT, 6])
        mv = sb("mv", [P, NT, 2])
        ve = sb("ve", [P, NT])
        rstd = sb("rstd", [P, NT])
        stackQ = sb("stackQ", [P, H, T], BF16)
        stackK = sb("stackK", [P, H, T], BF16)
        vAug = sb("vAug", [P, NT, H, VW])
        maxq = sb("maxq", [P, G * 16])
        mparts = sb("mparts", [16, 2, 2, P], BF16)
        probs_all = sb("probs_all", [P, 4 * (4 + 3 + 2 + 1) * P])
        o_sb = sb("o_sb", [P, 2, T])
        recip = sb("recip", [P, NT, 4])
        w1s = sb("w1s", [P, WSLOTS, F])
        w2s = sb("w2s", [P, WSLOTS, FT, D])
        mid = sb("mid", [P, MIDS, T])
        logits = sb("logits", [P, NT, E])
        top8 = sb("top8", [P, NT, 8])
        ex = sb("ex", [P, NT, E])
        gt = sb("gt", [P, NT, E])
        eq = sb("eq", [P, NT, E])
        rank = sb("rank", [P, NT, E])
        keep = sb("keep", [P, NT, E])
        wts = (sb("wts0", [P, NT, E]), sb("wts1", [P, NT, E]))
        tsum = sb("tsum", [P, NT])
        cnt = sb("cnt", [P, NT])
        bcS = sb("bcS", [3 * 32, T], BF16)
        dA = sb("dA", [P, 3, T])
        u_buf = sb("u_buf", [P, 2, T])
        h_buf = sb("h_buf", [P, 3, T])
        dt = sb("dt", [P, T])
        y = sb("y", [P, T])

        flat_tok = flat[:].rearrange("p a h i -> p a (h i)")
        x_next = flat_tok
        xn1 = g_tok
        hT = oT
        wT = oT[0:E, :]
        dtx = xnT[0]
        sp, bcR = u_buf[:, 0, :], u_buf[0:96, 1, :]
        at, probs = 0, []
        for kt in range(NT):
            W = T - P * kt
            probs.append(probs_all[:, at:at + 4 * W].rearrange("p (j t) -> p j t", j=4))
            at += 4 * W
        q32, qres, k32, kres = (probs_all[:, i * T:(i + 1) * T] for i in range(4))
        half = probs_all[:, 4 * T:7 * T].bitcast(BF16)
        qpart = [half[:, i * T:(i + 1) * T] for i in range(PARTS)]
        kpart = [half[:, (PARTS + i) * T:(PARTS + i + 1) * T] for i in range(PARTS)]

        ps = ctx.enter_context(nc.psum_tensor("ps", [P, 8, T], F32))
        scrF = nc.dram_tensor("scrF", [P, H, LBW], F32).ap()
        scrR = nc.dram_tensor("scrR", [P, H, LBW], BF16).ap()

        ld, ld_first = sem("ld"), sem("ld_first")
        pool_step, dve_step, act_step, pe_step = (sem(n) for n in ("pool_step", "dve_step", "act_step", "pe_step"))
        rows_ready, bias_written = sem("rows_ready"), sem("bias_written")

        fQ, fK = (bias_kT[:, i * H // 2:(i + 1) * H // 2, :].rearrange("p h t -> p (h t)") for i in range(2))
        off_ci, off_ri = fQ[0:NO, 0:1].bitcast(I32), fQ[0:NO, 8:8 + NO].bitcast(I32)
        off_c, off_r = fQ[0:NO, 96:97], fQ[0:NO, 104:104 + NO]
        same, apart, before = (fQ[0:NO, a:a + NO] for a in (200, 300, 400))
        dup, first = fQ[0:NO, 500:501], fQ[0:NO, 501:502]
        iota_i = fQ[0:NO, 512:512 + 2 * T].bitcast(I32)
        iota_f = fQ[0:NO, 1536:1536 + 2 * T]
        onehot = fQ[0:NO, 2560:2560 + 2 * T]
        pbmax, pbsum, joint, ones_oh = (fQ[0:NO, a:a + H] for a in (3600, 3620, 3640, 3660))
        pb = fK[0:NO, 0:H * NO].rearrange("p (h o) -> p h o", h=H)
        biasrow = fK[0:H, 1100:1100 + 2 * LBW]
        pen = fK[0:H, 2400:2400 + 2 * T]
        rev_bf = fK[0:H, 3440:3440 + LBW // 2].bitcast(BF16)
        N_LD = 7 + len(wmat)

        with nc.Block() as block:
            @block.sync
            def _(sp):
                sp.dma_start(off_ci, d["offsets"].rearrange("(o a) -> o a", a=1)).then_inc(ld_first, 16)
                sp.dma_start(off_ri, d["offsets"].partition_broadcast(NO)).then_inc(ld_first, 16)
                sp.dma_start(pb, d["pos_biasT"].partition_broadcast(NO)).then_inc(ld_first, 16)
                sp.dma_start(negA[:], d["A_log"][0, :].partition_broadcast(P)).then_inc(ld_first, 16)
                sp.dma_start(cols[:], d["cols"]).then_inc(ld, 16)
                sp.dma_start(rowb[:].rearrange("p r d -> p (r d)"), d["rows"][0, 0:4 * D].partition_broadcast(P))\
                    .then_inc(ld, 16)
                sp.dma_start(br0[:], d["rows"][:, 4 * D:4 * D + E]).then_inc(ld, 16)
                sp.dma_start(b1c[:], d["b1"]).then_inc(ld, 16)
                sp.dma_start(b2r[:], d["b2"]).then_inc(ld, 16)
                sp.dma_start(wbc[:], d["wbc"]).then_inc(ld, 16)
                sp.dma_start(wdelta[:], d["wdelta"]).then_inc(ld, 16)
                for k, w in wmat.items():
                    sp.dma_start(w[:], d[k]).then_inc(ld, 16)
                sp.wait_ge(pool_step, 1)
                for row in (KR, KR + 1):
                    sp.dma_start(stackK[row:row + 1, :, :], ones_bf[:]).then_inc(ld, 16)
                sp.wait_ge(ld, 16 * (N_LD + 2))

            @block.gpsimd
            def _(pool):
                nc.gpsimd.memset(ident[:], 0.0)
                nc.gpsimd.memset(mask_q[:], 0.0)
                nc.gpsimd.memset(ones_bf[:], 1.0)
                nc.gpsimd.memset(ones_row[:], 1.0)
                nc.gpsimd.memset(minus_half[:], -0.5)
                nc.gpsimd.memset(keep[:], 1.0)
                nc.gpsimd.memset(vAug[:], 0.0).then_inc(pool_step, 1)
                nc.gpsimd.iota(iota_i[:, 0:T], pattern=[[1, T]], base=0, channel_multiplier=0)
                nc.gpsimd.iota(iota_i[:, T:2 * T], pattern=[[-1, T]], base=T - 1,
                               channel_multiplier=0).then_inc(pool_step, 1)
                pool.wait_ge(pool_step, 1)
                nc.gpsimd.memset(keep[:, :, 0:1], 0.0)
                nc.gpsimd.memset(vAug[:, :, :, HD:HD + 1], 1.0)
                nc.gpsimd.affine_select(out=ident[:], in_=ident[:], compare_op=ALU.not_equal, fill=1.0,
                                        base=0, pattern=[[-1, P]], channel_multiplier=1)
                nc.gpsimd.affine_select(out=mask_q[:, T - P:T], in_=mask_q[:, T - P:T], compare_op=ALU.is_ge,
                                        fill=NEG, base=0, pattern=[[-1, P]],
                                        channel_multiplier=1).then_inc(pool_step, 1)
                pool.wait_ge(pool_step, 3)
                for r in range(3):
                    pool.wait_ge(pool_step, 3 + r)
                    nc.gpsimd.tensor_copy(bcast_sel[32 * r:32 * r + 32, :],
                                          ident[32 * r:32 * r + 32, 32 * r:32 * r + 32]).then_inc(pool_step, 1)
                pool.wait_ge(pool_step, 6)
                pool.wait_ge(dve_step, 3)
                nc.gpsimd.affine_select(out=before, in_=same, compare_op=ALU.is_gt, fill=0.0,
                                        base=0, pattern=[[-1, NO]],
                                        channel_multiplier=1).then_inc(pool_step, 1)

            @block.scalar
            def _(act):
                act.wait_ge(ld_first, 64)
                nc.scalar.activation(negA[:], negA[:], ACT.Exp).then_inc(act_step, 1)
                act.wait_ge(dve_step, 7)
                nc.scalar.activation(pb, pb, ACT.Exp).then_inc(act_step, 1)
                act.wait_ge(dve_step, 8)
                nc.scalar.activation(pbsum, pbsum, ACT.Ln).then_inc(act_step, 1)

            @block.tensor
            def _(pe):
                pe.wait_ge(dve_step, 14)
                for r in range(2):
                    oh = onehot[:, r * T:(r + 1) * T]
                    nc.tensor.matmul(ps[0:H, r, :], joint, oh, start=True, stop=True)
                    nc.tensor.matmul(ps[0:H, 2 + r, :], ones_oh, oh, start=True, stop=True).then_inc(pe_step, 1)

            @block.vector
            def _(dve):
                done = [0]

                def step(ins):
                    done[0] += 1
                    ins.then_inc(dve_step, 1)
                    dve.wait_ge(dve_step, done[0])

                dve.wait_ge(ld_first, 64)
                step(nc.vector.tensor_copy(off_c, off_ci))
                step(nc.vector.tensor_copy(off_r, off_ri))
                step(nc.vector.tensor_scalar(same, off_r, off_c, None, ALU.is_equal))
                step(nc.vector.tensor_scalar(apart, same, -1.0, -NEG, ALU.add, ALU.mult))
                step(nc.vector.tensor_tensor(pb, pb, apart.unsqueeze(1).to_broadcast([NO, H, NO]), ALU.add))
                step(nc.vector.tensor_reduce(pbmax, pb, AX.X, ALU.max))
                step(nc.vector.tensor_tensor(pb, pb, pbmax.unsqueeze(2).to_broadcast([NO, H, NO]),
                                             ALU.subtract))
                dve.wait_ge(act_step, 2)
                step(nc.vector.tensor_reduce(pbsum, pb, AX.X, ALU.add))
                dve.wait_ge(act_step, 3)
                step(nc.vector.tensor_tensor(joint, pbsum, pbmax, ALU.add))
                dve.wait_ge(pool_step, 7)
                step(nc.vector.tensor_reduce(dup, before, AX.X, ALU.add))
                step(nc.vector.tensor_scalar(first, dup, 0.0, None, ALU.is_equal))
                step(nc.vector.tensor_copy(iota_f, iota_i))
                step(nc.vector.memset(ones_oh, 1.0))
                step(nc.vector.tensor_scalar(onehot, iota_f, off_c, first, ALU.is_equal, ALU.mult))
                nc.vector.tensor_scalar(negA[:], negA[:], -1.0, None, ALU.mult)
                step(nc.vector.memset(biasrow, NEG))
                dve.wait_ge(pe_step, 2)
                step(nc.vector.tensor_scalar(pen.rearrange("h (a t) -> h a t", a=2), ps[0:H, 2:4, :],
                                             -1.0, -NEG, ALU.add, ALU.mult))
                nc.vector.tensor_tensor(biasrow[:, P - 1:P - 1 + T], ps[0:H, 0, :], pen[:, 0:T], ALU.add)
                step(nc.vector.tensor_tensor(biasrow[:, LBW:LBW + T], ps[0:H, 1, :], pen[:, T:2 * T], ALU.add))
                nc.vector.tensor_copy(rev_bf, biasrow[:, LBW:2 * LBW]).then_inc(rows_ready, 1)

        stackK_ready = sem("stackK_ready_0"), sem("stackK_ready_1")
        loop_sems = []

        def lsem(name):
            loop_sems.append(sem(name))
            return loop_sems[-1]

        def both(name):
            return lsem(name + "_0"), lsem(name + "_1")

        x_loaded, xcur_loaded, stored = (lsem(n) for n in ("x_loaded", "xcur_loaded", "stored"))
        dve_seq, act_seq = lsem("dve_seq"), lsem("act_seq")
        var_ready = [lsem(f"var_ready_{i}") for i in range(4)]
        rstd_ready = [lsem(f"rstd_ready_{i}") for i in range(4)]
        xn_ready = both("xn_ready")
        hh_ready, hT_ps, hT_ready, h2_ready = (lsem(n) for n in ("hh_ready", "hT_ps", "hT_ready", "h2_ready"))
        q_ps, k_ps, q32_ready, k32_ready = both("q_ps"), both("k_ps"), both("q32_ready"), both("k32_ready")
        gate_ps, gate_ready = lsem("gate_ps"), lsem("gate_ready")
        q_parts, k_parts, q_rest, k_rest = both("q_parts"), both("k_parts"), both("q_rest"), both("k_rest")
        stack_ready = both("stack_ready")
        s1_ps, max_done = both("s1_ps"), both("max_done")
        small_ps, small_free = lsem("small_ps"), lsem("small_free")
        m_rows = both("m_rows_even"), both("m_rows_odd")
        s2_ps, p_ready, pv_done, osb_ready = both("s2_ps"), both("p_ready"), both("pv_done"), both("osb_ready")
        biased, exp_done, res_ready = lsem("biased"), lsem("exp_done"), lsem("res_ready")
        bcd_ps, bc_ready, sp_ready, dt_ready, dtx_ready, y_ready = (
            lsem(n) for n in ("bcd_ps", "bc_ready", "sp_ready", "dt_ready", "dtx_ready", "y_ready"))
        dA_ready, b_ps, c_ps, b_used, scanned, c_used, y_added = (
            lsem(n) for n in ("dA_ready", "b_ps", "c_ps", "b_used", "scanned", "c_used", "y_added"))
        ex_in, ex_ready, w_ready = both("ex_in"), both("ex_ready"), both("w_ready")
        mid_ps, mid_ready, mid_used = both("mid_ps"), both("mid_ready"), both("mid_used")
        w_first_loaded = lsem("w_first_loaded")
        w_loaded = [both(f"w_loaded_{k}") for k in range(WSLOTS)]
        acc_done, silu_ready, prod_ready, x_ready = (
            both("acc_done"), both("silu_ready"), both("prod_ready"), both("x_ready"))

        units, pv_after = [], {}
        for g in range(G):
            for kt in range(NT):
                nh = (1, 1, 2, 4)[kt]
                for j in range(0, 4, nh):
                    units.append((g, kt, j, nh))
                pv_after[(g, kt)] = len(units)
        UPG = len(units) // G

        fills = []
        for h in range(0, H, 2):
            fills += [[(h, 0, 0), (h, 2, P)], [(h, 3, 0)], [(h, 1, 0), (h + 1, 1, 2 * P)],
                      [(h + 1, 0, 0), (h + 1, 2, P)], [(h + 1, 3, 0)]]
        FPG = len(fills) // G

        def steps(cur, nxt):
            place = []

            def put(t, *step):
                place.append((t, len(place), step))

            def spread(t0, t1, lst):
                for i, s in enumerate(lst):
                    put(t0 + (t1 - t0) * (i + 0.5) / len(lst), *s)

            def maxima(l, g, t0, t1):
                spread(t0, t1, [("max", l, f) for f in range(FPG * g, FPG * (g + 1))] + [("turn", l, g)])

            def group(l, g, t0, t1):
                lst, kt = [], 0
                for u in range(UPG * g, UPG * (g + 1)):
                    lst.append(("unit", l, u))
                    while kt < NT and u >= pv_after[(g, kt)] + 1:
                        lst.append(("pv", l, g, kt))
                        kt += 1
                lst += [("pv", l, g, k) for k in range(kt, NT)] + [("osb", l, g)]
                spread(t0, t1, lst)

            def first(l, r, t0, t1):
                spread(t0, t1, [("mm1", l, n) for n in range(8 * r, 8 * r + 8)])

            def second(l, r, t0, t1):
                lst = []
                for n in range(8 * r, 8 * r + 8):
                    lst.append(("mm2", l, n))
                    if n % FT == FT - 1:
                        lst.append(("add", l, n // FT))
                        e = l * E + n // FT + WSLOTS
                        if e < 2 * E or nxt:
                            lst.append(("weights", e // E, e % E))
                spread(t0, t1, lst)

            if nxt:
                t = PLACES["next" if cur else "first"]
                for step, at in zip(NEXT_STEPS, t["steps"]):
                    put(at, *step)
                for g in range(G):
                    maxima(0, g, *t["maxima"][g])
                    group(0, g, *t["units"][g])
                    put(t["out"][g], "out", 0, g)
                for m in range(N):
                    put(t["dA"][m], "dA", m)
                    put(t["stB"][m], "stB", m)
                    put(t["stC"][m], "stC", m)
            if cur:
                t = PLACES["current" if nxt else "last"]
                for step, at in zip(CURRENT_STEPS, t["steps"]):
                    put(at, *step)
                for l in range(2):
                    for r in range(NF // MIDS):
                        first(l, r, *t["first"][NF // MIDS * l + r])
                        second(l, r, *t["second"][NF // MIDS * l + r])
                for g in range(G):
                    maxima(1, g, *t["maxima"][g])
                    group(1, g, *t["units"][g])
                    put(t["out"][g], "out", 1, g)
            else:
                put(PLACES["first"]["maxima"][-1][1] + 0.1, "biases")
            return [s for _, _, s in sorted(place)]

        SMALL_STEPS = ("turnx", "projv", "turn", "out", "flatT", "attout", "turnh", "route", "wT", "b2", "sout")

        def window(i):
            return slice(T - P * (i + 1), T)

        def tile(i):
            return slice(i * P, (i + 1) * P)

        wq, wk, wv, wo, wr = ([wmat[n + s] for s in "01"] for n in ("wq", "wk", "wv", "wo", "wr"))
        BQ, BK = (BQ0, BQ1), (BK0, BK1)

        def over_tokens(row):
            return row.unsqueeze(1).to_broadcast([P, NT, D])
        moe_in = (h2T, xnT[1])

        def segment(cur, nxt):
            has_cur, has_nxt = cur is not None, nxt is not None
            order = steps(has_cur, has_nxt)
            small_of, ring_of = {}, []
            for s in order:
                k = ("projv", s[1]) if s[0] == "proj" else s
                if k[0] in SMALL_STEPS:
                    small_of[k] = len(small_of) + 1
                if s[0] in ("mm1", "unit", "max"):
                    ring_of.append(s)
                if s[0] == "proj":
                    ring_of += [("q", s[1], 0)] + [("gate", 1, 0)] * s[1]
            ring_at = {s: i for i, s in enumerate(ring_of)}

            def small(*step):
                return small_of[step]

            def ring_bank(step):
                return RING_BANKS[ring_at[step] % len(RING_BANKS)]

            def ring_wait(pe, step):
                i = ring_at[step] - len(RING_BANKS)
                if i >= 0:
                    kind, l, n = ring_of[i]
                    done = {"mm1": mid_ready[l], "unit": (exp_done, biased)[l], "max": max_done[l],
                            "q": q32_ready[l], "gate": gate_ready}[kind]
                    pe.wait_ge(done, n + 1)

            def order_of(table):
                for s in order:
                    if s[0] in table:
                        table[s[0]](*s[1:])

            with nc.Block() as block:
                @block.sync
                def _(sp):
                    if has_nxt:
                        sp.dma_start(x_next, d["x"][bass.ds(nxt, 1)].rearrange("b (a p) d -> p (b a) d", p=P))\
                            .then_inc(x_loaded, 16)

                    def weights(l, e):
                        if has_cur:
                            o = l * E + e - WSLOTS
                            sp.wait_ge(mid_used[o // E], FT * (o % E + 1))
                        k = e % WSLOTS
                        loaded = w_loaded[k][l] if l < 2 else w_first_loaded
                        sp.dma_start(w1s[:, k, :], d[f"w1_{l % 2}"][:, e, :]).then_inc(loaded, 16)
                        sp.dma_start(w2s[:, k, :, :], d[f"w2_{l % 2}"][:, e * FT:(e + 1) * FT, :])\
                            .then_inc(loaded, 16)

                    if not has_cur:
                        for e in range(WSLOTS):
                            weights(2, e)
                    else:
                        sp.dma_start(xcur[:], d["x"][bass.ds(cur, 1)].rearrange("b (a p) d -> p (b a) d", p=P))\
                            .then_inc(xcur_loaded, 16)

                    def stack_parts(l):
                        for a in range(PARTS):
                            sp.wait_ge(q_parts[l], a + 1)
                            for j in range(a * PARTS, (a + 1) * PARTS):
                                sp.dma_start(stackQ[HD * j:HD * (j + 1), :, :], qpart[a])\
                                    .then_inc(stack_ready[l], 16)
                        sp.wait_ge(k_parts[l], PARTS)
                        for j in range(PARTS - 1, PAIRS, PARTS):
                            sp.dma_start(stackK[HD * j:HD * (j + 1), :, :], kpart[PARTS - 1])\
                                .then_inc(stack_ready[l], 16)

                    def biases():
                        sp.wait_ge(rows_ready, 1)
                        fwd = biasrow[:, 0:LBW].unsqueeze(1).to_broadcast([H, P, LBW])
                        rev = rev_bf.unsqueeze(1).to_broadcast([H, P, LBW])
                        sp.dma_start(scrF.rearrange("c h t -> h c t"), fwd).then_inc(bias_written, 16)
                        sp.dma_start(scrR.rearrange("c h t -> h c t"), rev).then_inc(bias_written, 16)
                        sp.wait_ge(bias_written, 32)
                        for scr, dst in ((scrF, bias_kT), (scrR, bias_q)):
                            skew = bass.AP(tensor=scr.tensor, offset=P - 1, ap=[[H * LBW - 1, P], [LBW, H], [1, T]])
                            sp.dma_start(dst[:], skew).then_inc(bias_loaded, 16)

                    def maxima_rows(l, g):
                        sp.wait_ge(small_free, small("turn", l, g))
                        for r in range(2):
                            sp.dma_start(stackQ[KR + r:KR + r + 1, 4 * g:4 * g + 4, :],
                                         mparts[:, g % 2, r, :]).then_inc(m_rows[g % 2][l], 16)

                    order_of({"weights": weights, "proj": stack_parts, "biases": biases, "turn": maxima_rows})
                    if has_nxt:
                        sp.wait_ge(w_first_loaded, 32 * WSLOTS)
                    if has_cur:
                        sp.wait_ge(x_ready[1], 1)
                        sp.dma_start(out[bass.ds(cur, 1)].rearrange("b (a p) d -> p (b a) d", p=P), xcur[:])\
                            .then_inc(stored, 16)
                        sp.wait_ge(stored, 16)

                @block.tensor
                def _(pe):
                    def small_bank(*step):
                        if small(*step) > 1:
                            pe.wait_ge(small_free, small(*step) - 1)

                    def turn4(bank, src, signal):
                        for i in range(NT):
                            ins = nc.tensor.transpose(ps[:, bank, tile(i)], src(i), ident[:])
                        ins.then_inc(signal, 1)

                    def tokens_times(lhs, rhs, row, width=D):
                        for i in range(NT):
                            o = ps[:, SMALL_BANK, i * width:(i + 1) * width]
                            ins = nc.tensor.matmul(o, lhs[:, tile(i)], rhs, start=(i == 0),
                                                   stop=(row is None and i == NT - 1), skip_group_check=True)
                            if row is not None:
                                ins = nc.tensor.matmul(o, ones_row[:], row, start=False, stop=(i == NT - 1),
                                                       skip_group_check=True)
                        ins.then_inc(small_ps, 1)

                    def turn_x(l):
                        pe.wait_ge(xn_ready[l], 1)
                        small_bank("turnx", l)
                        xn = (xn0, xn1)[l]
                        turn4(SMALL_BANK, lambda i: xn[:, i, :], small_ps)

                    def turn_hh():
                        pe.wait_ge(hh_ready, 1)
                        turn4(O_BANK, lambda i: a_tok[:, i, :], hT_ps)

                    def projections(l):
                        if l == 0:
                            pe.wait_ge(hT_ready, 1)
                        else:
                            pe.wait_ge(small_free, small("turnx", 1))
                            if has_nxt:
                                pe.wait_ge(osb_ready[0], G)
                        aT = (hT, xnT[1])[l]
                        ring_wait(pe, ("q", l, 0))
                        nc.tensor.matmul(ps[:, ring_bank(("q", l, 0)), :], wq[l][:], aT[:], start=True, stop=True)\
                            .then_inc(q_ps[l], 1)
                        nc.tensor.matmul(ps[:, O_BANK, :], wk[l][:], aT[:], start=True, stop=True)\
                            .then_inc(k_ps[l], 1)
                        small_bank("projv", l)
                        tokens_times(aT, wv[l][:], None)
                        if l == 1:
                            ring_wait(pe, ("gate", 1, 0))
                            nc.tensor.matmul(ps[:, ring_bank(("gate", 1, 0)), :], wmat["wgate1"][:], aT[:], start=True, stop=True)\
                                .then_inc(gate_ps, 1)

                    def max_scores(l, f):
                        if f == 0:
                            pe.wait_ge(stack_ready[l], 16 * (PAIRS + PARTS))
                            pe.wait_ge(stackK_ready[l], ((nxt, cur)[l] + 1) * (16 * (PAIRS - PARTS)))
                        ring_wait(pe, ("max", l, f))
                        for h, i, c in fills[f]:
                            ins = nc.tensor.matmul(ps[:, ring_bank(("max", l, f)), c:c + P * (i + 1)],
                                                   stackQ[0:KR, h, tile(i)], stackK[0:KR, h, 0:P * (i + 1)],
                                                   start=True, stop=True, skip_group_check=True)
                        ins.then_inc(s1_ps[l], 1)

                    def turn_maxima(l, g):
                        pe.wait_ge(max_done[l], FPG * (g + 1))
                        small_bank("turn", l, g)
                        nc.tensor.transpose(ps[0:16, SMALL_BANK, 0:P], maxq[:, 16 * g:16 * g + 16], ident[:])\
                            .then_inc(small_ps, 1)

                    def unit_scores(l, u):
                        g, kt, j0, nh = units[u]
                        W = T - P * kt
                        if u % UPG == 0:
                            pe.wait_ge(m_rows[g % 2][l], 32 * (g // 2 + 1))
                        ring_wait(pe, ("unit", l, u))
                        bank = ring_bank(("unit", l, u))
                        for j in range(nh):
                            h, o = 4 * g + j0 + j, j * W
                            ins = nc.tensor.matmul(ps[:, bank, o:o + W], stackK[0:KR + 2, h, tile(kt)],
                                                   stackQ[0:KR + 2, h, P * kt:T], start=True, stop=True,
                                                   skip_group_check=True)
                        ins.then_inc(s2_ps[l], 1)

                    def weigh_values(l, g, kt):
                        pe.wait_ge(p_ready[l], pv_after[(g, kt)])
                        if kt == 0:
                            if g >= 1:
                                pe.wait_ge(osb_ready[l], g)
                            else:
                                pe.wait_ge(small_free, small("projv", l))
                        for j in range(4):
                            ins = nc.tensor.matmul(ps[32 * j:32 * j + VW, O_BANK, P * kt:T],
                                                   vAug[:, kt, 4 * g + j, :], probs[kt][:, j, :],
                                                   start=(kt == 0), stop=(kt == NT - 1), skip_group_check=True)
                        ins.then_inc(pv_done[l], 1)

                    def turn_output(l, g):
                        pe.wait_ge(osb_ready[l], g + 1)
                        small_bank("out", l, g)
                        turn4(SMALL_BANK, lambda i: o_sb[:, g % 2, tile(i)], small_ps)

                    def turn_flat(l):
                        pe.wait_ge(small_free, small("out", l, G - 1))
                        small_bank("flatT", l)
                        turn4(SMALL_BANK, lambda i: flat_tok[:, i, :], small_ps)

                    def attention_out(l):
                        small_bank("attout", l)
                        pe.wait_ge(small_free, small("flatT", l))
                        tokens_times(oT, wo[l][:], None)

                    def turn_h():
                        pe.wait_ge(h2_ready, 1)
                        small_bank("turnh")
                        turn4(SMALL_BANK, lambda i: flat_tok[:, i, :], small_ps)

                    def route(l):
                        pe.wait_ge(small_free, small(*(("turnh",) if l == 0 else ("turnx", 1))))
                        small_bank("route", l)
                        tokens_times(moe_in[l], wr[l][:], br0[:] if l == 0 else None, width=E)

                    def turn_weights():
                        pe.wait_ge(w_ready[0], 1)
                        small_bank("wT")
                        for i in range(NT):
                            ins = nc.tensor.transpose(ps[0:E, SMALL_BANK, tile(i)], wts[0][:, i, :], ident[:])
                        ins.then_inc(small_ps, 1)

                    def second_biases():
                        pe.wait_ge(small_free, small("wT"))
                        small_bank("b2")
                        tokens_times(wT, b2r[:], None)

                    def first_product(l, n):
                        if n == 0 and l == 1:
                            pe.wait_ge(small_free, small("turnx", 1))
                        if n % FT == 0 and (l == 1 or n // FT >= WSLOTS):
                            pe.wait_ge(w_loaded[n // FT % WSLOTS][l], 32 * (n // FT // WSLOTS + l))
                        ring_wait(pe, ("mm1", l, n))
                        nc.tensor.matmul(ps[:, ring_bank(("mm1", l, n)), :],
                                         w1s[:, n // FT % WSLOTS, tile(n % FT)], moe_in[l][:],
                                         start=True, stop=True).then_inc(mid_ps[l], 1)

                    def second_product(l, n):
                        e, ft = n // FT, n % FT
                        pe.wait_ge(mid_ready[l], n + 1)
                        if ft == 0 and e >= 1:
                            pe.wait_ge(acc_done[l], e)
                        elif ft == 0 and l == 1:
                            pe.wait_ge(acc_done[0], E)
                        for i in range(NT):
                            ins = nc.tensor.matmul(ps[:, OUT_BANK, tile(i)], mid[:, n % MIDS, tile(i)],
                                                   w2s[:, e % WSLOTS, ft, :], start=(ft == 0 and i == 0),
                                                   stop=(ft == FT - 1 and i == NT - 1), skip_group_check=True)
                        ins.then_inc(mid_used[l], 1)

                    def b_and_c():
                        pe.wait_ge(small_free, small("turnx", 0))
                        nc.tensor.matmul(ps[0:96, BC_BANK, :], wbc[:], xnT[0][:], start=True, stop=True)\
                            .then_inc(bcd_ps, 1)

                    def delta():
                        pe.wait_ge(bc_ready, 1)
                        nc.tensor.matmul(ps[:, BC_BANK, :], wdelta[:], xnT[0][:], start=True, stop=True)\
                            .then_inc(bcd_ps, 1)

                    def state_b(m):
                        if m == 0:
                            pe.wait_ge(dt_ready, 1)
                        else:
                            pe.wait_ge(c_used, m)
                        nc.tensor.matmul(ps[:, BC_BANK, :], bcast_sel[:, m:m + 1].to_broadcast([96, P]),
                                         bcS[:], start=True, stop=True).then_inc(b_ps, 1)

                    def state_c(m):
                        pe.wait_ge(b_used, m + 1)
                        nc.tensor.matmul(ps[:, BC_BANK, :], bcast_sel[:, N + m:N + m + 1].to_broadcast([96, P]),
                                         bcS[:], start=True, stop=True).then_inc(c_ps, 1)

                    def state_out():
                        pe.wait_ge(y_added, N)
                        small_bank("sout")
                        tokens_times(y, wmat["wout0"][:], None)

                    order_of({
                        "turnx": turn_x, "turnhh": turn_hh, "proj": projections, "max": max_scores,
                        "turn": turn_maxima, "unit": unit_scores, "pv": weigh_values, "out": turn_output,
                        "flatT": turn_flat, "attout": attention_out, "turnh": turn_h, "route": route,
                        "wT": turn_weights, "b2": second_biases, "mm1": first_product, "mm2": second_product,
                        "bc": b_and_c, "delta": delta, "stB": state_b, "stC": state_c, "sout": state_out})

                @block.scalar
                def _(act):
                    def small_in(*step):
                        act.wait_ge(small_ps, small(*step))

                    def turn_x(l):
                        small_in("turnx", l)
                        nc.scalar.copy(xnT[l][:], ps[:, SMALL_BANK, :]).then_inc(small_free, 1)

                    def turn_hh():
                        act.wait_ge(hT_ps, 1)
                        nc.scalar.activation(hT[:], ps[:, O_BANK, :], ACT.Identity, bias=B1, scale=G1)\
                            .then_inc(hT_ready, 1)

                    def projections(l):
                        if l == 1:
                            act.wait_ge(gate_ps, 1)
                            nc.scalar.activation(gateT[:], ps[:, ring_bank(("gate", 1, 0)), :], ACT.Sigmoid,
                                                 bias=BG1, scale=1.0)\
                                .then_inc(gate_ready, 1)

                    def exp_unit(l, u):
                        g, kt, j, nh = units[u]
                        W = T - P * kt
                        o = probs[kt][:, j:j + nh, :]
                        if l == 0:
                            act.wait_ge(s2_ps[0], u + 1)
                            if g >= 1:
                                act.wait_ge(pv_done[0], NT * (g - 1) + kt + 1)
                            i = ps[:, ring_bank(("unit", l, u)), 0:nh * W].rearrange("p (j t) -> p j t", j=nh)
                            nc.scalar.activation(o, i, ACT.Exp).then_inc(exp_done, 1)
                        else:
                            act.wait_ge(biased, u + 1)
                            nc.scalar.activation(o, o, ACT.Exp).then_inc(p_ready[1], 1)

                    def read_output(l, g):
                        act.wait_ge(pv_done[l], NT * (g + 1))
                        if g >= 2:
                            act.wait_ge(small_ps, small("out", l, g - 2))
                        elif l == 1 and has_nxt:
                            act.wait_ge(small_ps, small("out", 0, g + 2))
                        nc.scalar.copy(o_sb[:, g % 2, :], ps[:, O_BANK, :]).then_inc(osb_ready[l], 1)

                    def turn_flat(l):
                        if l == 0:
                            small_in("flatT", 0)
                            nc.scalar.copy(oT[:], ps[:, SMALL_BANK, :]).then_inc(small_free, 1)

                    def turn_h():
                        small_in("turnh")
                        nc.scalar.activation(h2T[:], ps[:, SMALL_BANK, :], ACT.Identity, bias=B2, scale=G2)\
                            .then_inc(small_free, 1)

                    def routing_exp(l):
                        act.wait_ge(ex_in[l], 1)
                        nc.scalar.activation(ex[:], ex[:], ACT.Exp).then_inc(ex_ready[l], 1)

                    def turn_weights():
                        small_in("wT")
                        nc.scalar.copy(wT, ps[0:E, SMALL_BANK, :]).then_inc(small_free, 1)

                    def gelu(l, n):
                        act.wait_ge(mid_ps[l], n + 1)
                        if n >= MIDS:
                            act.wait_ge(mid_used[l], n - MIDS + 1)
                        elif l == 1:
                            act.wait_ge(mid_used[0], NF - MIDS + n + 1)
                        nc.scalar.activation(mid[:, n % MIDS, :], ps[:, ring_bank(("mm1", l, n)), :], ACT.Gelu,
                                             bias=b1c[:, n:n + 1] if l == 0 else 0.0, scale=1.0)\
                            .then_inc(mid_ready[l], 1)

                    def silu(l):
                        act.wait_ge(acc_done[l], E)
                        nc.scalar.activation(g_tok[:], acc[:], ACT.Silu).then_inc(silu_ready[l], 1)

                    def update(l):
                        if l == 0:
                            silu(0)

                    def delta():
                        act.wait_ge(bcd_ps, 2)
                        nc.scalar.activation(sp, ps[:, BC_BANK, :], ACT.Abs).then_inc(act_seq, 1)
                        act.wait_ge(act_seq, 1)
                        nc.scalar.activation(sp, sp, ACT.Exp, scale=-1.0).then_inc(act_seq, 1)
                        act.wait_ge(act_seq, 2)
                        nc.scalar.activation(sp, sp, ACT.Ln, bias=1.0).then_inc(sp_ready, 1)

                    def decay(m):
                        if m == 0:
                            act.wait_ge(dt_ready, 1)
                        if m >= 3:
                            act.wait_ge(scanned, m - 2)
                        nc.scalar.activation(dA[:, m % 3, :], dt[:], ACT.Exp, scale=negA[:, m:m + 1])\
                            .then_inc(dA_ready, 1)

                    def state_out():
                        small_in("sout")
                        nc.scalar.copy(s_tok[:].rearrange("p a d -> p (a d)"), ps[:, SMALL_BANK, :])\
                            .then_inc(small_free, 1)

                    order_of({
                        "turnx": turn_x, "turnhh": turn_hh, "proj": projections, "unit": exp_unit,
                        "osb": read_output, "flatT": turn_flat, "turnh": turn_h,
                        "rexp": routing_exp, "wT": turn_weights, "mm1": gelu, "silu": silu, "upd": update,
                        "delta": delta, "dA": decay, "sout": state_out})

                @block.gpsimd
                def _(pool):
                    def rsqrt(n):
                        pool.wait_ge(var_ready[n], 1)
                        nc.gpsimd.tensor_tensor(rstd[:], ve[:], minus_half[:], ALU.pow).then_inc(rstd_ready[n], 1)

                    def norm(l):
                        if l == 0:
                            rsqrt(0)
                            rsqrt(1)
                        else:
                            rsqrt(3)

                    def stack_parts(l):
                        for b in range(PARTS - 1):
                            pool.wait_ge(k_parts[l], b + 1)
                            for j in range(b, PAIRS, PARTS):
                                nc.gpsimd.dma_start(stackK[HD * j:HD * (j + 1), :, :], kpart[b])\
                                    .then_inc(stackK_ready[l], 16)

                    def causal(l, u):
                        if l == 0:
                            g, kt, j, nh = units[u]
                            o = probs[kt][:, j:j + nh, 0:P]
                            pool.wait_ge(exp_done, u + 1)
                            nc.gpsimd.affine_select(out=o, in_=o, compare_op=ALU.is_ge, fill=0.0, base=0,
                                                    pattern=[[0, nh], [1, P]], channel_multiplier=-1)\
                                .then_inc(p_ready[0], 1)

                    def attention_out(l):
                        if l == 0:
                            rsqrt(2)

                    def residual():
                        pool.wait_ge(hh_ready, 1)
                        pool.wait_ge(small_ps, small("turnx", 0))
                        nc.gpsimd.tensor_tensor(xn0[:], xn0[:], over_tokens(rowb[:, 1, :]), ALU.add)\
                            .then_inc(res_ready, 1)

                    def y_start():
                        pool.wait_ge(small_free, small("turnx", 0))
                        nc.gpsimd.tensor_scalar(y[:], xnT[0][:], D_COL, None, ALU.mult).then_inc(y_ready, 1)

                    def state_add(m):
                        pool.wait_ge(c_used, m + 1)
                        if m == 0:
                            pool.wait_ge(y_ready, 1)
                        else:
                            pool.wait_ge(y_added, m)
                        nc.gpsimd.tensor_tensor(y[:], y[:], h_buf[:, m % 3, :], ALU.add).then_inc(y_added, 1)

                    order_of({"norm": norm, "proj": stack_parts, "unit": causal, "attout": attention_out,
                              "bc": y_start, "turnhh": residual, "stC": state_add})

                @block.vector
                def _(dve):
                    seq = [0]

                    def step(ins):
                        seq[0] += 1
                        ins.then_inc(dve_seq, 1)
                        dve.wait_ge(dve_seq, seq[0])

                    def moments(src, n):
                        for i in range(NT):
                            ins = nc.vector.bn_stats(stats[:, i, :], src[:, i, :])
                        step(ins)
                        for i in range(NT):
                            ins = nc.vector.bn_aggr(mv[:, i, :], stats[:, i, :])
                        step(ins)
                        nc.vector.tensor_scalar(ve[:], mv[:, :, 1], EPS, None, ALU.add).then_inc(var_ready[n], 1)

                    def normalize(dst, src, n, signal):
                        dve.wait_ge(rstd_ready[n], 1)
                        for i in range(NT):
                            ins = nc.vector.tensor_scalar(dst[:, i, :], src[:, i, :], mv[:, i, 0:1],
                                                          rstd[:, i:i + 1], ALU.subtract, ALU.mult)
                        ins.then_inc(signal, 1)
                        dve.wait_ge(signal, 1)

                    def norm(l):
                        if l == 1:
                            dve.wait_ge(x_ready[0], 1)
                            moments(xcur, 3)
                            normalize(xn1, xcur, 3, xn_ready[1])
                            return
                        dve.wait_ge(x_loaded, 16)
                        moments(x_next, 0)
                        normalize(xn0, x_next, 0, xn_ready[0])
                        step(nc.vector.tensor_tensor(ve[:], mv[:, :, 1], rstd[:], ALU.mult))
                        step(nc.vector.tensor_tensor(ve[:], ve[:], rstd[:], ALU.mult))
                        nc.vector.tensor_scalar(ve[:], ve[:], EPS, None, ALU.add).then_inc(var_ready[1], 1)
                        dve.wait_ge(rstd_ready[1], 1)
                        for i in range(NT):
                            ins = nc.vector.tensor_scalar(a_tok[:, i, :], xn0[:, i, :], rstd[:, i:i + 1], None,
                                                          ALU.mult)
                        ins.then_inc(hh_ready, 1)
                        dve.wait_ge(hh_ready, 1)

                    def split(l):
                        dve.wait_ge(q_ps[l], 1)
                        nc.vector.tensor_scalar(q32, ps[:, ring_bank(("q", l, 0)), :], BQ[l], SCALE,
                                                ALU.add, ALU.mult).then_inc(q32_ready[l], 1)
                        dve.wait_ge(k_ps[l], 1)
                        nc.vector.tensor_scalar(k32, ps[:, O_BANK, :], BK[l], None, ALU.add)\
                            .then_inc(k32_ready[l], 1)
                        dve.wait_ge(q32_ready[l], 1)
                        nc.vector.tensor_copy(qpart[0], q32).then_inc(q_parts[l], 1)
                        dve.wait_ge(k32_ready[l], 1)
                        nc.vector.tensor_copy(kpart[0], k32).then_inc(k_parts[l], 1)
                        dve.wait_ge(q_parts[l], 1)
                        nc.vector.tensor_tensor(qres, q32, qpart[0], ALU.subtract).then_inc(q_rest[l], 1)
                        dve.wait_ge(k_parts[l], 1)
                        nc.vector.tensor_tensor(kres, k32, kpart[0], ALU.subtract).then_inc(k_rest[l], 1)
                        dve.wait_ge(q_rest[l], 1)
                        nc.vector.tensor_copy(qpart[1], qres).then_inc(q_parts[l], 1)
                        dve.wait_ge(k_rest[l], 1)
                        nc.vector.tensor_copy(kpart[1], kres).then_inc(k_parts[l], 1)
                        dve.wait_ge(q_parts[l], 2)
                        nc.vector.tensor_tensor(qpart[2], qres, qpart[1], ALU.subtract).then_inc(q_parts[l], 1)
                        dve.wait_ge(k_parts[l], 2)
                        nc.vector.tensor_tensor(kpart[2], kres, kpart[1], ALU.subtract).then_inc(k_parts[l], 1)
                        dve.wait_ge(small_ps, small("projv", l))
                        for i in range(NT):
                            ins = nc.vector.tensor_tensor(
                                vAug[:, i, :, 0:HD], ps[:, SMALL_BANK, tile(i)].rearrange("p (h i) -> p h i", h=H),
                                rowb[:, 2 * l, :].rearrange("p (h i) -> p h i", h=H), ALU.add)
                        ins.then_inc(small_free, 1)

                    def row_max(l, f):
                        if l == 1 and f == 0:
                            dve.wait_ge(bias_loaded, 32)
                        dve.wait_ge(s1_ps[l], f + 1)
                        for h, i, c in fills[f]:
                            o = ps[:, ring_bank(("max", l, f)), c:c + P * (i + 1)]
                            extra = mask_q[:, window(i)] if l == 0 else bias_q[:, h, window(i)]
                            m = NT * h + i
                            ins = nc.vector.tensor_tensor_reduce(out=o, in0=o, in1=extra, scale=1.0,
                                                                 scalar=LOWEST, op0=ALU.add, op1=ALU.max,
                                                                 accum_out=maxq[:, m:m + 1])
                        ins.then_inc(max_done[l], 1)

                    def max_parts(l, g):
                        t = ps[0:16, SMALL_BANK, 0:P]
                        dve.wait_ge(small_ps, small("turn", l, g))
                        if g >= 2:
                            dve.wait_ge(m_rows[g % 2][l], 32 * (g // 2))
                        elif l == 1 and has_nxt:
                            dve.wait_ge(m_rows[g % 2][0], 64)
                        step(nc.vector.tensor_scalar(mparts[:, g % 2, 0, :], t, -1.0, None, ALU.mult))
                        nc.vector.scalar_tensor_tensor(out=mparts[:, g % 2, 1, :], in0=t, scalar=-1.0,
                                                       in1=mparts[:, g % 2, 0, :], op0=ALU.mult,
                                                       op1=ALU.subtract).then_inc(small_free, 1)

                    def add_bias(l, u):
                        if l == 0:
                            return
                        g, kt, j, nh = units[u]
                        W = T - P * kt
                        h = 4 * g + j
                        dve.wait_ge(s2_ps[1], u + 1)
                        if g >= 1:
                            dve.wait_ge(pv_done[1], NT * (g - 1) + kt + 1)
                        i = ps[:, ring_bank(("unit", l, u)), 0:nh * W].rearrange("p (j t) -> p j t", j=nh)
                        nc.vector.tensor_tensor(probs[kt][:, j:j + nh, :], i, bias_kT[:, h:h + nh, 0:W],
                                                ALU.add).then_inc(biased, 1)

                    def divide_output(l, g):
                        o = ps[:, SMALL_BANK, :].rearrange("p (a j c) -> p a j c", a=NT, j=4)
                        dve.wait_ge(small_ps, small("out", l, g))
                        step(nc.vector.reciprocal(recip[:], o[:, :, :, HD]))
                        nc.vector.tensor_tensor(flat[:, :, 4 * g:4 * g + 4, :], o[:, :, :, 0:HD],
                                                recip[:].unsqueeze(3).to_broadcast([P, NT, 4, HD]), ALU.mult)\
                            .then_inc(small_free, 1)
                        dve.wait_ge(small_free, small("out", l, g))

                    def turn_flat(l):
                        if l == 1:
                            dve.wait_ge(small_ps, small("flatT", 1))
                            dve.wait_ge(gate_ready, 1)
                            nc.vector.tensor_tensor(oT[:], ps[:, SMALL_BANK, :], gateT[:], ALU.mult)\
                                .then_inc(small_free, 1)

                    def attention_out(l):
                        if l == 0:
                            dve.wait_ge(small_ps, small("attout", 0))
                            dve.wait_ge(res_ready, 1)
                            nc.vector.tensor_tensor(a_tok[:].rearrange("p a d -> p (a d)"), ps[:, SMALL_BANK, :],
                                                    xn0[:].rearrange("p a d -> p (a d)"), ALU.add)\
                                .then_inc(small_free, 1)
                            dve.wait_ge(small_free, small("attout", 0))
                            moments(a_tok, 2)
                            normalize(flat_tok, a_tok, 2, h2_ready)
                        else:
                            dve.wait_ge(small_ps, small("attout", 1))
                            nc.vector.tensor_tensor(a_tok[:], ps[:, SMALL_BANK, :].rearrange("p (a d) -> p a d", a=NT),
                                                    over_tokens(rowb[:, 3, :]), ALU.add).then_inc(small_free, 1)

                    def second_biases():
                        dve.wait_ge(small_ps, small("b2"))
                        nc.vector.tensor_tensor(acc_next[:].rearrange("p a d -> p (a d)"), ps[:, SMALL_BANK, :],
                                                a_tok[:].rearrange("p a d -> p (a d)"), ALU.add)\
                            .then_inc(small_free, 1)

                    def b_and_c():
                        z = ps[0:96, BC_BANK, :]
                        dve.wait_ge(bcd_ps, 1)
                        step(nc.vector.tensor_copy(bcS[:], z))
                        step(nc.vector.tensor_tensor(bcR, z, bcS[:], ALU.subtract))
                        nc.vector.tensor_copy(bcS[32:64, :], bcR[32:64, :])
                        step(nc.vector.tensor_copy(bcS[64:96, :], bcR[64:96, :]))
                        step(nc.vector.tensor_tensor(bcR[64:96, :], bcR[64:96, :], bcS[64:96, :], ALU.subtract))
                        nc.vector.tensor_copy(bcS[64:96, :], bcR[64:96, :]).then_inc(bc_ready, 1)

                    def delta():
                        dve.wait_ge(sp_ready, 1)
                        nc.vector.scalar_tensor_tensor(out=dt[:], in0=ps[:, BC_BANK, :], scalar=0.0, in1=sp,
                                                       op0=ALU.max, op1=ALU.add).then_inc(dt_ready, 1)
                        dve.wait_ge(dt_ready, 1)
                        dve.wait_ge(y_ready, 1)
                        nc.vector.tensor_tensor(dtx[:], dt[:], xnT[0][:], ALU.mult).then_inc(dtx_ready, 1)

                    def state_b(m):
                        dve.wait_ge(b_ps, m + 1)
                        if m == 0:
                            dve.wait_ge(dtx_ready, 1)
                            dve.wait_ge(bc_ready, 1)
                        if m >= 2:
                            dve.wait_ge(scanned, m - 1)
                        nc.vector.tensor_tensor(u_buf[:, m % 2, :], dtx[:], ps[:, BC_BANK, :], ALU.mult)\
                            .then_inc(b_used, 1)

                    def state_c(m):
                        dve.wait_ge(b_used, m + 1)
                        dve.wait_ge(dA_ready, m + 1)
                        if m >= 3:
                            dve.wait_ge(y_added, m - 2)
                        nc.vector.tensor_tensor_scan(h_buf[:, m % 3, :], dA[:, m % 3, :], u_buf[:, m % 2, :],
                                                     0.0, ALU.mult, ALU.add).then_inc(scanned, 1)
                        dve.wait_ge(scanned, m + 1)
                        dve.wait_ge(c_ps, m + 1)
                        nc.vector.tensor_tensor(h_buf[:, m % 3, :], h_buf[:, m % 3, :], ps[:, BC_BANK, :],
                                                ALU.mult).then_inc(c_used, 1)

                    def wide(ap):
                        return ap.to_broadcast([P, NT, E])

                    def route(l):
                        dve.wait_ge(small_ps, small("route", l))
                        nc.vector.tensor_copy(logits[:].rearrange("p a e -> p (a e)"),
                                              ps[:, SMALL_BANK, 0:NT * E]).then_inc(small_free, 1)
                        dve.wait_ge(small_free, small("route", l))
                        for i in range(NT):
                            ins = nc.vector.max(top8[:, i, :], logits[:, i, :])
                        step(ins)
                        nc.vector.tensor_tensor(ex[:], logits[:], wide(top8[:, :, 0:1]), ALU.subtract)\
                            .then_inc(ex_in[l], 1)
                        if l == 0:
                            step(nc.vector.tensor_tensor(gt[:], logits[:], wide(top8[:, :, 1:2]), ALU.is_ge))
                        else:
                            step(nc.vector.tensor_tensor(gt[:], logits[:], wide(top8[:, :, 1:2]), ALU.is_gt))
                            step(nc.vector.tensor_tensor(eq[:], logits[:], wide(top8[:, :, 1:2]), ALU.is_equal))
                            nc.vector.tensor_reduce(cnt[:], gt[:], AX.X, ALU.add)
                            step(nc.vector.tensor_tensor_scan(rank[:].rearrange("p a e -> p (a e)"),
                                                              keep[:].rearrange("p a e -> p (a e)"),
                                                              eq[:].rearrange("p a e -> p (a e)"),
                                                              0.0, ALU.mult, ALU.add))
                            step(nc.vector.tensor_tensor(rank[:], rank[:], wide(cnt[:].unsqueeze(2)), ALU.add))
                            step(nc.vector.tensor_scalar(rank[:], rank[:], 2.5, None, ALU.is_le))
                            step(nc.vector.tensor_tensor(eq[:], eq[:], rank[:], ALU.mult))
                            step(nc.vector.tensor_tensor(gt[:], gt[:], eq[:], ALU.add))

                    def weights(l):
                        dve.wait_ge(ex_ready[l], 1)
                        if l == 0 and has_cur:
                            dve.wait_ge(acc_done[0], E)
                        step(nc.vector.tensor_tensor(gt[:], ex[:], gt[:], ALU.mult))
                        step(nc.vector.tensor_reduce(tsum[:], gt[:], AX.X, ALU.add))
                        step(nc.vector.reciprocal(cnt[:], tsum[:]))
                        nc.vector.tensor_tensor(wts[l][:], gt[:], wide(cnt[:].unsqueeze(2)), ALU.mult)\
                            .then_inc(w_ready[l], 1)
                        dve.wait_ge(w_ready[l], 1)

                    def add_expert(l, e):
                        dve.wait_ge(mid_used[l], FT * (e + 1))
                        if e >= 1:
                            dve.wait_ge(acc_done[l], e)
                        for i in range(NT):
                            o, w = ps[:, OUT_BANK, tile(i)], wts[l][:, i, e:e + 1]
                            if l == 1 and e == 0:
                                ins = nc.vector.tensor_scalar(acc[:, i, :], o, w, None, ALU.mult)
                            else:
                                before = (acc_next if e == 0 else acc)[:, i, :]
                                ins = nc.vector.scalar_tensor_tensor(out=acc[:, i, :], in0=o, scalar=w,
                                                                     in1=before, op0=ALU.mult, op1=ALU.add)
                        ins.then_inc(acc_done[l], 1)

                    def update(l):
                        dve.wait_ge(silu_ready[l], 1)
                        if l == 0:
                            dve.wait_ge(xcur_loaded, 16)
                        else:
                            dve.wait_ge(small_free, small("attout", 1))
                        s = (s_tok, a_tok)[l]
                        nc.vector.tensor_tensor(g_tok[:], s[:], g_tok[:], ALU.mult).then_inc(prod_ready[l], 1)
                        dve.wait_ge(prod_ready[l], 1)
                        nc.vector.tensor_tensor(xcur[:], xcur[:], g_tok[:], ALU.add).then_inc(x_ready[l], 1)

                    order_of({
                        "norm": norm, "proj": split, "max": row_max, "turn": max_parts, "unit": add_bias,
                        "out": divide_output, "flatT": turn_flat, "attout": attention_out,
                        "b2": second_biases, "bc": b_and_c, "delta": delta, "stB": state_b, "stC": state_c,
                        "route": route, "wts": weights, "add": add_expert, "upd": update})

            nums = [s.num for s in loop_sems]
            assert nums == list(range(nums[0], nums[0] + len(nums)))
            nc.multi_engine_barrier(list(nc.engines), sems_to_clear=range(nums[0], nums[-1] + 1))

        segment(None, 0)
        with nc.Fori(0, B - 1) as b:
            segment(b, b + 1)
        segment(B - 1, None)


def kernel(**inputs):
    import numpy as np
    import concourse.bacc as bacc
    from concourse.bass_utils import run_bass_kernel_spmd

    v = {k: np.asarray(a) for k, a in inputs.items()}
    x = v["L0_attn_x"]
    D = x.shape[2]
    N = v["L0_attn_A_log"].shape[0]
    H, HD, FT = 16, D // 16, v["L0_ffn_e_w1"].shape[2] // 128
    by_dim = np.arange(D).reshape(H, HD).T.ravel()
    Wx = v["L0_attn_Wx"]
    Wqkv, bqkv = v["L1_attn_Wqkv"], v["L1_attn_bqkv"]
    E, F = v["L0_ffn_e_b1"].shape
    data = {
        "x": x,
        "A_log": v["L0_attn_A_log"].reshape(1, N),
        "pos_bias": v["L1_attn_pos_bias"],
        "pos_biasT": v["L1_attn_pos_bias"].T,
        "offsets": v["L1_attn_offsets"],
        "cols": np.stack([v["L0_attn_D"], v["L0_ffn_ln1_g"], v["L0_ffn_ln1_b"], v["L0_ffn_ln2_g"],
                          v["L0_ffn_ln2_b"], v["L0_ffn_bq"][by_dim], v["L0_ffn_bk"][by_dim],
                          bqkv[:D][by_dim], bqkv[D:2 * D][by_dim], v["L1_attn_bgate"]], axis=1),
        "rows": np.concatenate([v["L0_ffn_bv"], v["L0_ffn_bo"], bqkv[2 * D:], v["L1_attn_bout"],
                                v["L0_ffn_br"]])[None, :],
        "b1": v["L0_ffn_e_b1"].reshape(E * FT, 128).T,
        "b2": v["L0_ffn_e_b2"],
        "wbc": np.concatenate([Wx[:2 * N].T] * 3, axis=1),
        "wdelta": Wx[2 * N:].T,
        "wout0": v["L0_attn_Wout"].T,
        "wq0": v["L0_ffn_Wq"][:, by_dim], "wk0": v["L0_ffn_Wk"][:, by_dim],
        "wv0": v["L0_ffn_Wv"], "wo0": v["L0_ffn_Wo"], "wr0": v["L0_ffn_Wr"],
        "wq1": Wqkv[:D][by_dim].T, "wk1": Wqkv[D:2 * D][by_dim].T, "wv1": Wqkv[2 * D:].T,
        "wgate1": v["L1_attn_Wgate"].T, "wo1": v["L1_attn_Wout"].T, "wr1": v["L1_ffn_router_w"].T,
        "w1_0": v["L0_ffn_e_w1"].transpose(1, 0, 2),
        "w2_0": v["L0_ffn_e_w2"].reshape(E * FT, 128, D).transpose(1, 0, 2),
        "w1_1": v["L1_ffn_expert_w1"].transpose(2, 0, 1),
        "w2_1": v["L1_ffn_expert_w2"].transpose(2, 0, 1).reshape(FT, 128, E, D).transpose(1, 2, 0, 3)
                .reshape(128, E * FT, D),
    }
    nc = bacc.Bacc("TRN2", target_bir_lowering=False, num_devices=1)
    arrays, aps = {}, {}
    for name, a in data.items():
        a = np.ascontiguousarray(a)
        arrays["in_" + name] = a
        aps[name] = nc.dram_tensor("in_" + name, a.shape, mybir.dt.from_np(a.dtype), kind="ExternalInput").ap()
    out = nc.dram_tensor("out_0", x.shape, mybir.dt.float32, kind="ExternalOutput").ap()
    build(nc, aps, out)
    r = run_bass_kernel_spmd(nc, [arrays], core_ids=[0])
    return r.results[0]["out_0"]
```
